# Optimizing a Trainium2 kernel written in Bass

```python
import numpy as np
import jax
import jax.numpy as jnp

def _softmax(x, axis=-1):
    return jax.nn.softmax(x, axis=axis)

def _gelu(x):
    return jax.nn.gelu(x, approximate=True)

def _silu(x):
    return jax.nn.silu(x)

def _sigmoid(x):
    return jax.nn.sigmoid(x)

def _layernorm(x, axis=-1, eps=1e-05):
    m = jnp.mean(x, axis=axis, keepdims=True)
    v = jnp.var(x, axis=axis, keepdims=True)
    return (x - m) / jnp.sqrt(v + eps)

def _scatter_add(tgt, idx, src, axis=0):
    return tgt.at[idx].add(src)

def _segment_sum(src, seg, n):
    return jax.ops.segment_sum(src, seg, n)
kernel_name = 'mk_decoder_preln_d2_seqx_r8_f9e179'

def setup_inputs(seed: int=0):
    np.random.seed(seed)
    _w = jnp.asarray

    def _rec_inputs():
        import jax
        import jax.numpy as jnp
        _rk = jax.random.key(seed)
        x = -0.0003929 + 0.9999 * jax.random.normal(jax.random.fold_in(_rk, 1), (1, 1024, 128), jnp.float32)
        _lenS = 1024 - jax.random.randint(jax.random.fold_in(_rk, 7), (1,), 0, max(1, 1024 // 4) + 1, jnp.int32)
        _lenS2 = 6404 - jax.random.randint(jax.random.fold_in(_rk, 8), (1,), 0, max(1, 6404 // 4) + 1, jnp.int32)
        _ctx_1024P = jax.random.normal(jax.random.fold_in(_rk, 11), (1, 16, 128), jnp.float32)
        _ctx_1024c = jax.random.dirichlet(jax.random.fold_in(_rk, 511), 0.3 * jnp.ones((16,), jnp.float32), (1, 6404))
        _ctx_1024t = jnp.einsum('bsk,bkd->bsd', _ctx_1024c, _ctx_1024P)
        _ctx_1024t = _ctx_1024t * jax.lax.rsqrt(jnp.mean(jnp.square(_ctx_1024t)) + 1e-12) * 0.953939
        ctx_1024 = -1.39393e-06 + 0.999914 * (_ctx_1024t + 0.3 * jax.random.normal(jax.random.fold_in(_rk, 611), (1, 6404, 128), jnp.float32))
        _validS = jnp.arange(1024)[None, :] < _lenS[:, None]
        _validS2 = jnp.arange(6404)[None, :] < _lenS2[:, None]
        _causal = jnp.tril(jnp.ones((1024, 1024), dtype=bool))
        mask_BxS2_bf1 = jnp.ones((1, 6404), dtype=bool)
        return (x, ctx_1024, mask_BxS2_bf1)
    x, ctx_1024, mask_BxS2_bf1 = _rec_inputs()

    def _L0_attn_setup():
        import jax, jax.numpy as jnp
        import numpy as np
        D_MODEL = 128
        LN_EPS = 1e-05
        DEN_EPS = 1e-06

        def _layer_norm(x, g, b):
            mu = jnp.mean(x, axis=-1, keepdims=True)
            var = jnp.mean(jnp.square(x - mu), axis=-1, keepdims=True)
            return (x - mu) * jax.lax.rsqrt(var + LN_EPS) * g + b
        key = jax.random.key(seed)
        ks = jax.random.split(key, 7)
        s = 1.0 / np.sqrt(D_MODEL)
        x = jax.random.normal(ks[0], (4, 256, D_MODEL), dtype=jnp.float32)
        qkv_w = jax.random.uniform(ks[1], (D_MODEL, 3 * D_MODEL), jnp.float32, -s, s)
        qkv_b = jax.random.uniform(ks[2], (3 * D_MODEL,), jnp.float32, -s, s)
        gate_w = jax.random.uniform(ks[3], (D_MODEL, D_MODEL), jnp.float32, -s, s)
        gate_b = jax.random.uniform(ks[4], (D_MODEL,), jnp.float32, -s, s)
        ln_g = jnp.ones((D_MODEL,), jnp.float32)
        ln_b = jnp.zeros((D_MODEL,), jnp.float32)
        return {'x': x, 'qkv_w': qkv_w, 'qkv_b': qkv_b, 'gate_w': gate_w, 'gate_b': gate_b, 'ln_g': ln_g, 'ln_b': ln_b}
    _L0_attn_all = _L0_attn_setup()
    _L0_attn_in = {k: v for k, v in _L0_attn_all.items() if k in ('qkv_w', 'qkv_b', 'gate_w', 'gate_b', 'ln_g', 'ln_b')}
    del _L0_attn_all

    def _L0_xattn_setup():
        import jax, jax.numpy as jnp
        import numpy as np
        GAMMA = 10.0
        BASE = 10000.0
        SCALE = 64 ** (-0.5)
        NUM_HEADS = 16

        def _larope(t, seq_len):
            B, H, L, D = t.shape
            inv_freq = 1.0 / BASE ** (jnp.arange(0, D, 2, dtype=jnp.float32) / D)
            pos = GAMMA * (jnp.arange(L, dtype=jnp.float32) / float(seq_len))
            ang = pos[:, None] * inv_freq
            cos = jnp.cos(ang)
            sin = jnp.sin(ang)
            te, to = (t[..., 0::2], t[..., 1::2])
            re = te * cos - to * sin
            ro = te * sin + to * cos
            return jnp.stack([re, ro], axis=-1).reshape(t.shape)
        key = jax.random.key(seed)
        ks = jax.random.split(key, 8)
        B, Lq, Lk, D = (8, 256, 64, 128)
        s = D ** (-0.5)
        return {'x': jax.random.normal(ks[0], (B, Lq, D), jnp.float32), 'context': jax.random.normal(ks[1], (B, Lk, D), jnp.float32), 'context_mask': jnp.ones((B, Lk), dtype=bool), 'Wq': jax.random.normal(ks[2], (D, D), jnp.float32) * s, 'bq': jnp.zeros((D,), jnp.float32), 'Wkv': jax.random.normal(ks[3], (D, 2 * D), jnp.float32) * s, 'bkv': jnp.zeros((2 * D,), jnp.float32), 'Wo': jax.random.normal(ks[4], (D, D), jnp.float32) * s, 'bo': jnp.zeros((D,), jnp.float32)}
    _L0_xattn_all = _L0_xattn_setup()
    _L0_xattn_in = {k: v for k, v in _L0_xattn_all.items() if k in ('Wq', 'bq', 'Wkv', 'bkv', 'Wo', 'bo')}
    del _L0_xattn_all

    def _L0_ffn_setup():
        import jax, jax.numpy as jnp
        import numpy as np
        B, L, D = (4, 256, 128)
        E, K, S = (8, 2, 2)
        F = 176
        SCALE = 1.0
        INIT = 0.02

        def _swiglu(x, wg, wu, wd):
            return jax.nn.silu(x @ wg) * (x @ wu) @ wd
        key = jax.random.key(seed)
        ks = jax.random.split(key, 8)
        return {'hidden_states': jax.random.normal(ks[0], (B, L, D), jnp.float32), 'gate_w': jax.random.normal(ks[1], (D, E), jnp.float32) * INIT, 'exp_gate': jax.random.normal(ks[2], (E, D, F), jnp.float32) * INIT, 'exp_up': jax.random.normal(ks[3], (E, D, F), jnp.float32) * INIT, 'exp_down': jax.random.normal(ks[4], (E, F, D), jnp.float32) * INIT, 'sh_gate': jax.random.normal(ks[5], (S, D, F), jnp.float32) * INIT, 'sh_up': jax.random.normal(ks[6], (S, D, F), jnp.float32) * INIT, 'sh_down': jax.random.normal(ks[7], (S, F, D), jnp.float32) * INIT}
    _L0_ffn_all = _L0_ffn_setup()
    _L0_ffn_in = {k: v for k, v in _L0_ffn_all.items() if k in ('gate_w', 'exp_gate', 'exp_up', 'exp_down', 'sh_gate', 'sh_up', 'sh_down')}
    del _L0_ffn_all

    def _L1_attn_setup():
        import jax, jax.numpy as jnp
        import numpy as np
        import math
        INPUT_SIZE = 128
        HIDDEN = 128
        SEQ_LEN = 32
        BATCH = 128

        def _lstm(input_seq, w, u, bias):
            H = u.shape[0]
            B = input_seq.shape[1]
            x_proj = jnp.einsum('sbi,ih->sbh', input_seq, w) + bias

            def step(carry, xp_t):
                h_prev, c_prev = carry
                g = xp_t + h_prev @ u
                gates = jax.nn.sigmoid(g[:, :3 * H])
                c_cand = jnp.tanh(g[:, 3 * H:])
                ig, fg, og = (gates[:, :H], gates[:, H:2 * H], gates[:, 2 * H:])
                c = fg * c_prev + ig * c_cand
                h = og * jnp.tanh(c)
                return ((h, c), h)
            init = (jnp.zeros((B, H), dtype=input_seq.dtype), jnp.zeros((B, H), dtype=input_seq.dtype))
            _, hs = jax.lax.scan(step, init, x_proj)
            return hs
        key = jax.random.key(seed)
        k1, k2, k3, k4 = jax.random.split(key, 4)
        stddev = 1.0 / math.sqrt(HIDDEN)
        input_seq = jax.random.normal(k1, (SEQ_LEN, BATCH, INPUT_SIZE), dtype=jnp.float32)
        w = jax.random.uniform(k2, (INPUT_SIZE, 4 * HIDDEN), minval=-stddev, maxval=stddev, dtype=jnp.float32)
        u = jax.random.uniform(k3, (HIDDEN, 4 * HIDDEN), minval=-stddev, maxval=stddev, dtype=jnp.float32)
        bias = jax.random.uniform(k4, (4 * HIDDEN,), minval=-stddev, maxval=stddev, dtype=jnp.float32)
        return {'input_seq': input_seq, 'w': w, 'u': u, 'bias': bias}
    _L1_attn_all = _L1_attn_setup()
    _L1_attn_in = {k: v for k, v in _L1_attn_all.items() if k in ('w', 'u', 'bias')}
    del _L1_attn_all

    def _L1_xattn_setup():
        import jax, jax.numpy as jnp
        import numpy as np
        B, M, N, DIM, DH, H = (8, 512, 64, 128, 128, 8)
        INNER = DH * H
        EPS = 1e-05

        def _layernorm(x, g, b):
            mu = jnp.mean(x, axis=-1, keepdims=True)
            var = jnp.var(x, axis=-1, keepdims=True)
            return (x - mu) * jax.lax.rsqrt(var + EPS) * g + b
        key = jax.random.key(seed)
        ks = jax.random.split(key, 8)
        sd = 0.02
        return {'x': jax.random.normal(ks[0], (B, M, DIM), jnp.float32), 'latents': jax.random.normal(ks[1], (B, N, DIM), jnp.float32), 'gamma_media': jnp.ones((DIM,), jnp.float32), 'beta_media': jnp.zeros((DIM,), jnp.float32), 'gamma_lat': jnp.ones((DIM,), jnp.float32), 'beta_lat': jnp.zeros((DIM,), jnp.float32), 'Wq': jax.random.normal(ks[2], (DIM, INNER), jnp.float32) * sd, 'bq': jnp.zeros((INNER,), jnp.float32), 'Wkv': jax.random.normal(ks[3], (DIM, 2 * INNER), jnp.float32) * sd, 'bkv': jnp.zeros((2 * INNER,), jnp.float32), 'Wo': jax.random.normal(ks[4], (INNER, DIM), jnp.float32) * sd, 'bo': jnp.zeros((DIM,), jnp.float32)}
    _L1_xattn_all = _L1_xattn_setup()
    _L1_xattn_in = {k: v for k, v in _L1_xattn_all.items() if k in ('gamma_media', 'beta_media', 'gamma_lat', 'beta_lat', 'Wq', 'bq', 'Wkv', 'bkv', 'Wo', 'bo')}
    del _L1_xattn_all

    def _L1_ffn_setup():
        import jax, jax.numpy as jnp
        import numpy as np
        N_EXPERTS = 32
        TOP_K = 8
        N_GROUP = 4
        TOPK_GROUP = 2
        ROUTED_SCALING = 2.5

        def _gate(x, gate_w, gate_bias):
            T, E = (x.shape[0], gate_w.shape[0])
            logits = jnp.einsum('th,eh->te', x, gate_w)
            scores = jax.nn.sigmoid(logits)
            scores_choice = scores + gate_bias[None, :]
            grp = scores_choice.reshape(T, N_GROUP, E // N_GROUP)
            top2, _ = jax.lax.top_k(grp, 2)
            group_scores = top2.sum(-1)
            _, grp_idx = jax.lax.top_k(group_scores, TOPK_GROUP)
            group_mask = jax.nn.one_hot(grp_idx, N_GROUP, dtype=scores.dtype).sum(1)
            expert_mask = jnp.repeat(group_mask, E // N_GROUP, axis=1)
            masked = jnp.where(expert_mask > 0, scores_choice, 0.0)
            _, topk_idx = jax.lax.top_k(masked, TOP_K)
            topk_w = jnp.take_along_axis(scores, topk_idx, axis=1)
            topk_w = topk_w / (topk_w.sum(-1, keepdims=True) + 1e-20)
            topk_w = topk_w * ROUTED_SCALING
            return (topk_idx, topk_w)

        def _mlp(x, wg, wu, wd):
            return jnp.einsum('...i,hi->...h', jax.nn.silu(jnp.einsum('...h,ih->...i', x, wg)) * jnp.einsum('...h,ih->...i', x, wu), wd)
        key = jax.random.key(seed)
        ks = jax.random.split(key, 9)
        B, S, H, I = (2, 64, 128, 64)
        w = 0.02
        return {'hidden_states': jax.random.normal(ks[0], (B, S, H), jnp.float32), 'gate_w': jax.random.normal(ks[1], (N_EXPERTS, H), jnp.float32) * w, 'gate_bias': jax.random.normal(ks[2], (N_EXPERTS,), jnp.float32) * w, 'expert_gate': jax.random.normal(ks[3], (N_EXPERTS, I, H), jnp.float32) * w, 'expert_up': jax.random.normal(ks[4], (N_EXPERTS, I, H), jnp.float32) * w, 'expert_down': jax.random.normal(ks[5], (N_EXPERTS, H, I), jnp.float32) * w, 'shared_gate': jax.random.normal(ks[6], (2 * I, H), jnp.float32) * w, 'shared_up': jax.random.normal(ks[7], (2 * I, H), jnp.float32) * w, 'shared_down': jax.random.normal(ks[8], (H, 2 * I), jnp.float32) * w}
    _L1_ffn_all = _L1_ffn_setup()
    _L1_ffn_in = {k: v for k, v in _L1_ffn_all.items() if k in ('gate_w', 'gate_bias', 'expert_gate', 'expert_up', 'expert_down', 'shared_gate', 'shared_up', 'shared_down')}
    del _L1_ffn_all
    return {'x': x, 'ctx_1024': ctx_1024, 'mask_BxS2_bf1': mask_BxS2_bf1, 'L0_attn_qkv_w': _L0_attn_in['qkv_w'], 'L0_attn_qkv_b': _L0_attn_in['qkv_b'], 'L0_attn_gate_w': _L0_attn_in['gate_w'], 'L0_attn_gate_b': _L0_attn_in['gate_b'], 'L0_attn_ln_g': _L0_attn_in['ln_g'], 'L0_attn_ln_b': _L0_attn_in['ln_b'], 'L0_xattn_Wq': _L0_xattn_in['Wq'], 'L0_xattn_bq': _L0_xattn_in['bq'], 'L0_xattn_Wkv': _L0_xattn_in['Wkv'], 'L0_xattn_bkv': _L0_xattn_in['bkv'], 'L0_xattn_Wo': _L0_xattn_in['Wo'], 'L0_xattn_bo': _L0_xattn_in['bo'], 'L0_ffn_gate_w': _L0_ffn_in['gate_w'], 'L0_ffn_exp_gate': _L0_ffn_in['exp_gate'], 'L0_ffn_exp_up': _L0_ffn_in['exp_up'], 'L0_ffn_exp_down': _L0_ffn_in['exp_down'], 'L0_ffn_sh_gate': _L0_ffn_in['sh_gate'], 'L0_ffn_sh_up': _L0_ffn_in['sh_up'], 'L0_ffn_sh_down': _L0_ffn_in['sh_down'], 'L1_attn_w': _L1_attn_in['w'], 'L1_attn_u': _L1_attn_in['u'], 'L1_attn_bias': _L1_attn_in['bias'], 'L1_xattn_gamma_media': _L1_xattn_in['gamma_media'], 'L1_xattn_beta_media': _L1_xattn_in['beta_media'], 'L1_xattn_gamma_lat': _L1_xattn_in['gamma_lat'], 'L1_xattn_beta_lat': _L1_xattn_in['beta_lat'], 'L1_xattn_Wq': _L1_xattn_in['Wq'], 'L1_xattn_bq': _L1_xattn_in['bq'], 'L1_xattn_Wkv': _L1_xattn_in['Wkv'], 'L1_xattn_bkv': _L1_xattn_in['bkv'], 'L1_xattn_Wo': _L1_xattn_in['Wo'], 'L1_xattn_bo': _L1_xattn_in['bo'], 'L1_ffn_gate_w': _L1_ffn_in['gate_w'], 'L1_ffn_gate_bias': _L1_ffn_in['gate_bias'], 'L1_ffn_expert_gate': _L1_ffn_in['expert_gate'], 'L1_ffn_expert_up': _L1_ffn_in['expert_up'], 'L1_ffn_expert_down': _L1_ffn_in['expert_down'], 'L1_ffn_shared_gate': _L1_ffn_in['shared_gate'], 'L1_ffn_shared_up': _L1_ffn_in['shared_up'], 'L1_ffn_shared_down': _L1_ffn_in['shared_down']}

def reference(x, ctx_1024, mask_BxS2_bf1, L0_attn_qkv_w, L0_attn_qkv_b, L0_attn_gate_w, L0_attn_gate_b, L0_attn_ln_g, L0_attn_ln_b, L0_xattn_Wq, L0_xattn_bq, L0_xattn_Wkv, L0_xattn_bkv, L0_xattn_Wo, L0_xattn_bo, L0_ffn_gate_w, L0_ffn_exp_gate, L0_ffn_exp_up, L0_ffn_exp_down, L0_ffn_sh_gate, L0_ffn_sh_up, L0_ffn_sh_down, L1_attn_w, L1_attn_u, L1_attn_bias, L1_xattn_gamma_media, L1_xattn_beta_media, L1_xattn_gamma_lat, L1_xattn_beta_lat, L1_xattn_Wq, L1_xattn_bq, L1_xattn_Wkv, L1_xattn_bkv, L1_xattn_Wo, L1_xattn_bo, L1_ffn_gate_w, L1_ffn_gate_bias, L1_ffn_expert_gate, L1_ffn_expert_up, L1_ffn_expert_down, L1_ffn_shared_gate, L1_ffn_shared_up, L1_ffn_shared_down):
    import jax
    import jax.numpy as jnp

    def _L0_attn_ref(x, qkv_w, qkv_b, gate_w, gate_b, ln_g, ln_b):
        import jax, jax.numpy as jnp
        import numpy as np
        D_MODEL = 128
        LN_EPS = 1e-05
        DEN_EPS = 1e-06

        def _layer_norm(x, g, b):
            mu = jnp.mean(x, axis=-1, keepdims=True)
            var = jnp.mean(jnp.square(x - mu), axis=-1, keepdims=True)
            return (x - mu) * jax.lax.rsqrt(var + LN_EPS) * g + b
        B, T, D = x.shape
        xn = _layer_norm(x, ln_g, ln_b)
        qkv = xn @ qkv_w + qkv_b
        q, k, v = jnp.split(qkv, 3, axis=-1)
        gate = jax.nn.sigmoid(xn @ gate_w + gate_b)
        k = k * gate
        q = jax.nn.elu(q) + 1.0
        k = jax.nn.elu(k) + 1.0
        attn = jnp.einsum('btd,bsd->bts', q, k)
        mask = jnp.tril(jnp.ones((T, T), dtype=attn.dtype))
        attn = attn * mask
        out_num = jnp.einsum('bts,bsd->btd', attn, v)
        k_cumsum = jnp.cumsum(k, axis=1)
        out_den = jnp.sum(q * k_cumsum, axis=-1, keepdims=True) + DEN_EPS
        return out_num / out_den

    def _L0_xattn_ref(x, context, context_mask, Wq, bq, Wkv, bkv, Wo, bo):
        import jax, jax.numpy as jnp
        import numpy as np
        GAMMA = 10.0
        BASE = 10000.0
        SCALE = 64 ** (-0.5)
        NUM_HEADS = 16

        def _larope(t, seq_len):
            B, H, L, D = t.shape
            inv_freq = 1.0 / BASE ** (jnp.arange(0, D, 2, dtype=jnp.float32) / D)
            pos = GAMMA * (jnp.arange(L, dtype=jnp.float32) / float(seq_len))
            ang = pos[:, None] * inv_freq
            cos = jnp.cos(ang)
            sin = jnp.sin(ang)
            te, to = (t[..., 0::2], t[..., 1::2])
            re = te * cos - to * sin
            ro = te * sin + to * cos
            return jnp.stack([re, ro], axis=-1).reshape(t.shape)
        B, Lq, D = x.shape
        Lk = context.shape[1]
        H = NUM_HEADS
        hd = D // H
        q = x @ Wq + bq
        kv = context @ Wkv + bkv
        k, v = jnp.split(kv, 2, axis=-1)
        q = q.reshape(B, Lq, H, hd).transpose(0, 2, 1, 3)
        k = k.reshape(B, Lk, H, hd).transpose(0, 2, 1, 3)
        v = v.reshape(B, Lk, H, hd).transpose(0, 2, 1, 3)
        q = _larope(q, Lq)
        k = _larope(k, Lk)
        scores = jnp.einsum('bhqd,bhkd->bhqk', q, k) * SCALE
        scores = jnp.where(context_mask[:, None, None, :], scores, -jnp.inf)
        attn = jax.nn.softmax(scores, axis=-1)
        out = jnp.einsum('bhqk,bhkd->bhqd', attn, v)
        out = out.transpose(0, 2, 1, 3).reshape(B, Lq, H * hd)
        return out @ Wo + bo

    def _L0_ffn_ref(hidden_states, gate_w, exp_gate, exp_up, exp_down, sh_gate, sh_up, sh_down):
        import jax, jax.numpy as jnp
        import numpy as np
        B, L, D = (4, 256, 128)
        E, K, S = (8, 2, 2)
        F = 176
        SCALE = 1.0
        INIT = 0.02

        def _swiglu(x, wg, wu, wd):
            return jax.nn.silu(x @ wg) * (x @ wu) @ wd
        Bx, Lx, Dx = hidden_states.shape
        x = hidden_states.reshape(-1, Dx)
        T = x.shape[0]
        shared = jnp.zeros_like(x)
        for i in range(sh_gate.shape[0]):
            shared = shared + _swiglu(x, sh_gate[i], sh_up[i], sh_down[i])
        logits = x @ gate_w
        probs = jax.nn.softmax(logits.astype(jnp.float32), axis=-1)
        w, sel = jax.lax.top_k(probs, K)
        w = w / jnp.sum(w, axis=-1, keepdims=True)
        w = w.astype(hidden_states.dtype)
        Wte = jnp.zeros((T, exp_gate.shape[0]), hidden_states.dtype)
        Wte = Wte.at[jnp.arange(T)[:, None], sel].add(w)
        routed = jnp.zeros_like(x)
        for e in range(exp_gate.shape[0]):
            routed = routed + Wte[:, e:e + 1] * _swiglu(x, exp_gate[e], exp_up[e], exp_down[e])
        out = shared + SCALE * routed
        return out.reshape(Bx, Lx, Dx)

    def _L1_attn_ref(input_seq, w, u, bias):
        import jax, jax.numpy as jnp
        import numpy as np
        import math
        INPUT_SIZE = 128
        HIDDEN = 128
        SEQ_LEN = 32
        BATCH = 128

        def _lstm(input_seq, w, u, bias):
            H = u.shape[0]
            B = input_seq.shape[1]
            x_proj = jnp.einsum('sbi,ih->sbh', input_seq, w) + bias

            def step(carry, xp_t):
                h_prev, c_prev = carry
                g = xp_t + h_prev @ u
                gates = jax.nn.sigmoid(g[:, :3 * H])
                c_cand = jnp.tanh(g[:, 3 * H:])
                ig, fg, og = (gates[:, :H], gates[:, H:2 * H], gates[:, 2 * H:])
                c = fg * c_prev + ig * c_cand
                h = og * jnp.tanh(c)
                return ((h, c), h)
            init = (jnp.zeros((B, H), dtype=input_seq.dtype), jnp.zeros((B, H), dtype=input_seq.dtype))
            _, hs = jax.lax.scan(step, init, x_proj)
            return hs
        return _lstm(input_seq, w, u, bias)

    def _L1_xattn_ref(x, latents, gamma_media, beta_media, gamma_lat, beta_lat, Wq, bq, Wkv, bkv, Wo, bo):
        import jax, jax.numpy as jnp
        import numpy as np
        B, M, N, DIM, DH, H = (8, 512, 64, 128, 128, 8)
        INNER = DH * H
        EPS = 1e-05

        def _layernorm(x, g, b):
            mu = jnp.mean(x, axis=-1, keepdims=True)
            var = jnp.var(x, axis=-1, keepdims=True)
            return (x - mu) * jax.lax.rsqrt(var + EPS) * g + b
        b = x.shape[0]
        xn = _layernorm(x, gamma_media, beta_media)
        ln = _layernorm(latents, gamma_lat, beta_lat)
        q = ln @ Wq + bq
        kv_input = jnp.concatenate([xn, ln], axis=1)
        kv = kv_input @ Wkv + bkv
        k, v = jnp.split(kv, 2, axis=-1)

        def to_heads(t):
            return t.reshape(b, t.shape[1], H, DH).transpose(0, 2, 1, 3)
        q, k, v = (to_heads(q), to_heads(k), to_heads(v))
        q = q * DH ** (-0.5)
        sim = jnp.einsum('bhid,bhjd->bhij', q, k)
        attn = jax.nn.softmax(sim, axis=-1)
        out = jnp.einsum('bhij,bhjd->bhid', attn, v)
        out = out.transpose(0, 2, 1, 3).reshape(b, -1, INNER)
        return out @ Wo + bo

    def _L1_ffn_ref(hidden_states, gate_w, gate_bias, expert_gate, expert_up, expert_down, shared_gate, shared_up, shared_down):
        import jax, jax.numpy as jnp
        import numpy as np
        N_EXPERTS = 32
        TOP_K = 8
        N_GROUP = 4
        TOPK_GROUP = 2
        ROUTED_SCALING = 2.5

        def _gate(x, gate_w, gate_bias):
            T, E = (x.shape[0], gate_w.shape[0])
            logits = jnp.einsum('th,eh->te', x, gate_w)
            scores = jax.nn.sigmoid(logits)
            scores_choice = scores + gate_bias[None, :]
            grp = scores_choice.reshape(T, N_GROUP, E // N_GROUP)
            top2, _ = jax.lax.top_k(grp, 2)
            group_scores = top2.sum(-1)
            _, grp_idx = jax.lax.top_k(group_scores, TOPK_GROUP)
            group_mask = jax.nn.one_hot(grp_idx, N_GROUP, dtype=scores.dtype).sum(1)
            expert_mask = jnp.repeat(group_mask, E // N_GROUP, axis=1)
            masked = jnp.where(expert_mask > 0, scores_choice, 0.0)
            _, topk_idx = jax.lax.top_k(masked, TOP_K)
            topk_w = jnp.take_along_axis(scores, topk_idx, axis=1)
            topk_w = topk_w / (topk_w.sum(-1, keepdims=True) + 1e-20)
            topk_w = topk_w * ROUTED_SCALING
            return (topk_idx, topk_w)

        def _mlp(x, wg, wu, wd):
            return jnp.einsum('...i,hi->...h', jax.nn.silu(jnp.einsum('...h,ih->...i', x, wg)) * jnp.einsum('...h,ih->...i', x, wu), wd)
        orig_shape = hidden_states.shape
        H = orig_shape[-1]
        residuals = hidden_states
        x = hidden_states.reshape(-1, H)
        topk_idx, topk_w = _gate(x, gate_w, gate_bias)
        g = jnp.einsum('th,eih->eti', x, expert_gate)
        u = jnp.einsum('th,eih->eti', x, expert_up)
        outs = jnp.einsum('eti,ehi->eth', jax.nn.silu(g) * u, expert_down)
        outs_t = jnp.transpose(outs, (1, 0, 2))
        gathered = jnp.take_along_axis(outs_t, topk_idx[:, :, None], axis=1)
        final = (gathered * topk_w[:, :, None]).sum(1)
        shared = _mlp(residuals, shared_gate, shared_up, shared_down)
        return final.reshape(orig_shape) + shared
    x = x + _L0_attn_ref(_layernorm(x, axis=-1), L0_attn_qkv_w, L0_attn_qkv_b, L0_attn_gate_w, L0_attn_gate_b, L0_attn_ln_g, L0_attn_ln_b)
    x = x + _L0_xattn_ref(_layernorm(x, axis=-1), ctx_1024, mask_BxS2_bf1, L0_xattn_Wq, L0_xattn_bq, L0_xattn_Wkv, L0_xattn_bkv, L0_xattn_Wo, L0_xattn_bo)
    x = x + _L0_ffn_ref(_layernorm(x, axis=-1), L0_ffn_gate_w, L0_ffn_exp_gate, L0_ffn_exp_up, L0_ffn_exp_down, L0_ffn_sh_gate, L0_ffn_sh_up, L0_ffn_sh_down)
    x = x + _L1_attn_ref(_layernorm(x, axis=-1), L1_attn_w, L1_attn_u, L1_attn_bias)
    x = x + _L1_xattn_ref(ctx_1024, _layernorm(x, axis=-1), L1_xattn_gamma_media, L1_xattn_beta_media, L1_xattn_gamma_lat, L1_xattn_beta_lat, L1_xattn_Wq, L1_xattn_bq, L1_xattn_Wkv, L1_xattn_bkv, L1_xattn_Wo, L1_xattn_bo)
    x = x + _L1_ffn_ref(_layernorm(x, axis=-1), L1_ffn_gate_w, L1_ffn_gate_bias, L1_ffn_expert_gate, L1_ffn_expert_up, L1_ffn_expert_down, L1_ffn_shared_gate, L1_ffn_shared_up, L1_ffn_shared_down)
    return x

_drawn_inputs = setup_inputs


def setup_inputs(seed=0):
    import zlib

    import numpy as np

    out = dict(_drawn_inputs(seed))
    spreads = {'L0_attn_ln_g': (1.0, 0.6),
     'L0_attn_ln_b': (0.0, 0.1),
     'L0_xattn_bq': (0.0, 0.8),
     'L0_xattn_bkv': (0.0, 0.1),
     'L0_xattn_bo': (0.0, 0.1),
     'L1_xattn_gamma_media': (1.0, 0.6),
     'L1_xattn_beta_media': (0.0, 0.74),
     'L1_xattn_gamma_lat': (1.0, 0.6),
     'L1_xattn_beta_lat': (0.0, 2.0),
     'L1_xattn_bq': (0.0, 2.0),
     'L1_xattn_bkv': (0.0, 0.1),
     'L1_xattn_bo': (0.0, 0.1)}
    factors = {'L0_attn_gate_w': 8.0,
     'L0_attn_gate_b': 42.682,
     'L0_ffn_gate_w': 8.0,
     'L0_ffn_exp_gate': 8.0,
     'L0_ffn_exp_up': 8.0,
     'L0_ffn_exp_down': 8.0,
     'L0_ffn_sh_gate': 6.744,
     'L0_ffn_sh_up': 6.843,
     'L0_ffn_sh_down': 6.793,
     'L1_attn_bias': 5.86,
     'L1_xattn_Wq': 8.0,
     'L1_ffn_gate_w': 8.0,
     'L1_ffn_gate_bias': 8.0,
     'L1_ffn_expert_gate': 8.0,
     'L1_ffn_expert_up': 8.0,
     'L1_ffn_expert_down': 8.0,
     'L1_ffn_shared_gate': 8.0,
     'L1_ffn_shared_up': 8.0,
     'L1_ffn_shared_down': 8.0}
    for name, (base, spread) in spreads.items():
        noise = np.random.default_rng([zlib.crc32(name.encode()), seed]).standard_normal(out[name].shape)
        drawn = base * np.exp(spread * noise) if base else spread * noise
        out[name] = jnp.asarray(drawn.astype(out[name].dtype))
    for name, factor in factors.items():
        out[name] = (out[name] * factor).astype(out[name].dtype)
    return out
```

```python
from contextlib import ExitStack

import numpy as np
import concourse.bass as bass
from concourse import mybir

F32 = mybir.dt.float32
F32R = mybir.dt.float32r
I32 = mybir.dt.int32
U8 = mybir.dt.uint8
ALU = mybir.AluOpType
ACT = mybir.ActivationFunctionType
AX = mybir.AxisListType

P = 128
T = 1024
NT = T // P
HALF = 512
LC = 6404
NK = -(-LC // P)
LAST = LC - P
REPEATED = NK * P - LC
LN_EPS = 1e-5
DEN_EPS = 1e-6
H0, D0 = 16, 8
G0 = 4
NG = H0 // G0
ROW = 32
U0 = 3
NI = NK // U0
SAFE = 40.0
SAFE_BITS = int(np.float32(SAFE).view(np.int32))
MASKED = -1e30


def stepper(engine):
    done = {}

    def step(instruction, semaphore, wait=True):
        instruction.then_inc(semaphore, 1)
        done[semaphore.name] = done.get(semaphore.name, 0) + 1
        if wait:
            engine.wait_ge(semaphore, done[semaphore.name])

    return step


def layer_norm(nc, dve, step, s_chain, stats, moments, src, dst, eps_done, root_done, out_done, n=NT, first=0):
    for t in range(n):
        step(nc.vector.bn_stats(stats[:, t, :], src[:, t, :]), s_chain, wait=t == n - 1)
    for t in range(n):
        step(nc.vector.bn_aggr(moments[:, t, :], stats[:, t, :]), s_chain, wait=t == n - 1)
    step(nc.vector.tensor_scalar(moments[:, 0:n, 1], moments[:, 0:n, 1], LN_EPS, None, ALU.add), eps_done)
    dve.wait_ge(root_done, first + 1)
    step(nc.vector.reciprocal(moments[:, 0:n, 1], moments[:, 0:n, 1]), s_chain)
    for t in range(n):
        step(nc.vector.tensor_scalar(dst[:, t, :], src[:, t, :], moments[:, t, 0:1], moments[:, t, 1:2],
                                     ALU.subtract, ALU.mult), out_done, wait=t == n - 1)


def root(nc, act, moments, eps_done, root_done, n=NT, first=0):
    act.wait_ge(eps_done, first + 1)
    nc.scalar.activation(moments[:, 0:n, 1], moments[:, 0:n, 1], ACT.Sqrt).then_inc(root_done, 1)


def transpose_tiles(nc, pe, bank, src, ident, done):
    for t in range(NT):
        last = nc.tensor.transpose(bank[:, t * P:(t + 1) * P], src[:, t, :], ident[:, :])
        if t % 4 == 3:
            last.then_inc(done, 1)


def columns(ap, width=P):
    return ap.rearrange("(c p) -> p c", p=width)


def spread(ap):
    return ap.rearrange("(a n) -> a n", a=1).to_broadcast([P, ap.shape[0]])


class Memory:

    taken = []

    def __init__(self, nc, stack, stage):
        self.nc, self.stack, self.stage = nc, stack, stage

    def sb(self, name, shape, dtype=F32):
        return self.stack.enter_context(self.nc.sbuf_tensor(f"{self.stage}_{name}", shape, dtype))

    def sem(self, name):
        semaphore = self.nc.alloc_semaphore(f"{self.stage}_{name}")
        self.taken.append(semaphore)
        return semaphore


def linear_attention(nc, kept, ps, a):
    with ExitStack() as stack:
        m = Memory(nc, stack, "lin")
        qkv_w, gate_w = m.sb("qkv_w", [P, 3 * P]), m.sb("gate_w", [P, P])
        biases = m.sb("biases", [P, 6])
        v_bias = m.sb("v_bias", [P, P])
        stats, moments, moments2 = m.sb("stats", [P, NT, 6]), m.sb("moments", [P, NT, 2]), m.sb("moments2", [P, NT, 2])
        normed, normed2 = m.sb("normed", [P, NT, P]), m.sb("normed2", [P, NT, P])
        xn = m.sb("xn", [P, T])
        q, k, gate, small = (m.sb(n, [P, T]) for n in ("q", "k", "gate", "small"))
        small_k = m.sb("small_k", [P, T])
        v = m.sb("v", [P, NT, P + 1])
        scores = m.sb("scores", [P, NT, T])
        den = m.sb("den", [P, NT])
        s_load = m.sem("loaded")
        s_vec, s_eps, s_root, s_norm, s_norm2 = (m.sem(n) for n in ("vector_step", "variance", "root", "normed", "normed2"))
        s_eps2, s_root2 = m.sem("variance2"), m.sem("root2")
        s_turned, s_xn_a, s_xn_v = m.sem("turned"), m.sem("xn_scalar"), m.sem("xn_vector")
        s_proj, s_gate, s_pre, s_exp, s_qk, s_v = (m.sem(n) for n in ("projected", "gate", "pre_elu", "exps", "q_k", "v"))
        s_score, s_sc, s_sum, s_x2 = (m.sem(n) for n in ("scores", "scores_kept", "sums", "x_done"))
        s_cp = m.sem("scores_copied")
        x, ident, tri = kept["x"], kept["ident"], m.sb("tri", [P, P])
        bank = ps[:, :, :].rearrange("p b c -> p (b c)")
        pairs = [(s, c) for s in range(NT) for c in range(s // 4, 2)]

        with nc.Block() as block:
            @block.sync
            def _(sp):
                sp.dma_start(qkv_w[:, :], a["L0_attn_qkv_w"]).then_inc(s_load, 16)
                sp.dma_start(gate_w[:, :], a["L0_attn_gate_w"]).then_inc(s_load, 16)
                sp.dma_start(v_bias[:, :], spread(a["L0_attn_qkv_b"][2 * P:3 * P])).then_inc(s_load, 16)
                sp.dma_start(biases[:, 0:3], columns(a["L0_attn_qkv_b"])).then_inc(s_load, 16)
                sp.dma_start(biases[:, 3:4], columns(a["L0_attn_gate_b"])).then_inc(s_load, 16)
                sp.dma_start(biases[:, 4:5], columns(a["L0_attn_ln_g"])).then_inc(s_load, 16)
                sp.dma_start(biases[:, 5:6], columns(a["L0_attn_ln_b"])).then_inc(s_load, 16)
                sp.dma_start(tri[:, :], a["tri"]).then_inc(s_load, 16)
                sp.wait_ge(s_load, 8 * 16)

            @block.scalar
            def _(act):
                root(nc, act, moments, s_eps, s_root)
                root(nc, act, moments2, s_eps2, s_root2)
                act.wait_ge(s_load, 8 * 16)
                act.wait_ge(s_turned, 1)
                nc.scalar.activation(xn[:, 0:HALF], bank[:, 0:HALF], ACT.Identity, bias=biases[:, 5:6],
                                     scale=biases[:, 4:5]).then_inc(s_xn_a, 1)
                act.wait_ge(s_proj, 2)
                nc.scalar.activation(gate[:, :], bank[:, 2 * T:3 * T], ACT.Sigmoid, bias=biases[:, 3:4]).then_inc(s_gate, 1)
                act.wait_ge(s_pre, 1)
                nc.scalar.activation(small[:, :], small[:, :], ACT.Exp).then_inc(s_exp, 1)
                act.wait_ge(s_pre, 2)
                nc.scalar.activation(small_k[:, :], small_k[:, :], ACT.Exp).then_inc(s_exp, 1)
                for n, (s, c) in enumerate(pairs):
                    if c * 4 > s:
                        act.wait_ge(s_score, n + 1)
                        nc.scalar.activation(scores[:, s, c * HALF:(c + 1) * HALF], ps[:, n % 4, :], ACT.Copy).then_inc(s_cp, 1)

            @block.vector
            def _(dve):
                step = stepper(dve)
                step(nc.vector.memset(v[:, :, P:P + 1], 1.0), s_vec, wait=False)
                layer_norm(nc, dve, step, s_vec, stats, moments, x, normed, s_eps, s_root, s_norm)
                layer_norm(nc, dve, step, s_vec, stats, moments2, normed, normed2, s_eps2, s_root2, s_norm2)
                dve.wait_ge(s_load, 8 * 16)
                dve.wait_ge(s_turned, 2)
                step(nc.vector.tensor_scalar(xn[:, HALF:T], bank[:, HALF:T], biases[:, 4:5], biases[:, 5:6],
                                             ALU.mult, ALU.add), s_xn_v)
                dve.wait_ge(s_proj, 1)
                step(nc.vector.tensor_scalar(q[:, :], bank[:, T:2 * T], biases[:, 0:1], None, ALU.add), s_vec)
                step(nc.vector.tensor_scalar(small[:, :], q[:, :], 0.0, None, ALU.min), s_pre)
                dve.wait_ge(s_proj, 3)
                dve.wait_ge(s_gate, 1)
                step(nc.vector.scalar_tensor_tensor(k[:, :], bank[:, 3 * T:4 * T], biases[:, 1:2], gate[:, :],
                                                    ALU.add, ALU.mult), s_vec)
                step(nc.vector.tensor_scalar(small_k[:, :], k[:, :], 0.0, None, ALU.min), s_pre)
                dve.wait_ge(s_exp, 1)
                step(nc.vector.scalar_tensor_tensor(q[:, :], q[:, :], 0.0, small[:, :], ALU.max, ALU.add), s_qk)
                dve.wait_ge(s_exp, 2)
                step(nc.vector.scalar_tensor_tensor(k[:, :], k[:, :], 0.0, small_k[:, :], ALU.max, ALU.add), s_qk)
                dve.wait_ge(s_proj, 4)
                step(nc.vector.tensor_tensor(v[:, :, 0:P], bank[:, 0:T].rearrange("p (t c) -> p t c", c=P),
                                             v_bias[:, :].unsqueeze(1).to_broadcast([P, NT, P]), ALU.add), s_v)
                for n, (s, c) in enumerate(pairs):
                    if c * 4 > s:
                        continue
                    dve.wait_ge(s_score, n + 1)
                    d, e = s * P, (s + 1) * P
                    b = d - c * HALF
                    if e < (c + 1) * HALF:
                        step(nc.vector.tensor_copy(scores[:, s, e:(c + 1) * HALF], ps[:, n % 4, b + P:HALF]), s_vec, wait=False)
                    step(nc.vector.tensor_tensor(scores[:, s, d:e], ps[:, n % 4, b:b + P], tri[:, :], ALU.mult), s_sc)
                for t in range(NT):
                    dve.wait_ge(s_sum, t + 1)
                    sums = ps[:, 4 + t % 4, 0:P + 1]
                    step(nc.vector.tensor_scalar(den[:, t:t + 1], sums[:, P:P + 1], DEN_EPS, None, ALU.add), s_vec)
                    step(nc.vector.reciprocal(den[:, t:t + 1], den[:, t:t + 1]), s_vec)
                    step(nc.vector.scalar_tensor_tensor(x[:, t, :], sums[:, 0:P], den[:, t:t + 1], x[:, t, :],
                                                        ALU.mult, ALU.add), s_x2, wait=False)

            @block.tensor
            def _(pe):
                pe.wait_ge(s_load, 8 * 16)
                pe.wait_ge(s_norm2, NT)
                transpose_tiles(nc, pe, bank, normed2, ident, s_turned)
                pe.wait_ge(s_xn_a, 1)
                pe.wait_ge(s_xn_v, 1)
                for w, b in ((qkv_w[:, 0:P], 2), (gate_w[:, :], 4), (qkv_w[:, P:2 * P], 6)):
                    for c in range(2):
                        last = nc.tensor.matmul(ps[:, b + c, :], w, xn[:, c * HALF:(c + 1) * HALF], start=True, stop=True)
                    last.then_inc(s_proj, 1)
                for t in range(NT):
                    last = nc.tensor.matmul(bank[:, t * P:(t + 1) * P], xn[:, t * P:(t + 1) * P], qkv_w[:, 2 * P:3 * P],
                                            start=True, stop=True)
                last.then_inc(s_proj, 1)
                pe.wait_ge(s_qk, 2)
                pe.wait_ge(s_v, 1)
                diagonal = off = 0
                kept_by = []
                for s, c in pairs:
                    kept_by.append((diagonal, off))
                    diagonal, off = (diagonal, off + 1) if c * 4 > s else (diagonal + 1, off)
                kept_by.append((diagonal, off))
                for n, (s, c) in enumerate(pairs):
                    if n >= 4:
                        for semaphore, count in zip((s_sc, s_cp), kept_by[n - 3]):
                            if count:
                                pe.wait_ge(semaphore, count)
                    lo = max(s * P, c * HALF)
                    nc.tensor.matmul(ps[:, n % 4, lo - c * HALF:HALF], k[:, s * P:(s + 1) * P], q[:, lo:(c + 1) * HALF],
                                     start=True, stop=True).then_inc(s_score, 1)
                pe.wait_ge(s_sc, NT)
                pe.wait_ge(s_cp, len(pairs) - NT)
                for t in range(NT):
                    if t >= 4:
                        pe.wait_ge(s_x2, t - 3)
                    for s in range(t + 1):
                        last = nc.tensor.matmul(ps[:, 4 + t % 4, 0:P + 1], scores[:, s, t * P:(t + 1) * P], v[:, s, :],
                                                start=s == 0, stop=s == t)
                    last.then_inc(s_sum, 1)


def context_keys(nc, kept, ps, a, stack):
    m = Memory(nc, stack, "ctx")
    key_rows = m.sb("key_rows", [P, NG, NK * P], F32R)
    values = m.sb("values", [P, NK, H0, D0 + 1])
    key_bound = m.sb("key_bound", [P, H0])
    kept.update(key_rows=key_rows, values=values, key_bound=key_bound)
    with ExitStack() as own:
        m = Memory(nc, own, "ctxb")
        rope = m.sb("rope", [P, NK, 2, D0 // 2])
        mask_u8, mask, mask_bias, fresh = m.sb("mask_u8", [P, NK], U8), m.sb("mask", [P, NK]), m.sb("mask_bias", [P, NK], F32R), m.sb("fresh", [P, 1])
        w_kv, b_kv = m.sb("w_kv", [P, 2 * P]), m.sb("b_kv", [P, 2 * P])
        rows, turned = m.sb("rows", [P, U0, P]), m.sb("turned", [P, U0, P])
        kv = m.sb("kv", [P, U0, 2 * P])
        rotated = m.sb("rotated", [P, U0, P])
        part = [m.sb(f"part{n}", [P, U0, H0, D0 // 2]) for n in range(4)]
        squares, norms, best = m.sb("squares", [P, U0, P]), m.sb("norms", [P, U0, H0]), m.sb("best", [P, U0, H0])
        packed = m.sb("packed", [P, U0, NG * G0, ROW], F32R)
        s_load, s_rows = m.sem("loaded"), [m.sem(f"rows_loaded{n}") for n in range(U0)]
        s_turn, s_turned, s_kv, s_kv_kept, s_packed, s_keys, s_keys_kept = (m.sem(n) for n in (
            "rows_turned", "turned_kept", "kv_projected", "kv_kept", "packed", "keys_turned", "keys_kept"))
        s_vec, s_pool, s_rot, s_copied, s_mask, s_norm, s_all, s_bound = (m.sem(n) for n in (
            "vector_step", "pool_step", "rotated", "high_copied", "mask", "norms", "bound_of_all", "bound_root"))
        s_prod = m.sem("products")
        ctx = a["ctx_1024"][0]
        ident = kept["ident"]

        with nc.Block() as block:
            @block.sync
            def _(sp):
                mask_rows = a["mask_BxS2_bf1"][0]
                sp.dma_start(rope[:, :, :, :], a["rope_k"]).then_inc(s_load, 16)
                sp.dma_start(w_kv[:, :], a["L0_xattn_Wkv"]).then_inc(s_load, 16)
                sp.dma_start(b_kv[:, :], spread(a["L0_xattn_bkv"])).then_inc(s_load, 16)
                sp.dma_start(fresh[:, :], a["fresh"]).then_inc(s_load, 16)
                sp.dma_start(mask_u8[:, 0:NK - 1], mask_rows[0:(NK - 1) * P].rearrange("(t p) -> p t", p=P)).then_inc(s_load, 16)
                sp.dma_start(mask_u8[:, NK - 1:NK], columns(mask_rows[LAST:LC])).then_inc(s_load, 16)
                for t in range(NK):
                    if t >= U0:
                        sp.wait_ge(s_turn, t // U0)
                    first = min(t * P, LAST)
                    sp.dma_start(rows[:, t % U0, :], ctx[first:first + P, :]).then_inc(s_rows[t % U0], 16)
                sp.wait_ge(s_load, 6 * 16)

            @block.tensor
            def _(pe):
                def project(i):
                    for n in range(U0):
                        pe.wait_ge(s_rows[n], 16 * i + 16)
                        last = nc.tensor.transpose(ps[:, 0, n * P:(n + 1) * P], rows[:, n, :], ident[:, :])
                    last.then_inc(s_turn, 1)
                    pe.wait_ge(s_turned, i + 1)
                    for n in range(U0):
                        last = nc.tensor.matmul(ps[:, 1 + n, 0:2 * P], turned[:, n, :], w_kv[:, :], start=True, stop=True)
                    last.then_inc(s_kv, 1)

                def turn_keys(i):
                    for n in range(U0):
                        for g in range(NG):
                            last = nc.tensor.transpose(ps[:, 4 + n, g * P:(g + 1) * P],
                                                       packed[:, n, g * G0:(g + 1) * G0, :].bitcast(F32).rearrange("p h r -> p (h r)"),
                                                       ident[:, :])
                        last.then_inc(s_keys, 1)

                pe.wait_ge(s_load, 6 * 16)
                project(0)
                with pe.Fori(0, NI - 1) as i:
                    pe.wait_ge(s_kv_kept, i + 1)
                    project(i + 1)
                    pe.wait_ge(s_packed, i + 1)
                    turn_keys(i)
                pe.wait_ge(s_packed, NI)
                pe.wait_ge(s_keys_kept, (NI - 1) * U0)
                turn_keys(NI - 1)

            @block.scalar
            def _(act):
                def keep_turned(i):
                    act.wait_ge(s_turn, i + 1)
                    nc.scalar.activation(turned[:, :, :].rearrange("p n c -> p (n c)"), ps[:, 0, 0:U0 * P], ACT.Copy).then_inc(s_turned, 1)

                def keep_keys(i):
                    for n in range(U0):
                        act.wait_ge(s_keys, i * U0 + n + 2)
                        nc.scalar.activation(key_rows[:, :, bass.ds(i * (U0 * P) + n * P, P)],
                                             ps[:, 4 + n, :].rearrange("p (g c) -> p g c", g=NG), ACT.Copy).then_inc(s_keys_kept, 1)

                keep_turned(0)
                with act.Fori(0, NI - 1) as i:
                    keep_turned(i + 1)
                    keep_keys(i)
                keep_keys(NI - 1)
                act.wait_ge(s_all, 1)
                nc.scalar.activation(key_bound[:, :], key_bound[:, :], ACT.Sqrt).then_inc(s_bound, 1)

            @block.gpsimd
            def _(pool):
                with pool.Fori(0, NI) as i:
                    pool.wait_ge(s_kv_kept, i + 1)
                    even, odd = (kv[:, :, j:P:2].rearrange("p n (h d) -> p n h d", h=H0) for j in (0, 1))
                    cos, sin = (rope[:, bass.ds(i * U0, U0), j, :].unsqueeze(2).to_broadcast([P, U0, H0, D0 // 2]) for j in (0, 1))
                    nc.gpsimd.tensor_tensor(part[2][:, :, :, :], even, sin, ALU.mult).then_inc(s_pool, 1)
                    nc.gpsimd.tensor_tensor(part[3][:, :, :, :], odd, cos, ALU.mult).then_inc(s_pool, 1)
                    pool.wait_ge(s_pool, i * 2 + 2)
                    nc.gpsimd.tensor_tensor(rotated[:, :, 1:P:2].rearrange("p n (h d) -> p n h d", h=H0),
                                            part[2][:, :, :, :], part[3][:, :, :, :], ALU.add).then_inc(s_rot, 1)
                pool.wait_ge(s_norm, 1)
                nc.gpsimd.partition_all_reduce(key_bound[:, :], best[:, 0, :], P, bass.bass_isa.ReduceOp.max).then_inc(s_all, 1)

            @block.vector
            def _(dve):
                step = stepper(dve)
                step(nc.vector.memset(packed[:, :, :, :].bitcast(F32), 0.0), s_keys)
                step(nc.vector.memset(packed[:, :, :, 3 * D0:3 * D0 + 2].bitcast(F32), 1.0), s_mask)
                step(nc.vector.memset(best[:, :, :], 0.0), s_mask)
                dve.wait_ge(s_load, 6 * 16)
                step(nc.vector.tensor_copy(mask[:, :], mask_u8[:, :]), s_mask)
                step(nc.vector.tensor_scalar(mask[:, NK - 1:NK], mask[:, NK - 1:NK], fresh[:, 0:1], None, ALU.mult), s_mask)
                step(nc.vector.tensor_scalar(mask_bias[:, :], mask[:, :], -MASKED, MASKED, ALU.mult, ALU.add), s_mask)
                with dve.Fori(0, NI) as i:
                    tiles = bass.ds(i * U0, U0)
                    dve.wait_ge(s_kv, i + 1)
                    nc.vector.tensor_tensor(kv[:, :, :], ps[:, 1:1 + U0, 0:2 * P], b_kv[:, :].unsqueeze(1).to_broadcast([P, U0, 2 * P]),
                                            ALU.add).then_inc(s_kv_kept, 1)
                    dve.wait_ge(s_kv_kept, i + 1)
                    even, odd = (kv[:, :, j:P:2].rearrange("p n (h d) -> p n h d", h=H0) for j in (0, 1))
                    cos, sin = (rope[:, tiles, j, :].unsqueeze(2).to_broadcast([P, U0, H0, D0 // 2]) for j in (0, 1))
                    nc.vector.tensor_tensor(part[0][:, :, :, :], even, cos, ALU.mult).then_inc(s_prod, 1)
                    nc.vector.tensor_tensor(part[1][:, :, :, :], odd, sin, ALU.mult).then_inc(s_prod, 1)
                    dve.wait_ge(s_prod, i * 2 + 2)
                    nc.vector.tensor_tensor(rotated[:, :, 0:P:2].rearrange("p n (h d) -> p n h d", h=H0),
                                            part[0][:, :, :, :], part[1][:, :, :, :], ALU.subtract).then_inc(s_vec, 1)
                    weight = mask[:, tiles].unsqueeze(2).to_broadcast([P, U0, P]).rearrange("p n (h d) -> p n h d", h=H0)
                    nc.vector.tensor_tensor(values[:, tiles, :, 0:D0], kv[:, :, P:2 * P].rearrange("p n (h d) -> p n h d", h=H0),
                                            weight, ALU.mult).then_inc(s_vec, 1)
                    nc.vector.tensor_copy(values[:, tiles, :, D0], mask[:, tiles].unsqueeze(2).to_broadcast([P, U0, H0])).then_inc(s_vec, 1)
                    dve.wait_ge(s_vec, i * 9 + 3)
                    dve.wait_ge(s_rot, i + 1)
                    heads = rotated[:, :, :].rearrange("p n (h d) -> p (n h) d", h=H0)
                    rows_of = packed[:, :, :, :].rearrange("p n h r -> p (n h) r")

                    dve.wait_ge(s_keys, i * U0 + 1)
                    nc.vector.tensor_copy(rows_of[:, :, 0:D0], heads).then_inc(s_vec, 1)
                    dve.wait_ge(s_vec, i * 9 + 4)
                    nc.vector.tensor_copy(rows_of[:, :, D0:2 * D0], heads).then_inc(s_vec, 1)
                    nc.vector.tensor_tensor(rows_of[:, :, 2 * D0:3 * D0], heads, rows_of[:, :, 0:D0].bitcast(F32), ALU.subtract).then_inc(s_vec, 1)
                    nc.vector.tensor_copy(packed[:, :, :, 3 * D0 + 2], mask_bias[:, tiles].bitcast(F32).unsqueeze(2).to_broadcast([P, U0, H0])).then_inc(s_packed, 1)
                    nc.vector.tensor_tensor(squares[:, :, :], rotated[:, :, :], rotated[:, :, :], ALU.mult).then_inc(s_vec, 1)
                    dve.wait_ge(s_vec, i * 9 + 7)
                    nc.vector.tensor_reduce(norms[:, :, :], squares[:, :, :].rearrange("p n (h d) -> p n h d", h=H0), AX.X, ALU.add).then_inc(s_vec, 1)
                    dve.wait_ge(s_vec, i * 9 + 8)
                    nc.vector.tensor_tensor(best[:, :, :], best[:, :, :], norms[:, :, :], ALU.max).then_inc(s_vec, 1)
                    dve.wait_ge(s_vec, i * 9 + 9)
                nc.vector.tensor_tensor(best[:, 0, :], best[:, 0, :], best[:, 1, :], ALU.max).then_inc(s_vec, 1)
                dve.wait_ge(s_vec, NI * 9 + 1)
                nc.vector.tensor_tensor(best[:, 0, :], best[:, 0, :], best[:, 2, :], ALU.max).then_inc(s_norm, 1)


def cross_attention(nc, kept, ps, a):
    with ExitStack() as stack:
        context_keys(nc, kept, ps, a, stack)
        key_rows, values, key_bound, x, ident = (kept[n] for n in ("key_rows", "values", "key_bound", "x", "ident"))
        m = Memory(nc, stack, "att")
        scaled = m.sb("scaled", [P, NT, P])
        guard = m.sb("guard", [P, NT, H0])
        attended = scaled
        flag = m.sb("flag", [P, 2])
        with ExitStack() as own:
            m = Memory(nc, own, "qry")
            w_q, b_q, rope = m.sb("w_q", [P, P]), m.sb("b_q", [P, P]), m.sb("rope", [P, NT, 2, D0 // 2])
            stats, moments, normed, xn = m.sb("stats", [P, NT, 6]), m.sb("moments", [P, NT, 2]), m.sb("normed", [P, NT, P]), m.sb("xn", [P, T])
            q, squares = m.sb("q", [P, NT, P]), m.sb("squares", [P, NT, P])
            part = [m.sb(f"part{n}", [P, NT, H0, D0 // 2]) for n in range(4)]
            s_load, s_vec, s_eps, s_root, s_norm, s_turned, s_xn_a, s_xn_v, s_proj, s_sq, s_len, s_top, s_all = (m.sem(n) for n in (
                "loaded", "vector_step", "variance", "root", "normed", "turned", "xn_scalar", "xn_vector", "projected", "squares", "lengths", "top", "top_of_all"))
            bank = ps[:, :, :].rearrange("p b c -> p (b c)")
            with nc.Block() as block:
                @block.sync
                def _(sp):
                    sp.dma_start(w_q[:, :], a["L0_xattn_Wq"]).then_inc(s_load, 16)
                    sp.dma_start(b_q[:, :], spread(a["L0_xattn_bq"])).then_inc(s_load, 16)
                    sp.dma_start(rope[:, :, :, :], a["rope_q"]).then_inc(s_load, 16)
                    sp.wait_ge(s_load, 3 * 16)

                @block.scalar
                def _(act):
                    root(nc, act, moments, s_eps, s_root)
                    act.wait_ge(s_turned, 1)
                    nc.scalar.activation(xn[:, 0:HALF], bank[:, 0:HALF], ACT.Copy).then_inc(s_xn_a, 1)
                    act.wait_ge(s_sq, 1)
                    nc.scalar.activation(guard[:, :, :], guard[:, :, :], ACT.Sqrt).then_inc(s_len, 1)

                @block.tensor
                def _(pe):
                    pe.wait_ge(s_norm, NT)
                    transpose_tiles(nc, pe, bank, normed, ident, s_turned)
                    pe.wait_ge(s_load, 3 * 16)
                    pe.wait_ge(s_xn_a, 1)
                    pe.wait_ge(s_xn_v, 1)
                    for t in range(NT):
                        last = nc.tensor.matmul(bank[:, T + t * P:T + (t + 1) * P], xn[:, t * P:(t + 1) * P], w_q[:, :], start=True, stop=True)
                    last.then_inc(s_proj, 1)

                @block.vector
                def _(dve):
                    step = stepper(dve)
                    layer_norm(nc, dve, step, s_vec, stats, moments, x, normed, s_eps, s_root, s_norm)
                    dve.wait_ge(s_turned, 2)
                    step(nc.vector.tensor_copy(xn[:, HALF:T], bank[:, HALF:T]), s_xn_v)
                    dve.wait_ge(s_load, 3 * 16)
                    dve.wait_ge(s_proj, 1)
                    step(nc.vector.tensor_tensor(q[:, :, :], bank[:, T:2 * T].rearrange("p (t c) -> p t c", c=P),
                                                 b_q[:, :].unsqueeze(1).to_broadcast([P, NT, P]), ALU.add), s_vec)
                    even, odd = (q[:, :, j:P:2].rearrange("p n (h d) -> p n h d", h=H0) for j in (0, 1))
                    cos, sin = (rope[:, :, j, :].unsqueeze(2).to_broadcast([P, NT, H0, D0 // 2]) for j in (0, 1))
                    for n, (u, w) in enumerate(((even, cos), (odd, sin), (even, sin), (odd, cos))):
                        step(nc.vector.tensor_tensor(part[n][:, :, :, :], u, w, ALU.mult), s_vec, wait=n == 3)
                    for n, op in ((0, ALU.subtract), (1, ALU.add)):
                        step(nc.vector.tensor_tensor(q[:, :, n:P:2].rearrange("p n (h d) -> p n h d", h=H0),
                                                     part[2 * n][:, :, :, :], part[2 * n + 1][:, :, :, :], op), s_vec)
                    step(nc.vector.tensor_scalar(scaled[:, :, :], q[:, :, :], D0 ** -1.0, None, ALU.mult), s_vec)
                    step(nc.vector.tensor_tensor(squares[:, :, :], scaled[:, :, :], scaled[:, :, :], ALU.mult), s_vec)
                    step(nc.vector.tensor_reduce(guard[:, :, :], squares[:, :, :].rearrange("p n (h d) -> p n h d", h=H0), AX.X, ALU.add), s_sq)
                    dve.wait_ge(s_len, 1)
                    step(nc.vector.tensor_tensor(guard[:, :, :], guard[:, :, :], key_bound[:, :].unsqueeze(1).to_broadcast([P, NT, H0]), ALU.mult), s_vec)
                    step(nc.vector.tensor_reduce(flag[:, 0:1], guard[:, :, :], AX.XY, ALU.max), s_top)

                @block.gpsimd
                def _(pool):
                    pool.wait_ge(s_top, 1)
                    nc.gpsimd.partition_all_reduce(flag[:, 1:2], flag[:, 0:1], P, bass.bass_isa.ReduceOp.max).then_inc(s_all, 1)

        attend(nc, kept, ps, a, scaled, guard, attended, flag)

        with ExitStack() as own:
            m = Memory(nc, own, "prj")
            turned, w_out, b_out = m.sb("turned", [P, T]), m.sb("w_out", [P, P]), m.sb("b_out", [P, P])
            s_load = m.sem("loaded")
            s_turned, s_a, s_v, s_proj, s_vec = (m.sem(n) for n in ("turned", "kept_scalar", "kept_vector", "projected", "vector_step"))
            bank = ps[:, :, :].rearrange("p b c -> p (b c)")
            with nc.Block() as block:
                @block.sync
                def _(sp):
                    sp.dma_start(w_out[:, :], a["L0_xattn_Wo"]).then_inc(s_load, 16)
                    sp.dma_start(b_out[:, :], spread(a["L0_xattn_bo"])).then_inc(s_load, 16)
                    sp.wait_ge(s_load, 2 * 16)

                @block.tensor
                def _(pe):
                    transpose_tiles(nc, pe, bank, attended, ident, s_turned)
                    pe.wait_ge(s_load, 2 * 16)
                    pe.wait_ge(s_a, 1)
                    pe.wait_ge(s_v, 1)
                    for t in range(NT):
                        last = nc.tensor.matmul(bank[:, T + t * P:T + (t + 1) * P], turned[:, t * P:(t + 1) * P], w_out[:, :], start=True, stop=True)
                    last.then_inc(s_proj, 1)

                @block.scalar
                def _(act):
                    act.wait_ge(s_turned, 1)
                    nc.scalar.activation(turned[:, 0:HALF], bank[:, 0:HALF], ACT.Copy).then_inc(s_a, 1)

                @block.vector
                def _(dve):
                    step = stepper(dve)
                    dve.wait_ge(s_load, 2 * 16)
                    step(nc.vector.tensor_tensor(x[:, :, :], x[:, :, :], b_out[:, :].unsqueeze(1).to_broadcast([P, NT, P]), ALU.add), s_vec)
                    dve.wait_ge(s_turned, 2)
                    step(nc.vector.tensor_copy(turned[:, HALF:T], bank[:, HALF:T]), s_v)
                    dve.wait_ge(s_proj, 1)
                    step(nc.vector.tensor_tensor(x[:, :, :], bank[:, T:2 * T].rearrange("p (t c) -> p t c", c=P), x[:, :, :], ALU.add), s_vec)


def attend(nc, kept, ps, a, scaled, guard, attended, flag):
    key_rows, values, ident = kept["key_rows"], kept["values"], kept["ident"]
    NP = 12
    BODY = U0 * G0
    SG = NK * G0
    VG = NK + 2
    with ExitStack() as own:
        m = Memory(nc, own, "loop")
        head_rows = m.sb("head_rows", [P, G0])
        query_rows = m.sb("query_rows", [P, G0, T], F32R)
        key_tile = [m.sb(f"key_tile{n}", [P, P], F32R) for n in range(U0)]
        value_tile = [m.sb(f"value_tile{n}", [P, G0, ROW]) for n in range(U0)]
        exps = [m.sb(f"exps{n}", [P, T]) for n in range(NP)]
        packed = exps[NP - 1][:, :].rearrange("p (t h r) -> p t h r", h=G0, r=ROW).bitcast(F32R)
        sums = exps[0]
        inverse = m.sb("inverse", [P, NT, G0])
        zero = m.sb("zero", [P, P])
        row_max, chunk_max, new_guard = m.sb("row_max", [P, NT, G0]), m.sb("chunk_max", [P, NT, G0]), m.sb("new_guard", [P, NT, G0])
        s_load, s_set, s_packed, s_turned, s_queries_a, s_queries_v = (m.sem(n) for n in (
            "loaded", "set", "packed", "queries_turned", "queries_scalar", "queries_vector"))
        s_vec, s_key, s_value, s_score, s_exp, s_weighted = (m.sem(n) for n in (
            "vector_step", "key_tile", "value_tile", "scores", "exps", "weighted"))
        s_closed, s_sums_a, s_sums_v, s_back, s_norm = (m.sem(n) for n in ("closed", "sums_scalar", "sums_vector", "sums_turned", "normalised"))
        x_scores, x_max, x_pack, x_packed, x_turned, x_queries, x_step = (m.sem(n) for n in (
            "exact_scores", "exact_max", "exact_high", "exact_packed", "exact_turned", "exact_queries", "exact_step"))
        CHUNK = U0 * P

        def turn_queries(semaphore):
            for t in range(NT):
                last = nc.tensor.transpose(ps[:, t // 4, (t % 4) * P:(t % 4 + 1) * P],
                                           packed[:, t, :, :].bitcast(F32).rearrange("p h r -> p (h r)"), ident[:, :])
            last.then_inc(semaphore, 1)

        with nc.Block() as block:
            @block.sync
            def _(sp):
                sp.dma_start(head_rows[:, :], a["head_rows"]).then_inc(s_load, 16)
                sp.wait_ge(s_load, 16)

            @block.tensor
            def _(pe):
                def scores(g, i, c):
                    if c >= U0 or not isinstance(i, int):
                        pe.wait_ge(s_exp, g * SG + i * BODY + (c - U0 + 1))
                    if c % G0 == 0:
                        pe.wait_ge(s_key, g * NK + i * U0 + (c // G0 + 1))
                    for b in range(2):
                        last = nc.tensor.matmul(ps[:, 2 * (c % 3) + b, :], key_tile[c // G0 % U0][:, :],
                                                query_rows[:, c % G0, b * HALF:(b + 1) * HALF], start=True, stop=True)
                    last.then_inc(s_score, 1)

                def weigh(g, i, n):
                    pe.wait_ge(s_value, g * NK + i * U0 + (n + 1))
                    pe.wait_ge(s_exp, g * SG + i * BODY + G0 * (n + 1))
                    for b in range(2):
                        for h in range(G0):
                            last = nc.tensor.matmul(ps[h * ROW:(h + 1) * ROW, 6 + b, :], value_tile[n][:, h, :],
                                                    exps[(n * G0 + h) % NP][:, b * HALF:(b + 1) * HALF], start=False, stop=False,
                                                    skip_group_check=True)
                    last.then_inc(s_weighted, 1)

                def zeros(b, opening):
                    return nc.tensor.matmul(ps[:, 6 + b, :], zero[:, :], zero[:, 0:1].to_broadcast([P, HALF]), start=opening, stop=not opening,
                                            skip_group_check=True)

                pe.wait_ge(s_load, 16)
                bits = nc.tensor.value_load(flag[0:1, 1:2].bitcast(I32))
                pe.wait_ge(s_set, 4)
                with pe.Fori(0, NG) as g:
                    pe.wait_ge(s_packed, g * 4 + 4)
                    turn_queries(s_turned)
                    pe.wait_ge(s_queries_a, g * 2 + 2)
                    pe.wait_ge(s_queries_v, g * 2 + 2)
                    with pe.If(bits > SAFE_BITS):
                        with pe.Fori(0, NI) as i:
                            for n in range(NT * G0):
                                if n >= 6:
                                    pe.wait_ge(x_max, (g * NI + i) * (NT * G0) + (n - 5))
                                nc.tensor.matmul(ps[:, n % 6, 0:CHUNK], query_rows[:, n % G0, (n // G0) * P:(n // G0 + 1) * P],
                                                 key_rows[:, g, bass.ds(i * CHUNK, CHUNK)], start=True, stop=True).then_inc(x_scores, 1)
                            pe.wait_ge(x_max, (g * NI + i + 1) * (NT * G0))
                        pe.wait_ge(x_packed, g + 1)
                        turn_queries(x_turned)
                        pe.wait_ge(x_queries, (g + 1) * G0)
                    for b in range(2):
                        zeros(b, True).then_inc(s_weighted, 1)
                    for c in range(3):
                        scores(g, 0, c)
                    with pe.Fori(0, NI - 1) as i:
                        for n in range(U0):
                            for c in range(G0):
                                step = n * G0 + c + 3
                                scores(g, i, step) if step < BODY else scores(g, i + 1, step - BODY)
                            weigh(g, i, n)
                    for n in range(U0):
                        for c in range(G0):
                            if n * G0 + c + 3 < BODY:
                                scores(g, NI - 1, n * G0 + c + 3)
                        weigh(g, NI - 1, n)
                    for b in range(2):
                        zeros(b, False).then_inc(s_closed, 1)
                    pe.wait_ge(s_sums_a, g + 1)
                    pe.wait_ge(s_sums_v, g + 1)
                    for t in range(NT):
                        last = nc.tensor.transpose(ps[:, t // 4, (t % 4) * P:(t % 4 + 1) * P], sums[:, t * P:(t + 1) * P], ident[:, :])
                    last.then_inc(s_back, 1)
                    pe.wait_ge(s_norm, g + 1)

            @block.scalar
            def _(act):
                act.wait_ge(s_load, 16)
                with act.Fori(0, NG) as g:
                    act.wait_ge(s_turned, g + 1)
                    for h in range(2):
                        nc.scalar.activation(query_rows[:, h, :], ps[:, 0:2, :].rearrange("p b c -> p (b c)"), ACT.Copy,
                                             scale=head_rows[:, h:h + 1]).then_inc(s_queries_a, 1)
                    with act.Fori(0, NI) as i:
                        for c in range(BODY):
                            act.wait_ge(s_score, g * SG + i * BODY + (c + 1))
                            if c % G0 == NP % G0:
                                act.wait_ge(s_weighted, g * VG + i * U0 + (3 + (c - NP) // G0))
                            nc.scalar.activation(exps[c % NP][:, :], ps[:, 2 * (c % 3):2 * (c % 3) + 2, :].rearrange("p b c -> p (b c)"),
                                                 ACT.Exp).then_inc(s_exp, 1)
                    act.wait_ge(s_closed, g * 2 + 2)
                    nc.scalar.activation(sums[:, 0:HALF], ps[:, 6, :], ACT.Copy).then_inc(s_sums_a, 1)

            @block.vector
            def _(dve):
                step = stepper(dve)
                for tile in value_tile:
                    step(nc.vector.memset(tile[:, :, :], 0.0), s_set, wait=False)
                step(nc.vector.memset(zero[:, :], 0.0), s_set)
                dve.wait_ge(s_load, 16)
                bits = nc.vector.value_load(flag[0:1, 1:2].bitcast(I32))

                def stage_keys(g, i, n):
                    nc.vector.tensor_copy(key_tile[n][:, :], key_rows[:, g, bass.ds(i * CHUNK + n * P, P)].bitcast(F32)).then_inc(s_key, 1)

                def stage_values(g, i, n):
                    nc.vector.tensor_copy(value_tile[n][:, :, 0:D0 + 1], values[:, i * U0 + n, bass.ds(g * G0, G0), :]).then_inc(s_value, 1)

                with dve.Fori(0, NG) as g:
                    heads = scaled[:, :, bass.ds(g * ROW, ROW)].rearrange("p t (h d) -> p t h d", h=G0)
                    guards = guard[:, :, bass.ds(g * G0, G0)]
                    high = packed[:, :, :, 0:D0]
                    nc.vector.memset(packed[:, :, :, 3 * D0 + 3:ROW].bitcast(F32), 0.0).then_inc(s_vec, 1)
                    nc.vector.memset(packed[:, :, :, 3 * D0 + 2:3 * D0 + 3].bitcast(F32), 1.0).then_inc(s_vec, 1)
                    nc.vector.tensor_copy(high, heads).then_inc(s_vec, 1)
                    dve.wait_ge(s_vec, g * 4 + 3)
                    nc.vector.tensor_tensor(packed[:, :, :, D0:2 * D0], heads, high.bitcast(F32), ALU.subtract).then_inc(s_packed, 1)
                    nc.vector.tensor_copy(packed[:, :, :, 2 * D0:3 * D0], heads).then_inc(s_packed, 1)
                    nc.vector.tensor_scalar(packed[:, :, :, 3 * D0], guards, -1.0, None, ALU.mult).then_inc(s_packed, 1)
                    dve.wait_ge(s_packed, g * 4 + 3)
                    nc.vector.scalar_tensor_tensor(packed[:, :, :, 3 * D0 + 1], guards, -1.0, packed[:, :, :, 3 * D0].bitcast(F32),
                                                   ALU.mult, ALU.subtract).then_inc(s_packed, 1)
                    dve.wait_ge(s_turned, g + 1)
                    dve.wait_ge(s_queries_a, g * 2 + 2)
                    for h in range(2, G0):
                        nc.vector.tensor_scalar(query_rows[:, h, :], ps[:, 0:2, :].rearrange("p b c -> p (b c)"), head_rows[:, h:h + 1], None,
                                                ALU.mult).then_inc(s_queries_v, 1)
                    with dve.If(bits > SAFE_BITS):
                        nc.vector.memset(row_max[:, :, :], MASKED).then_inc(x_step, 1)
                        with dve.Fori(0, NI) as i:
                            for n in range(NT * G0):
                                dve.wait_ge(x_scores, (g * NI + i) * (NT * G0) + (n + 1))
                                nc.vector.tensor_reduce(chunk_max[:, n // G0, n % G0:n % G0 + 1], ps[:, n % 6, 0:CHUNK], AX.X, ALU.max).then_inc(x_max, 1)
                            dve.wait_ge(x_max, (g * NI + i + 1) * (NT * G0))
                            dve.wait_ge(x_step, g * (NI + 2) + i + 1)
                            nc.vector.tensor_tensor(row_max[:, :, :], row_max[:, :, :], chunk_max[:, :, :], ALU.max).then_inc(x_step, 1)
                            dve.wait_ge(x_step, g * (NI + 2) + i + 2)
                        nc.vector.tensor_tensor(new_guard[:, :, :], row_max[:, :, :], guards, ALU.add).then_inc(x_step, 1)
                        dve.wait_ge(x_step, g * (NI + 2) + NI + 2)
                        nc.vector.tensor_scalar(packed[:, :, :, 3 * D0], new_guard[:, :, :], -1.0, None, ALU.mult).then_inc(x_pack, 1)
                        dve.wait_ge(x_pack, g + 1)
                        nc.vector.scalar_tensor_tensor(packed[:, :, :, 3 * D0 + 1], new_guard[:, :, :], -1.0, packed[:, :, :, 3 * D0].bitcast(F32),
                                                       ALU.mult, ALU.subtract).then_inc(x_packed, 1)
                        dve.wait_ge(x_turned, g + 1)
                        for h in range(G0):
                            nc.vector.tensor_scalar(query_rows[:, h, :], ps[:, 0:2, :].rearrange("p b c -> p (b c)"), head_rows[:, h:h + 1], None,
                                                    ALU.mult).then_inc(x_queries, 1)
                    for n in range(U0):
                        stage_keys(g, 0, n)
                        stage_values(g, 0, n)
                    with dve.Fori(0, NI - 1) as i:
                        for n in range(U0):
                            dve.wait_ge(s_score, g * SG + i * BODY + G0 * (n + 1))
                            stage_keys(g, i + 1, n)
                            dve.wait_ge(s_weighted, g * VG + i * U0 + (n + 3))
                            stage_values(g, i + 1, n)
                    dve.wait_ge(s_closed, g * 2 + 2)
                    nc.vector.tensor_copy(sums[:, HALF:T], ps[:, 7, :]).then_inc(s_sums_v, 1)
                    dve.wait_ge(s_back, g + 1)
                    back = ps[:, 0:2, :].rearrange("p b (t h r) -> p (b t) h r", h=G0, r=ROW)
                    nc.vector.reciprocal(inverse[:, :, :], back[:, :, :, D0]).then_inc(s_vec, 1)
                    dve.wait_ge(s_vec, g * 4 + 4)
                    nc.vector.tensor_tensor(attended[:, :, bass.ds(g * ROW, ROW)].rearrange("p t (h d) -> p t h d", h=G0), back[:, :, :, 0:D0],
                                            inverse[:, :, :].unsqueeze(3).to_broadcast([P, NT, G0, D0]), ALU.mult).then_inc(s_norm, 1)


def route_top2(nc, dve, step, s_vec, s_exp_in, s_exp_out, m, logits, order, weights):
    E = order.shape[1]
    peak, prob, total = m["peak"], m["prob"], m["total"]
    larger, equal, rank = m["larger"], m["equal"], m["rank"]
    step(nc.vector.tensor_reduce(peak[:, :], logits, AX.X, ALU.max), s_vec)
    step(nc.vector.tensor_tensor(prob[:, :, :], logits, peak[:, :].unsqueeze(2).to_broadcast([P, NT, E]), ALU.subtract), s_exp_in)
    dve.wait_ge(s_exp_out, 1)
    step(nc.vector.tensor_reduce(total[:, :], prob[:, :, :], AX.X, ALU.add), s_vec)
    step(nc.vector.reciprocal(total[:, :], total[:, :]), s_vec)
    step(nc.vector.tensor_tensor(prob[:, :, :], prob[:, :, :], total[:, :].unsqueeze(2).to_broadcast([P, NT, E]), ALU.mult), s_vec)
    select(nc, step, s_vec, prob, order, larger, equal, rank, 2)
    step(nc.vector.tensor_tensor(weights[:, :, :], prob[:, :, :], rank[:, :, :], ALU.mult), s_vec)
    step(nc.vector.tensor_reduce(total[:, :], weights[:, :, :], AX.X, ALU.add), s_vec)
    step(nc.vector.reciprocal(total[:, :], total[:, :]), s_vec)
    step(nc.vector.tensor_tensor(weights[:, :, :], weights[:, :, :], total[:, :].unsqueeze(2).to_broadcast([P, NT, E]), ALU.mult), s_vec)


def select(nc, step, s_vec, values, order, larger, equal, rank, top):
    E = order.shape[1]
    for t in range(NT):
        other = values[:, t, :].unsqueeze(1).to_broadcast([P, E, E])
        mine = values[:, t, :].unsqueeze(2).to_broadcast([P, E, E])
        step(nc.vector.tensor_tensor(larger[:, t, :, :], other, mine, ALU.is_gt), s_vec, wait=False)
        step(nc.vector.tensor_tensor(equal[:, t, :, :], other, mine, ALU.is_equal), s_vec, wait=t == NT - 1)
    step(nc.vector.tensor_tensor(equal[:, :, :, :].rearrange("p t e f -> p t (e f)"), equal[:, :, :, :].rearrange("p t e f -> p t (e f)"),
                                 order[:, :, :].rearrange("p e f -> p (e f)").unsqueeze(1).to_broadcast([P, NT, E * E]), ALU.mult), s_vec)
    step(nc.vector.tensor_tensor(larger[:, :, :, :], larger[:, :, :, :], equal[:, :, :, :], ALU.add), s_vec)
    step(nc.vector.tensor_reduce(rank[:, :, :], larger[:, :, :, :], AX.X, ALU.add), s_vec)
    step(nc.vector.tensor_scalar(rank[:, :, :], rank[:, :, :], float(top), None, ALU.is_lt), s_vec)


def mixture(nc, kept, ps, a, layer):
    E = 32 if layer else 8
    HID = 64 if layer else 176
    ROUTED = E * HID // P
    SHARED = 1 if layer else 3
    NH = ROUTED + SHARED
    rows_of = [P] * NH
    if not layer:
        rows_of[-1] = 2 * HID - 2 * P
    x, ident = kept["x"], kept["ident"]
    bank = ps[:, :, :].rearrange("p b c -> p (b c)")
    with ExitStack() as stack:
        m = Memory(nc, stack, f"mix{layer}")
        w_gate, w_up, w_down = (m.sb(n, [P, NH, P]) for n in ("w_gate", "w_up", "w_down"))
        xn = m.sb("xn", [P, T])
        picks = m.sb("picks", [P, ROUTED, P], F32R)
        route_rows = m.sb("route_rows", [P, T], F32R)
        with ExitStack() as own:
            b = Memory(nc, own, f"mixb{layer}")
            picks_in = b.sb("picks_in", [P, ROUTED, P])
            router, order = b.sb("router", [P, E]), b.sb("order", [P, 8 if not layer else 4, 8 if not layer else 4])
            raw = b.sb("raw", [P, 3, ROUTED + SHARED, P]) if layer else None
            router_raw, router_bias = (b.sb("router_raw", [E, P]), b.sb("router_bias", [P, E])) if layer else (None, None)
            stats, moments, normed = b.sb("stats", [P, NT, 6]), b.sb("moments", [P, NT, 2]), b.sb("normed", [P, NT, P])
            packed = b.sb("packed", [P, NT, P], F32R)
            weights = b.sb("weights", [P, NT, E])
            R = order.shape[1]
            scratch = {n: b.sb(n, s) for n, s in {"peak": [P, NT], "total": [P, NT], "prob": [P, NT, E], "larger": [P, NT, R, R],
                                                  "equal": [P, NT, R, R], "rank": [P, NT, R], "choice": [P, NT, E], "best": [P, NT, 4, 8],
                                                  "top": [P, NT, 8], "left": [P, NT, E], "groups": [P, NT, 4]}.items()}
            s_load, s_late, s_vec, s_eps, s_root, s_norm, s_turned, s_xn_a, s_xn_v, s_logit, s_exp_in, s_exp_out = (b.sem(n) for n in (
                "loaded", "weights_loaded", "vector_step", "variance", "root", "normed", "turned", "xn_scalar", "xn_vector", "logits", "exp_input", "exps"))
            s_packed, s_routes, s_kept, s_w_turned, s_w_kept, s_router = (b.sem(n) for n in (
                "packed", "routes_turned", "routes_kept", "weights_turned", "weights_kept", "router_kept"))

            with nc.Block() as block:
                @block.sync
                def _(sp):
                    if layer:
                        loads = [(router_raw[:, :], a["L1_ffn_gate_w"]), (router_bias[:, :], spread(a["L1_ffn_gate_bias"])),
                                 (order[:, :, :], a["order4"])]
                        late = [(raw[:, 0, 0:ROUTED, :], a["L1_ffn_expert_gate"].rearrange("e i h -> (e i) h").rearrange("(n p) h -> p n h", p=P)),
                                (raw[:, 1, 0:ROUTED, :], a["L1_ffn_expert_up"].rearrange("e i h -> (e i) h").rearrange("(n p) h -> p n h", p=P)),
                                (raw[:, 2, 0:ROUTED, :].rearrange("p n (e i) -> p (n e) i", e=2), a["L1_ffn_expert_down"].rearrange("e h i -> h e i")),
                                (raw[:, 0, ROUTED, :], a["L1_ffn_shared_gate"]), (raw[:, 1, ROUTED, :], a["L1_ffn_shared_up"]),
                                (raw[:, 2, ROUTED, :], a["L1_ffn_shared_down"])]
                    else:
                        loads = [(router[:, :], a["L0_ffn_gate_w"]), (order[:, :, :], a["order8"])]
                        late = []
                        for w, name in ((w_gate, "gate"), (w_up, "up")):
                            flat = w[:, :, :].rearrange("p n c -> p (n c)")
                            late.append((flat[:, 0:E * HID].rearrange("p (e f) -> p e f", e=E), a[f"L0_ffn_exp_{name}"].rearrange("e d f -> d e f")))
                            late.append((flat[:, E * HID:(E + 2) * HID].rearrange("p (e f) -> p e f", e=2), a[f"L0_ffn_sh_{name}"].rearrange("e d f -> d e f")))
                        late.append((w_down[:, 0:ROUTED, :], a["L0_ffn_exp_down"].rearrange("e f d -> (e f) d").rearrange("(n p) d -> p n d", p=P)))
                        shared = a["L0_ffn_sh_down"].rearrange("e f d -> (e f) d")
                        late.append((w_down[:, ROUTED:ROUTED + 2, :], shared[0:2 * P, :].rearrange("(n p) d -> p n d", p=P)))
                        late.append((w_down[0:rows_of[-1], NH - 1, :], shared[2 * P:2 * HID, :]))
                    late.append((picks_in[:, :, :], a[f"picks{layer}"]))
                    for dst, src in loads:
                        sp.dma_start(dst, src).then_inc(s_load, 16)
                    for dst, src in late:
                        sp.dma_start(dst, src).then_inc(s_late, 16)
                    sp.wait_ge(s_load, len(loads) * 16)
                    sp.wait_ge(s_late, len(late) * 16)

                n_loads, n_late = (3, 7) if layer else (2, 8)

                @block.tensor
                def _(pe):
                    pe.wait_ge(s_load, n_loads * 16)
                    if layer:
                        nc.tensor.transpose(ps[:, 3, 0:E], router_raw[:, :], ident[0:E, 0:E]).then_inc(s_w_turned, 1)
                    pe.wait_ge(s_norm, NT)
                    transpose_tiles(nc, pe, bank, normed, ident, s_turned)
                    pe.wait_ge(s_xn_a, 1)
                    pe.wait_ge(s_xn_v, 1)
                    if layer:
                        pe.wait_ge(s_router, 1)
                    for t in range(NT):
                        last = nc.tensor.matmul(ps[:, 2, t * E:(t + 1) * E], xn[:, t * P:(t + 1) * P], router[:, :], start=True, stop=True)
                    last.then_inc(s_logit, 1)
                    if layer:
                        pe.wait_ge(s_late, n_late * 16)
                        for n in range(3 * NH):
                            if n >= 4:
                                pe.wait_ge(s_w_kept, n - 3)
                            nc.tensor.transpose(ps[:, 4 + n % 4, 0:P], raw[:, n // NH, n % NH, :], ident[:, :]).then_inc(s_w_turned, 1)
                    pe.wait_ge(s_packed, 1)
                    for t in range(NT):
                        last = nc.tensor.transpose(ps[:, t // 4, (t % 4) * P:(t % 4 + 1) * P], packed[:, t, :].bitcast(F32), ident[:, :])
                    last.then_inc(s_routes, 1)

                @block.scalar
                def _(act):
                    root(nc, act, moments, s_eps, s_root)
                    act.wait_ge(s_turned, 1)
                    nc.scalar.activation(xn[:, 0:HALF], bank[:, 0:HALF], ACT.Copy).then_inc(s_xn_a, 1)
                    if layer:
                        act.wait_ge(s_w_turned, 1)
                        nc.scalar.activation(router[:, :], ps[:, 3, 0:E], ACT.Copy).then_inc(s_router, 1)
                    act.wait_ge(s_exp_in, 1)
                    prob = scratch["prob"]
                    if layer:
                        nc.scalar.activation(prob[:, :, :], ps[:, 2, 0:NT * E].rearrange("p (t e) -> p t e", e=E), ACT.Sigmoid).then_inc(s_exp_out, 1)
                        for n in range(3 * NH):
                            act.wait_ge(s_w_turned, n + 2)
                            nc.scalar.activation((w_gate, w_up, w_down)[n // NH][:, n % NH, :], ps[:, 4 + n % 4, 0:P], ACT.Copy).then_inc(s_w_kept, 1)
                    else:
                        nc.scalar.activation(prob[:, :, :], prob[:, :, :], ACT.Exp).then_inc(s_exp_out, 1)

                @block.vector
                def _(dve):
                    step = stepper(dve)
                    step(nc.vector.memset(packed[:, :, :].bitcast(F32), 0.0), s_vec)
                    layer_norm(nc, dve, step, s_vec, stats, moments, x, normed, s_eps, s_root, s_norm)
                    dve.wait_ge(s_turned, 2)
                    step(nc.vector.tensor_copy(xn[:, HALF:T], bank[:, HALF:T]), s_xn_v)
                    dve.wait_ge(s_load, n_loads * 16)
                    dve.wait_ge(s_logit, 1)
                    if layer:
                        step(nc.vector.memset(scratch["peak"][:, :], 0.0), s_exp_in)
                        dve.wait_ge(s_exp_out, 1)
                        route_groups(nc, dve, step, s_vec, scratch, router_bias, order, weights)
                    else:
                        logits = ps[:, 2, 0:NT * E].rearrange("p (t e) -> p t e", e=E)
                        route_top2(nc, dve, step, s_vec, s_exp_in, s_exp_out, scratch, logits, order, weights)
                    step(nc.vector.tensor_copy(packed[:, :, 0:E], weights[:, :, :]), s_vec)
                    step(nc.vector.tensor_tensor(packed[:, :, 32:32 + E], weights[:, :, :], packed[:, :, 0:E].bitcast(F32), ALU.subtract), s_packed)
                    dve.wait_ge(s_late, n_late * 16)
                    step(nc.vector.tensor_copy(picks[:, :, :], picks_in[:, :, :]), s_vec)
                    dve.wait_ge(s_routes, 1)
                    step(nc.vector.tensor_copy(route_rows[:, :], bank[:, 0:T]), s_kept)

        with ExitStack() as own:
            b = Memory(nc, own, f"mixc{layer}")
            silu = [b.sb(f"silu{n}", [P, T]) for n in range(2)]
            hidden = [b.sb(f"hidden{n}", [P, T]) for n in range(2)]
            zero = b.sb("zero", [P, P])
            s_zero, s_gate, s_up, s_route, s_silu, s_prod, s_hidden, s_down, s_end = (b.sem(n) for n in (
                "zero", "gate", "up", "route", "silu", "product", "hidden", "down", "end"))
            with nc.Block() as block:
                @block.tensor
                def _(pe):
                    def down(n):
                        k = rows_of[n]
                        pe.wait_ge(s_hidden, n + 1)
                        for t in range(NT):
                            last = nc.tensor.matmul(bank[:, 6 * HALF + t * P:6 * HALF + (t + 1) * P], hidden[n % 2][0:k, t * P:(t + 1) * P],
                                                    w_down[0:k, n, :], start=False, stop=n == NH - 1 and t % 4 == 3, skip_group_check=True)
                        last.then_inc(s_down, 1)

                    pe.wait_ge(s_zero, 1)
                    for c in range(2):
                        nc.tensor.matmul(ps[:, 6 + c, :], zero[:, :], zero[:, 0:1].to_broadcast([P, HALF]), start=True, stop=False, skip_group_check=True)
                    for n in range(NH):
                        k = rows_of[n]
                        if n:
                            pe.wait_ge(s_silu, n)
                        for c in range(2):
                            last = nc.tensor.matmul(ps[0:k, c, :], w_gate[:, n, 0:k], xn[:, c * HALF:(c + 1) * HALF], start=True, stop=True)
                        last.then_inc(s_gate, 1)
                        if n:
                            pe.wait_ge(s_prod, n)
                        for c in range(2):
                            last = nc.tensor.matmul(ps[0:k, 2 + c, :], w_up[:, n, 0:k], xn[:, c * HALF:(c + 1) * HALF], start=True, stop=True)
                        last.then_inc(s_up, 1)
                        if n < ROUTED:
                            if n:
                                pe.wait_ge(s_hidden, n)
                            for c in range(2):
                                last = nc.tensor.matmul(ps[:, 4 + c, :], picks[:, n, :], route_rows[:, c * HALF:(c + 1) * HALF], start=True, stop=True)
                            last.then_inc(s_route, 1)
                        if n:
                            down(n - 1)
                    down(NH - 1)

                @block.scalar
                def _(act):
                    for n in range(NH):
                        k = rows_of[n]
                        act.wait_ge(s_gate, n + 1)
                        if n >= 2:
                            act.wait_ge(s_prod, n - 1)
                        nc.scalar.activation(silu[n % 2][0:k, :], bank[0:k, 0:T], ACT.Silu).then_inc(s_silu, 1)

                @block.vector
                def _(dve):
                    nc.vector.memset(zero[:, :], 0.0).then_inc(s_zero, 1)
                    for n in range(NH):
                        k = rows_of[n]
                        dve.wait_ge(s_silu, n + 1)
                        dve.wait_ge(s_up, n + 1)
                        if n < ROUTED:
                            nc.vector.tensor_tensor(silu[n % 2][0:k, :], silu[n % 2][0:k, :], bank[0:k, T:2 * T], ALU.mult).then_inc(s_prod, 1)
                            dve.wait_ge(s_prod, n + 1)
                            dve.wait_ge(s_route, n + 1)
                        if n >= 2:
                            dve.wait_ge(s_down, n - 1)
                        if n < ROUTED:
                            nc.vector.tensor_tensor(hidden[n % 2][0:k, :], silu[n % 2][0:k, :], bank[0:k, 2 * T:3 * T], ALU.mult).then_inc(s_hidden, 1)
                        else:
                            nc.vector.tensor_tensor(hidden[n % 2][0:k, :], silu[n % 2][0:k, :], bank[0:k, T:2 * T], ALU.mult).then_inc(s_hidden, 1)
                            if n < NH - 1:
                                nc.vector.memset(zero[:, 0:1], 0.0).then_inc(s_prod, 1)
                    dve.wait_ge(s_down, NH)
                    nc.vector.tensor_tensor(x[:, :, :], x[:, :, :], bank[:, 3 * T:4 * T].rearrange("p (t c) -> p t c", c=P), ALU.add).then_inc(s_end, 1)
                    dve.wait_ge(s_end, 1)


def route_groups(nc, dve, step, s_vec, s, bias, order, weights):
    E, scores, choice = 32, s["prob"], s["choice"]
    step(nc.vector.tensor_tensor(choice[:, :, :], scores[:, :, :], bias[:, :].unsqueeze(1).to_broadcast([P, NT, E]), ALU.add), s_vec)
    for n in range(NT * 4):
        t, g = n // 4, n % 4
        step(nc.vector.max(s["best"][:, t, g, :], choice[:, t, g * 8:(g + 1) * 8]), s_vec, wait=n == NT * 4 - 1)
    step(nc.vector.tensor_tensor(s["groups"][:, :, :], s["best"][:, :, :, 0], s["best"][:, :, :, 1], ALU.add), s_vec)
    select(nc, step, s_vec, s["groups"], order, s["larger"], s["equal"], s["rank"], 2)
    step(nc.vector.tensor_tensor(choice[:, :, :].rearrange("p t (g e) -> p (t g) e", g=4), choice[:, :, :].rearrange("p t (g e) -> p (t g) e", g=4),
                                 s["rank"][:, :, :].rearrange("p t g -> p (t g)").unsqueeze(2).to_broadcast([P, NT * 4, 8]), ALU.mult), s_vec)
    for t in range(NT):
        step(nc.vector.max(s["top"][:, t, :], choice[:, t, :]), s_vec, wait=t == NT - 1)
    for t in range(NT):
        step(nc.vector.match_replace(s["left"][:, t, :], s["top"][:, t, :], choice[:, t, :], MASKED), s_vec, wait=t == NT - 1)
    step(nc.vector.tensor_scalar(s["left"][:, :, :], s["left"][:, :, :], MASKED, None, ALU.is_equal), s_vec)
    step(nc.vector.tensor_tensor(weights[:, :, :], scores[:, :, :], s["left"][:, :, :], ALU.mult), s_vec)
    step(nc.vector.tensor_reduce(s["total"][:, :], weights[:, :, :], AX.X, ALU.add), s_vec)
    step(nc.vector.tensor_scalar(s["total"][:, :], s["total"][:, :], 1e-20, None, ALU.add), s_vec)
    step(nc.vector.reciprocal(s["total"][:, :], s["total"][:, :]), s_vec)
    step(nc.vector.tensor_tensor(weights[:, :, :], weights[:, :, :], s["total"][:, :].unsqueeze(2).to_broadcast([P, NT, E]), ALU.mult), s_vec)
    step(nc.vector.tensor_scalar(weights[:, :, :], weights[:, :, :], 2.5, None, ALU.mult), s_vec)


def mixture0(nc, kept, ps, a):
    mixture(nc, kept, ps, a, 0)


def mixture1(nc, kept, ps, a):
    mixture(nc, kept, ps, a, 1)


def lstm_step(nc, kept, ps, a):
    x, ident = kept["x"], kept["ident"]
    bank = ps[:, :, :].rearrange("p b c -> p (b c)")
    with ExitStack() as stack:
        m = Memory(nc, stack, "lstm")
        w, bias = m.sb("w", [P, 4 * P]), m.sb("bias", [P, 4])
        stats, moments, normed, xn = m.sb("stats", [P, NT, 6]), m.sb("moments", [P, NT, 2]), m.sb("normed", [P, NT, P]), m.sb("xn", [P, T])
        gate_in, gate_out, cand = m.sb("gate_in", [P, T]), m.sb("gate_out", [P, T]), m.sb("cand", [P, T])
        s_load, s_vec, s_eps, s_root, s_norm, s_turned, s_xn_a, s_xn_v, s_gates, s_act, s_cell, s_tanh, s_h, s_back, s_x = (m.sem(n) for n in (
            "loaded", "vector_step", "variance", "root", "normed", "turned", "xn_scalar", "xn_vector", "gates", "activated", "cell", "tanh",
            "state", "state_turned", "x_done"))
        with nc.Block() as block:
            @block.sync
            def _(sp):
                sp.dma_start(w[:, :], a["L1_attn_w"]).then_inc(s_load, 16)
                sp.dma_start(bias[:, :], columns(a["L1_attn_bias"])).then_inc(s_load, 16)
                sp.wait_ge(s_load, 2 * 16)

            @block.tensor
            def _(pe):
                pe.wait_ge(s_load, 2 * 16)
                pe.wait_ge(s_norm, NT)
                transpose_tiles(nc, pe, bank, normed, ident, s_turned)
                pe.wait_ge(s_xn_a, 1)
                pe.wait_ge(s_xn_v, 1)
                for n, g in enumerate((0, 2, 3)):
                    for c in range(2):
                        last = nc.tensor.matmul(ps[:, 2 + 2 * n + c, :], w[:, g * P:(g + 1) * P], xn[:, c * HALF:(c + 1) * HALF], start=True, stop=True)
                    last.then_inc(s_gates, 1)
                pe.wait_ge(s_h, 1)
                for t in range(NT):
                    last = nc.tensor.transpose(bank[:, t * P:(t + 1) * P], cand[:, t * P:(t + 1) * P], ident[:, :])
                last.then_inc(s_back, 1)

            @block.scalar
            def _(act):
                root(nc, act, moments, s_eps, s_root)
                act.wait_ge(s_load, 2 * 16)
                act.wait_ge(s_turned, 1)
                nc.scalar.activation(xn[:, 0:HALF], bank[:, 0:HALF], ACT.Copy).then_inc(s_xn_a, 1)
                for n, (dst, g, f) in enumerate(((gate_in, 0, ACT.Sigmoid), (gate_out, 2, ACT.Sigmoid), (cand, 3, ACT.Tanh))):
                    act.wait_ge(s_gates, n + 1)
                    nc.scalar.activation(dst[:, :], bank[:, (n + 1) * T:(n + 2) * T], f, bias=bias[:, g:g + 1]).then_inc(s_act, 1)
                act.wait_ge(s_cell, 1)
                nc.scalar.activation(cand[:, :], cand[:, :], ACT.Tanh).then_inc(s_tanh, 1)

            @block.vector
            def _(dve):
                step = stepper(dve)
                layer_norm(nc, dve, step, s_vec, stats, moments, x, normed, s_eps, s_root, s_norm)
                dve.wait_ge(s_turned, 2)
                step(nc.vector.tensor_copy(xn[:, HALF:T], bank[:, HALF:T]), s_xn_v)
                dve.wait_ge(s_act, 3)
                step(nc.vector.tensor_tensor(cand[:, :], gate_in[:, :], cand[:, :], ALU.mult), s_cell)
                dve.wait_ge(s_tanh, 1)
                step(nc.vector.tensor_tensor(cand[:, :], gate_out[:, :], cand[:, :], ALU.mult), s_h)
                dve.wait_ge(s_back, 1)
                step(nc.vector.tensor_tensor(x[:, :, :], x[:, :, :], bank[:, 0:T].rearrange("p (t c) -> p t c", c=P), ALU.add), s_x)


def latent_attention(nc, kept, ps, a):
    H1 = 8
    NM, NL = NK, NT
    NZ = NM + NL
    x, ident = kept["x"], kept["ident"]
    bank = ps[:, :, :].rearrange("p b c -> p (b c)")
    with ExitStack() as stack:
        m = Memory(nc, stack, "lat")
        z_rows = [m.sb(f"z_rows_{n}", [P, NZ, P], F32R) for n in ("high", "low")]
        z_cols = [m.sb(f"z_cols_{n}", [P, NZ * P], F32R) for n in ("high", "low")]
        mix = m.sb("mix", [P, 2 * P])
        latents = m.sb("latents", [P, T])

        with ExitStack() as own:
            b = Memory(nc, own, "zed")
            rows, z = b.sb("rows", [P, U0, P]), b.sb("z", [P, U0, P])
            stats, moments, shift = b.sb("stats", [P, U0, 6]), b.sb("moments", [P, U0, 2]), b.sb("shift", [P, U0])
            fresh, norms = b.sb("fresh", [P, 1]), b.sb("norms", [P, 4])
            lstats, lmoments = b.sb("lstats", [P, NT, 6]), b.sb("lmoments", [P, NT, 2])
            lmoments2, normed, normed2 = b.sb("lmoments2", [P, NT, 2]), b.sb("normed", [P, NT, P]), b.sb("normed2", [P, NT, P])
            s_load, s_rows = b.sem("loaded"), [b.sem(f"rows_loaded{n}") for n in range(U0)]
            s_vec, s_stat, s_var, s_root, s_shift, s_z, s_high, s_low, s_turned, s_chigh, s_clow = (b.sem(n) for n in (
                "vector_step", "statistics", "variance", "root", "shift", "z", "rows_high", "rows_low", "turned", "columns_high", "columns_low"))
            s_eps1, s_root1, s_norm1, s_eps2, s_root2, s_norm2, s_lturned, s_mix = (b.sem(n) for n in (
                "eps1", "root1", "norm1", "eps2", "root2", "norm2", "latents_turned", "mix"))
            ctx = a["ctx_1024"][0]
            with nc.Block() as block:
                @block.sync
                def _(sp):
                    for n in range(U0):
                        sp.dma_start(rows[:, n, :], ctx[n * P:(n + 1) * P, :]).then_inc(s_rows[n], 16)
                    sp.dma_start(fresh[:, :], a["fresh"]).then_inc(s_load, 16)
                    for n, name in enumerate(("gamma_media", "beta_media", "gamma_lat", "beta_lat")):
                        sp.dma_start(norms[:, n:n + 1], columns(a[f"L1_xattn_{name}"])).then_inc(s_load, 16)
                    for t in range(U0, NM):
                        sp.wait_ge(s_z, t - U0 + 1)
                        first = min(t * P, LAST)
                        sp.dma_start(rows[:, t % U0, :], ctx[first:first + P, :]).then_inc(s_rows[t % U0], 16)
                    sp.wait_ge(s_load, 5 * 16)

                @block.scalar
                def _(act):
                    def roots(i):
                        act.wait_ge(s_var, i + 1)
                        nc.scalar.activation(moments[:, :, 1], moments[:, :, 1], ACT.Sqrt).then_inc(s_root, 1)

                    def norm(i):
                        act.wait_ge(s_shift, i + 1)
                        for n in range(U0):
                            nc.scalar.activation(z[:, n, :], rows[:, n, :], ACT.Identity, bias=shift[:, n:n + 1], scale=moments[:, n, 1:2]).then_inc(s_z, 1)

                    def high(i):
                        act.wait_ge(s_turned, i + 1)
                        nc.scalar.activation(z_cols[0][:, bass.ds(i * (U0 * P), U0 * P)], ps[:, 0, 0:U0 * P], ACT.Copy).then_inc(s_chigh, 1)

                    roots(0)
                    norm(0)
                    with act.Fori(0, NI - 1) as i:
                        roots(i + 1)
                        high(i)
                        act.wait_ge(s_low, i + 1)
                        norm(i + 1)
                    high(NI - 1)
                    root(nc, act, lmoments, s_eps1, s_root1)
                    root(nc, act, lmoments2, s_eps2, s_root2)

                @block.tensor
                def _(pe):
                    def turn(i):
                        pe.wait_ge(s_z, i * U0 + U0)
                        for n in range(U0):
                            last = nc.tensor.transpose(ps[:, 0, n * P:(n + 1) * P], z[:, n, :], ident[:, :])
                        last.then_inc(s_turned, 1)

                    turn(0)
                    with pe.Fori(0, NI - 1) as i:
                        pe.wait_ge(s_clow, i + 1)
                        turn(i + 1)
                    pe.wait_ge(s_norm2, NT)
                    for t in range(NT):
                        last = nc.tensor.transpose(ps[:, 2 + t // 4, (t % 4) * P:(t % 4 + 1) * P], normed2[:, t, :], ident[:, :])
                        if t % 4 == 3:
                            last.then_inc(s_lturned, 1)

                @block.vector
                def _(dve):
                    step = stepper(dve)

                    def statistics(i):
                        for n in range(U0):
                            dve.wait_ge(s_rows[n], i * 16 + 16)
                            nc.vector.bn_stats(stats[:, n, :], rows[:, n, :]).then_inc(s_stat, 1)

                    def variance(i):
                        for n in range(U0):
                            nc.vector.bn_aggr(moments[:, n, :], stats[:, n, :]).then_inc(s_stat, 1)
                        dve.wait_ge(s_stat, i * 8 + 6)
                        nc.vector.tensor_scalar(moments[:, :, 1], moments[:, :, 1], LN_EPS, None, ALU.add).then_inc(s_var, 1)

                    def shifts(i):
                        dve.wait_ge(s_root, i + 1)
                        nc.vector.reciprocal(moments[:, :, 1], moments[:, :, 1]).then_inc(s_stat, 1)
                        dve.wait_ge(s_stat, i * 8 + 7)
                        nc.vector.scalar_tensor_tensor(shift[:, :], moments[:, :, 0], -1.0, moments[:, :, 1], ALU.mult, ALU.mult).then_inc(s_stat, 1)
                        dve.wait_ge(s_stat, i * 8 + 8)
                        nc.vector.tensor_scalar(shift[:, :], shift[:, :], 1.0, None, ALU.add).then_inc(s_shift, 1)

                    def split_rows(i):
                        dve.wait_ge(s_z, i * U0 + U0)
                        tiles = bass.ds(i * U0, U0)
                        nc.vector.tensor_copy(z_rows[0][:, tiles, :], z[:, :, :]).then_inc(s_high, 1)
                        dve.wait_ge(s_high, i + 1)
                        if not isinstance(i, int):
                            dve.wait_ge(s_stat, i * 8 + 11)
                        nc.vector.tensor_tensor(z_rows[1][:, tiles, :], z[:, :, :], z_rows[0][:, tiles, :].bitcast(F32), ALU.subtract).then_inc(s_low, 1)

                    def split_columns(i):
                        dve.wait_ge(s_chigh, i + 1)
                        cols = bass.ds(i * (U0 * P), U0 * P)
                        nc.vector.tensor_tensor(z_cols[1][:, cols], ps[:, 0, 0:U0 * P], z_cols[0][:, cols].bitcast(F32), ALU.subtract).then_inc(s_clow, 1)

                    statistics(0)
                    dve.wait_ge(s_stat, 3)
                    variance(0)
                    shifts(0)
                    with dve.Fori(0, NI - 1) as i:
                        dve.wait_ge(s_z, i * U0 + U0)
                        statistics(i + 1)
                        split_rows(i)
                        variance(i + 1)
                        shifts(i + 1)
                        split_columns(i)
                    split_rows(NI - 1)
                    split_columns(NI - 1)
                    dve.wait_ge(s_load, 5 * 16)
                    dve.wait_ge(s_low, NI)
                    for part in z_rows:
                        step(nc.vector.tensor_scalar(part[:, NM - 1, :], part[:, NM - 1, :].bitcast(F32), fresh[:, 0:1], None, ALU.mult), s_vec)
                    layer_norm(nc, dve, step, s_vec, lstats, lmoments, x, normed, s_eps1, s_root1, s_norm1)
                    layer_norm(nc, dve, step, s_vec, lstats, lmoments2, normed, normed2, s_eps2, s_root2, s_norm2)
                    for n in range(2):
                        gain, offset = norms[:, 2 * n:2 * n + 1], norms[:, 2 * n + 1:2 * n + 2]
                        step(nc.vector.tensor_tensor(shift[:, n:n + 1], offset, gain, ALU.subtract), s_vec)
                        step(nc.vector.tensor_scalar(shift[:, n:n + 1], shift[:, n:n + 1], 1.0 / P, None, ALU.mult), s_vec)
                        step(nc.vector.tensor_scalar(mix[:, n * P:(n + 1) * P], ident[:, :], gain, shift[:, n:n + 1], ALU.mult, ALU.add), s_mix)
                    for c in range(2):
                        lo, hi = c * HALF, (c + 1) * HALF
                        dve.wait_ge(s_lturned, 2)
                        step(nc.vector.tensor_scalar(latents[:, lo:hi], ps[:, 2 + c, :], norms[:, 2:3], norms[:, 3:4], ALU.mult, ALU.add), s_vec)
                        step(nc.vector.tensor_scalar(normed[:, 4 * c:4 * c + 4, :].rearrange("p t c -> p (t c)"), ps[:, 2 + c, :], 1.0, None, ALU.add), s_vec)
                        step(nc.vector.tensor_copy(z_cols[0][:, NM * P + lo:NM * P + hi], normed[:, 4 * c:4 * c + 4, :].rearrange("p t c -> p (t c)")), s_vec)
                        step(nc.vector.tensor_tensor(z_cols[1][:, NM * P + lo:NM * P + hi], normed[:, 4 * c:4 * c + 4, :].rearrange("p t c -> p (t c)"),
                                                     z_cols[0][:, NM * P + lo:NM * P + hi].bitcast(F32), ALU.subtract), s_vec)
                    step(nc.vector.tensor_scalar(normed2[:, :, :], normed2[:, :, :], 1.0, None, ALU.add), s_vec)
                    step(nc.vector.tensor_copy(z_rows[0][:, NM:NZ, :], normed2[:, :, :]), s_vec)
                    step(nc.vector.tensor_tensor(z_rows[1][:, NM:NZ, :], normed2[:, :, :], z_rows[0][:, NM:NZ, :].bitcast(F32), ALU.subtract), s_vec)

        latent_heads(nc, kept, ps, a, z_rows, z_cols, mix, latents, H1, NM, NL)


def latent_heads(nc, kept, ps, a, z_rows, z_cols, mix, latents, H1, NM, NL):
    x, ident = kept["x"], kept["ident"]
    NZ = NM + NL
    REACH = 11.4
    ROUNDS = 3
    U_LATENTS, TAKE_LATENTS, FOLD_V, OUT_WEIGHTS, OUTPUTS, SCALE, ADD = 0, 1, 3, 5, (7, 8), 9, 10
    FOLD_K, QUERY, R_AT, BOUND, EXACT = 12, 14, (16, 24), 30, 32
    SUM, SQUARES = 2, 4
    TAKE_MEDIA, U_MEDIA = NM, NM + 2
    bank = ps[:, :, :].rearrange("p b c -> p (b c)")
    mid = bank[:, 6 * HALF:8 * HALF]
    with ExitStack() as own:
        b = Memory(nc, own, "hed")
        w_q, w_k, w_v, w_o = (b.sb(n, [P, P]) for n in ("w_q", "w_k", "w_v", "w_o"))
        biases = b.sb("biases", [P, 3, H1])
        b_o = b.sb("b_o", [P, P])
        k2, v2, w2 = (b.sb(n, [P, 2, P]) for n in ("k2", "v2", "w2"))
        q = b.sb("q", [P, T])
        r = [[b.sb(f"r_{g}_{part}", [P, T], F32R) for part in ("high", "low")] for g in ("media", "latents")]
        r_next = [[b.sb(f"r_next_{g}_{part}", [P, T], F32R) for part in ("high", "low")] for g in ("media", "latents")]
        squares = b.sb("squares", [P, T], F32R)
        ones_in, ones, mean = b.sb("ones_in", [P, P]), b.sb("ones", [P, P], F32R), b.sb("mean", [P, 1])
        peak = b.sb("peak", [P, 2, 2])
        twice, quotient = b.sb("twice", [P, 2]), b.sb("quotient", [P, 2])
        bound, minus, minus_next = b.sb("bound", [P, 1]), b.sb("minus", [P, 1]), b.sb("minus_next", [P, 1])
        exps = [b.sb(f"exps{n}", [P, T]) for n in range(2)]
        high = [b.sb(f"exps_high{n}", [P, T], F32R) for n in range(2)]
        low = [b.sb(f"exps_low{n}", [P, T], F32R) for n in range(2)]
        u = [b.sb(f"u_{g}", [P, T]) for g in ("media", "latents")]
        inverse = b.sb("inverse", [P, NT])
        row_max, chunk_max, spread_max = b.sb("row_max", [P, NT]), b.sb("chunk_max", [P, NT]), b.sb("spread_max", [P, P])
        s_bias, s_w_qk, s_w_vo, s_set, s_end = (b.sem(n) for n in ("biases_loaded", "w_q_k_loaded", "w_v_o_loaded", "set", "end"))
        s_fold_k, s_k2, s_q, s_q_kept, s_r, s_r_high, s_r_low, s_sq, s_bound_mm, s_peak, s_root, s_bound, s_ready = (b.sem(n) for n in (
            "keys_folded", "k2", "q", "q_kept", "r", "r_high", "r_low", "squares", "bound_sums", "peaks", "root", "bound_step", "ready"))
        s_take_low, s_take_high = ([b.sem(f"taken_{part}_{g}") for g in ("media", "latents")] for part in ("low", "high"))
        s_minus = b.sem("minus")
        s_score, s_exp, s_high, s_low, s_weighted = (b.sem(n) for n in ("scores", "exps", "exps_high", "exps_low", "weighted"))
        s_u_media, s_u_latents, s_fold_v, s_v2, s_w2, s_w2_kept, s_den, s_inv, s_y, s_scaled, s_added = (b.sem(n) for n in (
            "u_media", "u_latents", "values_folded", "v2", "w2", "w2_kept", "denominators", "inverse", "outputs", "outputs_scaled", "added"))
        x_score, x_max, x_row, x_spread, x_turned, x_fixed, x_done = (b.sem(n) for n in (
            "exact_scores", "exact_max", "exact_row", "exact_spread", "exact_turned", "exact_fixed", "exact_done"))
        XN = NI * NT + 2 * NT
        ROWS = NI + 3

        with nc.Block() as block:
            @block.sync
            def _(sp):
                for n, name in enumerate(("bq", "bk", "bv")):
                    src = a["L1_xattn_bq"] if n == 0 else a["L1_xattn_bkv"][(n - 1) * H1 * P:n * H1 * P]
                    sp.dma_start(biases[:, n, :], columns(src)).then_inc(s_bias, 16)
                sp.dma_start(b_o[:, :], spread(a["L1_xattn_bo"])).then_inc(s_bias, 16)

                def load_qk(h):
                    sp.dma_start(w_q[:, :], a["L1_xattn_Wq"][:, bass.ds(h * P, P)]).then_inc(s_w_qk, 16)
                    sp.dma_start(w_k[:, :], a["L1_xattn_Wkv"][:, bass.ds(h * P, P)]).then_inc(s_w_qk, 16)

                def load_vo(h):
                    sp.dma_start(w_v[:, :], a["L1_xattn_Wkv"][:, bass.ds(h * P + H1 * P, P)]).then_inc(s_w_vo, 16)
                    sp.dma_start(w_o[:, :], a["L1_xattn_Wo"][bass.ds(h * P, P), :]).then_inc(s_w_vo, 16)

                load_qk(0)
                load_vo(0)
                with sp.Fori(0, H1 - 1) as h:
                    sp.wait_ge(s_q, h + 1)
                    load_qk(h + 1)
                    sp.wait_ge(s_w2, h + 1)
                    load_vo(h + 1)
                sp.wait_ge(s_w_qk, H1 * 2 * 16)
                sp.wait_ge(s_w_vo, H1 * 2 * 16)
                sp.wait_ge(s_bias, 4 * 16)

            @block.tensor
            def _(pe):
                def scores(h, t):
                    if t >= 2:
                        pe.wait_ge(s_high, h * NZ + (t - 1))
                    elif t == 0 and not first_head(h):
                        pe.wait_ge(s_high, h * NZ)
                    if t in (0, NM):
                        pe.wait_ge(s_take_low[t >= NM], h + 1)
                        pe.wait_ge(s_take_high[t >= NM], h + 1)
                    group = r[t >= NM]
                    for c in range(2):
                        for n, (zp, rp) in enumerate(((0, 0), (0, 1), (1, 0))):
                            last = nc.tensor.matmul(ps[:, 2 * (t % 2) + c, :], z_cols[zp][:, t * P:(t + 1) * P], group[rp][:, c * HALF:(c + 1) * HALF],
                                                    start=n == 0, stop=n == 2)
                    last.then_inc(s_score, 1)

                def weigh(h, t):
                    if t == 0 and not first_head(h):
                        pe.wait_ge(s_u_media, h)
                    if t == NM and not first_head(h):
                        pe.wait_ge(s_added, h)
                    pe.wait_ge(s_low, h * NZ + (t + 1))
                    first, last_tile = (0, NM - 1) if t < NM else (NM, NZ - 1)
                    for c in range(2):
                        for n, (zp, e) in enumerate(((0, high), (0, low), (1, high))):
                            last = nc.tensor.matmul(ps[:, (4 if t < NM else 6) + c, :], z_rows[zp][:, t, :], e[t % 2][:, c * HALF:(c + 1) * HALF],
                                                    start=t == first and n == 0, stop=t == last_tile and n == 2)
                    last.then_inc(s_weighted, 1)

                def finish(h, at):
                    if at == U_LATENTS:
                        weigh(h, NZ - 1)
                    elif at == FOLD_V:
                        pe.wait_ge(s_w_vo, h * 32 + 32)
                        pe.wait_ge(s_u_latents, h + 1)
                        nc.tensor.matmul(ps[:, 6, 0:2 * P], w_v[:, :], mix[:, :], start=True, stop=True).then_inc(s_fold_v, 1)
                    elif at == OUT_WEIGHTS:
                        pe.wait_ge(s_v2, h + 1)
                        for g in range(2):
                            last = nc.tensor.matmul(ps[:, 6, g * P:(g + 1) * P], v2[:, g, :], w_o[:, :], start=True, stop=True)
                        last.then_inc(s_w2, 1)
                        pe.wait_ge(s_u_media, h + 1)
                        for t in range(NT):
                            for g in range(2):
                                last = nc.tensor.matmul(ps[:, 7, t:t + 1], u[g][:, t * P:(t + 1) * P], mean[:, :], start=g == 0, stop=g == 1)
                        last.then_inc(s_den, 1)
                    elif at in OUTPUTS:
                        if at == OUTPUTS[0]:
                            pe.wait_ge(s_w2_kept, h + 1)
                            pe.wait_ge(s_inv, h + 1)
                        c = OUTPUTS.index(at)
                        for t in range(4 * c, 4 * c + 4):
                            for g in range(2):
                                last = nc.tensor.matmul(mid[:, t * P:(t + 1) * P], u[g][:, t * P:(t + 1) * P], w2[:, g, :], start=g == 0, stop=g == 1)
                        last.then_inc(s_y, 1)

                def prepare(h, at):
                    if at == FOLD_K:
                        pe.wait_ge(s_w_qk, h * 32 + 32)
                        nc.tensor.matmul(ps[:, 6, 0:2 * P], w_k[:, :], mix[:, :], start=True, stop=True).then_inc(s_fold_k, 1)
                    elif at == QUERY:
                        pe.wait_ge(s_k2, h + 1)
                        for c in range(2):
                            last = nc.tensor.matmul(ps[:, 6 + c, :], w_q[:, :], latents[:, c * HALF:(c + 1) * HALF], start=True, stop=True)
                        last.then_inc(s_q, 1)
                    for g in range(2):
                        if at == R_AT[g]:
                            if g == 0:
                                pe.wait_ge(s_q_kept, h + 1)
                            else:
                                pe.wait_ge(s_peak, h * 4 + 2)
                            for c in range(2):
                                last = nc.tensor.matmul(ps[:, 6 + c, :], k2[:, g, :], q[:, c * HALF:(c + 1) * HALF], start=True, stop=True)
                            last.then_inc(s_r, 1)
                        elif at == R_AT[g] + SUM:
                            pe.wait_ge(s_r_low, h * 2 + (g + 1))
                            for c in range(2):
                                last = nc.tensor.matmul(ps[:, 6 + c, :], ones[:, :], r_next[g][0][:, c * HALF:(c + 1) * HALF], start=True, stop=True)
                            last.then_inc(s_bound_mm, 1)
                        elif at == R_AT[g] + SQUARES:
                            pe.wait_ge(s_sq, h * 2 + (g + 1))
                            pe.wait_ge(s_peak, h * 4 + (2 * g + 1))
                            for c in range(2):
                                last = nc.tensor.matmul(ps[:, 6 + c, :], ones[:, :], squares[:, c * HALF:(c + 1) * HALF], start=True, stop=True)
                            last.then_inc(s_bound_mm, 1)
                    if at == EXACT:
                        pe.wait_ge(s_ready, h + 1)
                        nc.tensor.matmul(ps[:, 6, 0:1], ident[:, :], bound[:, :], start=True, stop=True)
                        bits = nc.tensor.value_load(bound[0:1, 0:1].bitcast(I32))
                        with pe.If(bits > SAFE_BITS):
                            exact(h)

                def exact(h):
                    def block_scores(g, cols, n, base, width):
                        if n >= 2:
                            pe.wait_ge(x_max, h * XN + base + (n - 1))
                        for k, (rp, zp) in enumerate(((0, 0), (0, 1), (1, 0))):
                            last = nc.tensor.matmul(ps[:, 6 + n % 2, 0:width], r_next[g][rp][:, n % NT * P:(n % NT + 1) * P], z_cols[zp][:, cols],
                                                    start=k == 0, stop=k == 2)
                        last.then_inc(x_score, 1)

                    with pe.Fori(0, NI) as i:
                        pe.wait_ge(x_row, h * ROWS + i + 1)
                        for n in range(NT):
                            block_scores(0, bass.ds(i * (U0 * P), U0 * P), n, i * NT, U0 * P)
                    pe.wait_ge(x_row, h * ROWS + NI + 1)
                    for n in range(2 * NT):
                        block_scores(1, slice(NM * P + n // NT * HALF, NM * P + (n // NT + 1) * HALF), n, NI * NT, HALF)
                    for t in range(NT):
                        pe.wait_ge(x_spread, h * NT + (t + 1))
                        nc.tensor.matmul(mid[:, t * P:(t + 1) * P], spread_max[:, :], ident[:, :], start=True, stop=True).then_inc(x_turned, 1)
                    pe.wait_ge(x_done, h + 1)

                def head(h, before=True, after=True):
                    for t in range(NZ):
                        scores(h, t)
                        if t >= 2:
                            weigh(h, t - 2)
                        if before:
                            finish(h - 1, t)
                        if after:
                            prepare(h + 1, t)
                    weigh(h, NZ - 2)

                pe.wait_ge(s_set, 4)
                for at in range(NZ):
                    prepare(0, at)
                head(0, before=False)
                with pe.Fori(1, H1 - 1) as h:
                    head(h)
                head(H1 - 1, after=False)
                for at in range(NZ):
                    finish(H1 - 1, at)

            @block.scalar
            def _(act):
                def tile(h, t):
                    act.wait_ge(s_score, h * NZ + (t + 1))
                    if t >= 2:
                        act.wait_ge(s_low, h * NZ + (t - 1))
                    pair = bank[:, 2 * (t % 2) * HALF:(2 * (t % 2) + 2) * HALF]
                    nc.scalar.activation(exps[t % 2][:, :], pair, ACT.Exp, bias=minus[:, 0:1]).then_inc(s_exp, 1)
                    if t >= 2:
                        act.wait_ge(s_weighted, h * NZ + (t - 1))
                    elif t == 0 and not first_head(h):
                        act.wait_ge(s_weighted, h * NZ)
                    nc.scalar.activation(high[t % 2][:, :], pair, ACT.Exp, bias=minus[:, 0:1]).then_inc(s_high, 1)

                def finish(h, at):
                    if at == OUT_WEIGHTS:
                        act.wait_ge(s_w2, h + 1)
                        nc.scalar.activation(w2[:, :, :], ps[:, 6, 0:2 * P].rearrange("p (g c) -> p g c", g=2), ACT.Copy).then_inc(s_w2_kept, 1)

                def prepare(h, at):
                    for g in range(2):
                        if at == R_AT[g]:
                            act.wait_ge(s_r, h * 2 + (g + 1))
                            if not first_head(h):
                                act.wait_ge(s_take_high[g], h)
                            nc.scalar.activation(r_next[g][0][:, :], mid, ACT.Copy).then_inc(s_r_high, 1)
                        elif at == R_AT[g] + SUM:
                            act.wait_ge(s_r_high, h * 2 + (g + 1))
                            if g:
                                act.wait_ge(s_bound_mm, h * 4 + 2)
                            nc.scalar.activation(squares[:, :], r_next[g][0][:, :].bitcast(F32), ACT.Square).then_inc(s_sq, 1)

                def take(h, g):
                    act.wait_ge(s_take_low[g], h + 1)
                    nc.scalar.activation(r[g][0][:, :], r_next[g][0][:, :].bitcast(F32), ACT.Copy).then_inc(s_take_high[g], 1)

                def head(h, before=True, after=True):
                    if before:
                        act.wait_ge(s_high, h * NZ)
                    act.wait_ge(s_take_low[0], h + 1)
                    nc.scalar.activation(minus[:, :], minus_next[:, :], ACT.Copy).then_inc(s_minus, 1)
                    act.wait_ge(s_minus, h + 1)
                    if before:
                        act.wait_ge(s_low, h * NZ)
                    for t in range(NZ):
                        tile(h, t)
                        if t == TAKE_LATENTS:
                            take(h, 1)
                        if before:
                            finish(h - 1, t)
                        if after:
                            prepare(h + 1, t)
                            if t == TAKE_MEDIA:
                                take(h + 1, 0)
                        if t == U_MEDIA:
                            copy_media(h, before)

                def copy_media(h, before):
                    act.wait_ge(s_weighted, h * NZ + NM)
                    if before:
                        act.wait_ge(s_y, h * 2)
                    nc.scalar.activation(u[0][:, :], bank[:, 4 * HALF:6 * HALF], ACT.Copy).then_inc(s_u_media, 1)

                act.wait_ge(s_set, 4)
                for at in range(NZ):
                    prepare(0, at)
                take(0, 0)
                head(0, before=False)
                with act.Fori(1, H1 - 1) as h:
                    head(h)
                head(H1 - 1, after=False)
                for at in range(NZ):
                    finish(H1 - 1, at)

            @block.vector
            def _(dve):
                step = stepper(dve)

                def exact(h):
                    def maxima(base, done, width):
                        dve.wait_ge(x_row, h * ROWS + done)
                        for n in range(NT):
                            dve.wait_ge(x_score, h * XN + base + (n + 1))
                            nc.vector.tensor_reduce(chunk_max[:, n:n + 1], ps[:, 6 + n % 2, 0:width], AX.X, ALU.max).then_inc(x_max, 1)
                        dve.wait_ge(x_max, h * XN + base + NT)
                        nc.vector.tensor_tensor(row_max[:, :], row_max[:, :], chunk_max[:, :], ALU.max).then_inc(x_row, 1)

                    nc.vector.memset(row_max[:, :], MASKED).then_inc(x_row, 1)
                    with dve.Fori(0, NI) as i:
                        maxima(i * NT, i + 1, U0 * P)
                    for k in range(2):
                        maxima(NI * NT + k * NT, NI + 1 + k, HALF)
                    dve.wait_ge(x_row, h * ROWS + NI + 3)
                    for t in range(NT):
                        if t:
                            dve.wait_ge(x_turned, h * NT + t)
                        nc.vector.tensor_copy(spread_max[:, :], row_max[:, t:t + 1].to_broadcast([P, P])).then_inc(x_spread, 1)
                    dve.wait_ge(x_turned, h * NT + NT)
                    for g in range(2):
                        nc.vector.tensor_tensor(q[:, :], r_next[g][0][:, :].bitcast(F32), r_next[g][1][:, :].bitcast(F32), ALU.add).then_inc(x_fixed, 1)
                        dve.wait_ge(x_fixed, h * 8 + (4 * g + 1))
                        nc.vector.scalar_tensor_tensor(q[:, :], mid, -1.0 / P, q[:, :], ALU.mult, ALU.add).then_inc(x_fixed, 1)
                        dve.wait_ge(x_fixed, h * 8 + (4 * g + 2))
                        nc.vector.tensor_copy(r_next[g][0][:, :], q[:, :]).then_inc(x_fixed, 1)
                        dve.wait_ge(x_fixed, h * 8 + (4 * g + 3))
                        nc.vector.tensor_tensor(r_next[g][1][:, :], q[:, :], r_next[g][0][:, :].bitcast(F32), ALU.subtract).then_inc(x_fixed, 1)
                        dve.wait_ge(x_fixed, h * 8 + (4 * g + 4))
                    nc.vector.memset(minus_next[:, :], 0.0).then_inc(x_done, 1)

                def finish(h, at):
                    if at == U_LATENTS:
                        dve.wait_ge(s_weighted, h * NZ + NZ)
                        nc.vector.tensor_copy(u[1][:, :], mid).then_inc(s_u_latents, 1)
                    elif at == FOLD_V:
                        dve.wait_ge(s_fold_v, h + 1)
                        nc.vector.tensor_scalar(v2[:, :, :], ps[:, 6, 0:2 * P].rearrange("p (g c) -> p g c", g=2),
                                                biases[:, 2, bass.ds(h, 1)], None, ALU.add).then_inc(s_v2, 1)
                    elif at == OUT_WEIGHTS:
                        dve.wait_ge(s_den, h + 1)
                        nc.vector.reciprocal(inverse[:, :], ps[:, 7, 0:NT]).then_inc(s_inv, 1)
                    elif at == SCALE:
                        dve.wait_ge(s_y, h * 2 + 2)
                        nc.vector.tensor_tensor(q[:, :].rearrange("p (t c) -> p t c", c=P), mid.rearrange("p (t c) -> p t c", c=P),
                                                inverse[:, :].unsqueeze(2).to_broadcast([P, NT, P]), ALU.mult).then_inc(s_scaled, 1)
                    elif at == ADD:
                        dve.wait_ge(s_scaled, h + 1)
                        if not first_head(h):
                            dve.wait_ge(s_added, h)
                        nc.vector.tensor_tensor(x[:, :, :], x[:, :, :], q[:, :].rearrange("p (t c) -> p t c", c=P), ALU.add).then_inc(s_added, 1)

                def prepare(h, at):
                    if at == FOLD_K:
                        dve.wait_ge(s_fold_k, h + 1)
                        nc.vector.tensor_scalar(k2[:, :, :], ps[:, 6, 0:2 * P].rearrange("p (g c) -> p g c", g=2),
                                                biases[:, 1, bass.ds(h, 1)], None, ALU.add).then_inc(s_k2, 1)
                    elif at == QUERY:
                        dve.wait_ge(s_q, h + 1)
                        if not (first_head(h) or first_head(h - 1)):
                            dve.wait_ge(s_added, h - 1)
                        nc.vector.tensor_scalar(q[:, :], mid, biases[:, 0, bass.ds(h, 1)], float(P) ** -0.5, ALU.add, ALU.mult).then_inc(s_q_kept, 1)
                    for g in range(2):
                        if at == R_AT[g]:
                            dve.wait_ge(s_r_high, h * 2 + (g + 1))
                            if not first_head(h):
                                dve.wait_ge(s_take_low[g], h)
                            nc.vector.tensor_tensor(r_next[g][1][:, :], mid, r_next[g][0][:, :].bitcast(F32), ALU.subtract).then_inc(s_r_low, 1)
                        elif at == R_AT[g] + SUM:
                            dve.wait_ge(s_bound_mm, h * 4 + (2 * g + 1))
                            nc.vector.tensor_reduce(peak[:, g, 0:1], mid, AX.X, ALU.max, apply_absolute_value=True).then_inc(s_peak, 1)
                        elif at == R_AT[g] + SQUARES:
                            dve.wait_ge(s_bound_mm, h * 4 + (2 * g + 2))
                            nc.vector.tensor_reduce(peak[:, g, 1:2], mid, AX.X, ALU.max).then_inc(s_peak, 1)
                    if at == BOUND:
                        dve.wait_ge(s_peak, h * 4 + 4)
                        nc.vector.tensor_scalar(twice[:, :], peak[:, :, 1], 1.0, None, ALU.add).then_inc(s_root, 1)
                        for n in range(ROUNDS):
                            dve.wait_ge(s_root, h * (3 * ROUNDS + 1) + 3 * n + 1)
                            nc.vector.reciprocal(quotient[:, :], twice[:, :]).then_inc(s_root, 1)
                            dve.wait_ge(s_root, h * (3 * ROUNDS + 1) + 3 * n + 2)
                            nc.vector.scalar_tensor_tensor(quotient[:, :], quotient[:, :], 2.0, peak[:, :, 1], ALU.mult, ALU.mult).then_inc(s_root, 1)
                            dve.wait_ge(s_root, h * (3 * ROUNDS + 1) + 3 * n + 3)
                            nc.vector.scalar_tensor_tensor(twice[:, :], twice[:, :], 0.5, quotient[:, :], ALU.mult, ALU.add).then_inc(s_root, 1)
                        dve.wait_ge(s_root, (h + 1) * (3 * ROUNDS + 1))
                        nc.vector.scalar_tensor_tensor(peak[:, :, 0], twice[:, :], REACH / 2, peak[:, :, 0], ALU.mult, ALU.add).then_inc(s_bound, 1)
                        dve.wait_ge(s_bound, h * 2 + 1)
                        nc.vector.tensor_reduce(bound[:, :], peak[:, :, 0], AX.X, ALU.max).then_inc(s_bound, 1)
                        dve.wait_ge(s_bound, h * 2 + 2)
                        if not first_head(h):
                            dve.wait_ge(s_minus, h)
                        nc.vector.tensor_scalar(minus_next[:, :], bound[:, :], -1.0, None, ALU.mult).then_inc(s_ready, 1)
                    elif at == EXACT:
                        bits = nc.vector.value_load(bound[0:1, 0:1].bitcast(I32))
                        with dve.If(bits > SAFE_BITS):
                            exact(h)

                def take(h, g):
                    if not first_head(h):
                        dve.wait_ge(s_score, h * NZ if g else h * NZ - NL)
                    nc.vector.tensor_copy(r[g][1][:, :], r_next[g][1][:, :].bitcast(F32)).then_inc(s_take_low[g], 1)

                def head(h, before=True, after=True):
                    for t in range(NZ):
                        dve.wait_ge(s_high, h * NZ + (t + 1))
                        nc.vector.tensor_tensor(low[t % 2][:, :], exps[t % 2][:, :], high[t % 2][:, :].bitcast(F32), ALU.subtract).then_inc(s_low, 1)
                        if t == TAKE_LATENTS:
                            take(h, 1)
                        if before:
                            finish(h - 1, t)
                        if after:
                            prepare(h + 1, t)
                            if t == TAKE_MEDIA:
                                take(h + 1, 0)

                step(nc.vector.memset(ones_in[:, :], 1.0), s_set)
                step(nc.vector.tensor_copy(ones[:, :], ones_in[:, :]), s_set)
                step(nc.vector.memset(mean[:, :], 1.0 / P), s_set)
                dve.wait_ge(s_bias, 4 * 16)
                step(nc.vector.tensor_scalar(biases[:, 1:3, :], biases[:, 1:3, :], 1.0 / P, None, ALU.mult), s_set)
                for at in range(NZ):
                    prepare(0, at)
                take(0, 0)
                head(0, before=False)
                with dve.Fori(1, H1 - 1) as h:
                    head(h)
                head(H1 - 1, after=False)
                for at in range(NZ):
                    finish(H1 - 1, at)
                dve.wait_ge(s_added, H1)
                step(nc.vector.tensor_tensor(x[:, :, :], x[:, :, :], b_o[:, :].unsqueeze(1).to_broadcast([P, NT, P]), ALU.add), s_end)


def first_head(h):
    return isinstance(h, int) and h == 0


STAGES = [linear_attention, cross_attention, mixture0, lstm_step, latent_attention, mixture1]


def decoder(nc, a, out):
    with nc.allow_non_contiguous_dma(reason="columns of biases"):
        program(nc, a, out)


def program(nc, a, out):
    with ExitStack() as stack:
        kept = {
            "x": stack.enter_context(nc.sbuf_tensor("x", [P, NT, P], F32)),
            "ident": stack.enter_context(nc.sbuf_tensor("ident", [P, P], F32)),
        }
        ps = stack.enter_context(nc.psum_tensor("ps", [P, 8, HALF], F32))
        s_start = nc.alloc_semaphore("start_loaded")
        with nc.Block() as block:
            @block.sync
            def _(sp):
                sp.dma_start(kept["x"][:, :, :], a["x"][0].rearrange("(t p) c -> p t c", p=P)).then_inc(s_start, 16)
                sp.dma_start(kept["ident"][:, :], a["ident"]).then_inc(s_start, 16)
                sp.wait_ge(s_start, 2 * 16)
        for stage in STAGES:
            stage(nc, kept, ps, a)
            nc.clear_and_free_semaphores(list(Memory.taken))
            Memory.taken.clear()
            nc.all_engine_barrier()
        s_out = nc.alloc_semaphore("out_written")
        with nc.Block() as block:
            @block.sync
            def _(sp):
                sp.dma_start(out[0].rearrange("(t p) c -> p t c", p=P), kept["x"][:, :, :]).then_inc(s_out, 16)
                sp.wait_ge(s_out, 16)


def shape_constants():
    def angles(rows, length):
        inv_freq = np.float32(1.0) / np.float32(10000.0) ** (np.arange(0, D0, 2, dtype=np.float32) / np.float32(D0))
        pos = np.float32(10.0) * (np.arange(length, dtype=np.float32) / np.float32(length))
        ang = pos[rows][..., None] * inv_freq
        return np.stack([np.cos(ang), np.sin(ang)], axis=-2).astype(np.float32)

    def before(n):
        return np.broadcast_to(np.tril(np.ones((n, n), np.float32), -1), (P, n, n)).copy()

    def picks(experts, hidden):
        unit = np.arange(experts * hidden) // hidden
        rows = np.arange(P)[:, None]
        return ((rows == unit) | (rows == unit + 32)).astype(np.float32).reshape(P, -1, P)

    p = np.arange(P)
    keys = np.stack([t * P + p if t < NK - 1 else LAST + p for t in range(NK)], axis=1)
    return {
        "ident": np.eye(P, dtype=np.float32),
        "tri": np.triu(np.ones((P, P), np.float32)),
        "rope_q": angles(np.stack([t * P + p for t in range(NT)], axis=1), T),
        "rope_k": angles(keys, LC),
        "fresh": (p >= REPEATED).astype(np.float32)[:, None].copy(),
        "order8": before(8),
        "order4": before(4),
        "picks0": picks(8, 176),
        "picks1": picks(32, 64),
        "head_rows": (p[:, None] // ROW == np.arange(G0)[None, :]).astype(np.float32),
    }


def kernel(**inputs):
    import concourse.bacc as bacc
    from concourse.bass_utils import run_bass_kernel_spmd

    nc = bacc.Bacc("TRN2", target_bir_lowering=False, num_devices=1)
    arrays, aps = {}, {}
    for name, array in {**inputs, **shape_constants()}.items():
        array = np.ascontiguousarray(array)
        if array.dtype == np.bool_:
            array = array.view(np.uint8)
        arrays[f"in_{name}"] = array
        aps[name] = nc.dram_tensor(f"in_{name}", array.shape, mybir.dt.from_np(array.dtype), kind="ExternalInput").ap()
    out = nc.dram_tensor("out", (1, T, P), F32, kind="ExternalOutput").ap()
    decoder(nc, aps, out)
    result = run_bass_kernel_spmd(nc, [arrays], core_ids=[0])
    return result.results[0]["out"]
```

```python
from contextlib import ExitStack

import numpy as np
import concourse.bass as bass
from concourse import mybir

F32 = mybir.dt.float32
F32R = mybir.dt.float32r
I32 = mybir.dt.int32
U8 = mybir.dt.uint8
ALU = mybir.AluOpType
ACT = mybir.ActivationFunctionType
AX = mybir.AxisListType

P = 128
T = 1024
NT = T // P
HALF = 512
LC = 6404
NK = -(-LC // P)
LAST = LC - P
REPEATED = NK * P - LC
LN_EPS = 1e-5
DEN_EPS = 1e-6
H0, D0 = 16, 8
G0 = 4
NG = H0 // G0
ROW = 32
U0 = 3
NI = NK // U0
SAFE = 40.0
SAFE_BITS = int(np.float32(SAFE).view(np.int32))
MASKED = -1e30


def stepper(engine):
    done = {}

    def step(instruction, semaphore, wait=True):
        instruction.then_inc(semaphore, 1)
        done[semaphore.name] = done.get(semaphore.name, 0) + 1
        if wait:
            engine.wait_ge(semaphore, done[semaphore.name])

    return step


def layer_norm(nc, dve, step, s_chain, stats, moments, src, dst, eps_done, root_done, out_done, n=NT, first=0):
    for t in range(n):
        step(nc.vector.bn_stats(stats[:, t, :], src[:, t, :]), s_chain, wait=t == n - 1)
    for t in range(n):
        step(nc.vector.bn_aggr(moments[:, t, :], stats[:, t, :]), s_chain, wait=t == n - 1)
    step(nc.vector.tensor_scalar(moments[:, 0:n, 1], moments[:, 0:n, 1], LN_EPS, None, ALU.add), eps_done)
    dve.wait_ge(root_done, first + 1)
    step(nc.vector.reciprocal(moments[:, 0:n, 1], moments[:, 0:n, 1]), s_chain)
    for t in range(n):
        step(nc.vector.tensor_scalar(dst[:, t, :], src[:, t, :], moments[:, t, 0:1], moments[:, t, 1:2],
                                     ALU.subtract, ALU.mult), out_done, wait=t == n - 1)


def root(nc, act, moments, eps_done, root_done, n=NT, first=0):
    act.wait_ge(eps_done, first + 1)
    nc.scalar.activation(moments[:, 0:n, 1], moments[:, 0:n, 1], ACT.Sqrt).then_inc(root_done, 1)


def transpose_tiles(nc, pe, bank, src, ident, done):
    for t in range(NT):
        last = nc.tensor.transpose(bank[:, t * P:(t + 1) * P], src[:, t, :], ident[:, :])
        if t % 4 == 3:
            last.then_inc(done, 1)


def columns(ap, width=P):
    return ap.rearrange("(c p) -> p c", p=width)


def spread(ap):
    return ap.rearrange("(a n) -> a n", a=1).to_broadcast([P, ap.shape[0]])


class Memory:

    taken = []

    def __init__(self, nc, stack, stage):
        self.nc, self.stack, self.stage = nc, stack, stage

    def sb(self, name, shape, dtype=F32):
        return self.stack.enter_context(self.nc.sbuf_tensor(f"{self.stage}_{name}", shape, dtype))

    def sem(self, name):
        semaphore = self.nc.alloc_semaphore(f"{self.stage}_{name}")
        self.taken.append(semaphore)
        return semaphore


def linear_attention(nc, kept, ps, a):
    with ExitStack() as stack:
        m = Memory(nc, stack, "lin")
        qkv_w, gate_w = m.sb("qkv_w", [P, 3 * P]), m.sb("gate_w", [P, P])
        biases = m.sb("biases", [P, 6])
        v_bias = m.sb("v_bias", [P, P])
        stats, moments, moments2 = m.sb("stats", [P, NT, 6]), m.sb("moments", [P, NT, 2]), m.sb("moments2", [P, NT, 2])
        normed, normed2 = m.sb("normed", [P, NT, P]), m.sb("normed2", [P, NT, P])
        xn = m.sb("xn", [P, T])
        q, k, gate, small = (m.sb(n, [P, T]) for n in ("q", "k", "gate", "small"))
        small_k = m.sb("small_k", [P, T])
        v = m.sb("v", [P, NT, P + 1])
        scores = m.sb("scores", [P, NT, T])
        den = m.sb("den", [P, NT])
        s_load = m.sem("loaded")
        s_vec, s_eps, s_root, s_norm, s_norm2 = (m.sem(n) for n in ("vector_step", "variance", "root", "normed", "normed2"))
        s_eps2, s_root2 = m.sem("variance2"), m.sem("root2")
        s_turned, s_xn_a, s_xn_v = m.sem("turned"), m.sem("xn_scalar"), m.sem("xn_vector")
        s_proj, s_gate, s_pre, s_exp, s_qk, s_v = (m.sem(n) for n in ("projected", "gate", "pre_elu", "exps", "q_k", "v"))
        s_score, s_sc, s_sum, s_x2 = (m.sem(n) for n in ("scores", "scores_kept", "sums", "x_done"))
        s_cp = m.sem("scores_copied")
        x, ident, tri = kept["x"], kept["ident"], m.sb("tri", [P, P])
        bank = ps[:, :, :].rearrange("p b c -> p (b c)")
        pairs = [(s, c) for s in range(NT) for c in range(s // 4, 2)]

        with nc.Block() as block:
            @block.sync
            def _(sp):
                sp.dma_start(qkv_w[:, :], a["L0_attn_qkv_w"]).then_inc(s_load, 16)
                sp.dma_start(gate_w[:, :], a["L0_attn_gate_w"]).then_inc(s_load, 16)
                sp.dma_start(v_bias[:, :], spread(a["L0_attn_qkv_b"][2 * P:3 * P])).then_inc(s_load, 16)
                sp.dma_start(biases[:, 0:3], columns(a["L0_attn_qkv_b"])).then_inc(s_load, 16)
                sp.dma_start(biases[:, 3:4], columns(a["L0_attn_gate_b"])).then_inc(s_load, 16)
                sp.dma_start(biases[:, 4:5], columns(a["L0_attn_ln_g"])).then_inc(s_load, 16)
                sp.dma_start(biases[:, 5:6], columns(a["L0_attn_ln_b"])).then_inc(s_load, 16)
                sp.dma_start(tri[:, :], a["tri"]).then_inc(s_load, 16)
                sp.wait_ge(s_load, 8 * 16)

            @block.scalar
            def _(act):
                root(nc, act, moments, s_eps, s_root)
                root(nc, act, moments2, s_eps2, s_root2)
                act.wait_ge(s_load, 8 * 16)
                act.wait_ge(s_turned, 1)
                nc.scalar.activation(xn[:, 0:HALF], bank[:, 0:HALF], ACT.Identity, bias=biases[:, 5:6],
                                     scale=biases[:, 4:5]).then_inc(s_xn_a, 1)
                act.wait_ge(s_proj, 2)
                nc.scalar.activation(gate[:, :], bank[:, 2 * T:3 * T], ACT.Sigmoid, bias=biases[:, 3:4]).then_inc(s_gate, 1)
                act.wait_ge(s_pre, 1)
                nc.scalar.activation(small[:, :], small[:, :], ACT.Exp).then_inc(s_exp, 1)
                act.wait_ge(s_pre, 2)
                nc.scalar.activation(small_k[:, :], small_k[:, :], ACT.Exp).then_inc(s_exp, 1)
                for n, (s, c) in enumerate(pairs):
                    if c * 4 > s:
                        act.wait_ge(s_score, n + 1)
                        nc.scalar.activation(scores[:, s, c * HALF:(c + 1) * HALF], ps[:, n % 4, :], ACT.Copy).then_inc(s_cp, 1)

            @block.vector
            def _(dve):
                step = stepper(dve)
                step(nc.vector.memset(v[:, :, P:P + 1], 1.0), s_vec, wait=False)
                layer_norm(nc, dve, step, s_vec, stats, moments, x, normed, s_eps, s_root, s_norm)
                layer_norm(nc, dve, step, s_vec, stats, moments2, normed, normed2, s_eps2, s_root2, s_norm2)
                dve.wait_ge(s_load, 8 * 16)
                dve.wait_ge(s_turned, 2)
                step(nc.vector.tensor_scalar(xn[:, HALF:T], bank[:, HALF:T], biases[:, 4:5], biases[:, 5:6],
                                             ALU.mult, ALU.add), s_xn_v)
                dve.wait_ge(s_proj, 1)
                step(nc.vector.tensor_scalar(q[:, :], bank[:, T:2 * T], biases[:, 0:1], None, ALU.add), s_vec)
                step(nc.vector.tensor_scalar(small[:, :], q[:, :], 0.0, None, ALU.min), s_pre)
                dve.wait_ge(s_proj, 3)
                dve.wait_ge(s_gate, 1)
                step(nc.vector.scalar_tensor_tensor(k[:, :], bank[:, 3 * T:4 * T], biases[:, 1:2], gate[:, :],
                                                    ALU.add, ALU.mult), s_vec)
                step(nc.vector.tensor_scalar(small_k[:, :], k[:, :], 0.0, None, ALU.min), s_pre)
                dve.wait_ge(s_exp, 1)
                step(nc.vector.scalar_tensor_tensor(q[:, :], q[:, :], 0.0, small[:, :], ALU.max, ALU.add), s_qk)
                dve.wait_ge(s_exp, 2)
                step(nc.vector.scalar_tensor_tensor(k[:, :], k[:, :], 0.0, small_k[:, :], ALU.max, ALU.add), s_qk)
                dve.wait_ge(s_proj, 4)
                step(nc.vector.tensor_tensor(v[:, :, 0:P], bank[:, 0:T].rearrange("p (t c) -> p t c", c=P),
                                             v_bias[:, :].unsqueeze(1).to_broadcast([P, NT, P]), ALU.add), s_v)
                for n, (s, c) in enumerate(pairs):
                    if c * 4 > s:
                        continue
                    dve.wait_ge(s_score, n + 1)
                    d, e = s * P, (s + 1) * P
                    b = d - c * HALF
                    if e < (c + 1) * HALF:
                        step(nc.vector.tensor_copy(scores[:, s, e:(c + 1) * HALF], ps[:, n % 4, b + P:HALF]), s_vec, wait=False)
                    step(nc.vector.tensor_tensor(scores[:, s, d:e], ps[:, n % 4, b:b + P], tri[:, :], ALU.mult), s_sc)
                for t in range(NT):
                    dve.wait_ge(s_sum, t + 1)
                    sums = ps[:, 4 + t % 4, 0:P + 1]
                    step(nc.vector.tensor_scalar(den[:, t:t + 1], sums[:, P:P + 1], DEN_EPS, None, ALU.add), s_vec)
                    step(nc.vector.reciprocal(den[:, t:t + 1], den[:, t:t + 1]), s_vec)
                    step(nc.vector.scalar_tensor_tensor(x[:, t, :], sums[:, 0:P], den[:, t:t + 1], x[:, t, :],
                                                        ALU.mult, ALU.add), s_x2, wait=False)

            @block.tensor
            def _(pe):
                pe.wait_ge(s_load, 8 * 16)
                pe.wait_ge(s_norm2, NT)
                transpose_tiles(nc, pe, bank, normed2, ident, s_turned)
                pe.wait_ge(s_xn_a, 1)
                pe.wait_ge(s_xn_v, 1)
                for w, b in ((qkv_w[:, 0:P], 2), (gate_w[:, :], 4), (qkv_w[:, P:2 * P], 6)):
                    for c in range(2):
                        last = nc.tensor.matmul(ps[:, b + c, :], w, xn[:, c * HALF:(c + 1) * HALF], start=True, stop=True)
                    last.then_inc(s_proj, 1)
                for t in range(NT):
                    last = nc.tensor.matmul(bank[:, t * P:(t + 1) * P], xn[:, t * P:(t + 1) * P], qkv_w[:, 2 * P:3 * P],
                                            start=True, stop=True)
                last.then_inc(s_proj, 1)
                pe.wait_ge(s_qk, 2)
                pe.wait_ge(s_v, 1)
                diagonal = off = 0
                kept_by = []
                for s, c in pairs:
                    kept_by.append((diagonal, off))
                    diagonal, off = (diagonal, off + 1) if c * 4 > s else (diagonal + 1, off)
                kept_by.append((diagonal, off))
                for n, (s, c) in enumerate(pairs):
                    if n >= 4:
                        for semaphore, count in zip((s_sc, s_cp), kept_by[n - 3]):
                            if count:
                                pe.wait_ge(semaphore, count)
                    lo = max(s * P, c * HALF)
                    nc.tensor.matmul(ps[:, n % 4, lo - c * HALF:HALF], k[:, s * P:(s + 1) * P], q[:, lo:(c + 1) * HALF],
                                     start=True, stop=True).then_inc(s_score, 1)
                pe.wait_ge(s_sc, NT)
                pe.wait_ge(s_cp, len(pairs) - NT)
                for t in range(NT):
                    if t >= 4:
                        pe.wait_ge(s_x2, t - 3)
                    for s in range(t + 1):
                        last = nc.tensor.matmul(ps[:, 4 + t % 4, 0:P + 1], scores[:, s, t * P:(t + 1) * P], v[:, s, :],
                                                start=s == 0, stop=s == t)
                    last.then_inc(s_sum, 1)


def context_keys(nc, kept, ps, a, stack):
    m = Memory(nc, stack, "ctx")
    key_rows = m.sb("key_rows", [P, NG, NK * P], F32R)
    values = m.sb("values", [P, NK, H0, D0 + 1])
    key_bound = m.sb("key_bound", [P, H0])
    kept.update(key_rows=key_rows, values=values, key_bound=key_bound)
    with ExitStack() as own:
        m = Memory(nc, own, "ctxb")
        rope = m.sb("rope", [P, NK, 2, D0 // 2])
        mask_u8, mask, mask_bias, fresh = m.sb("mask_u8", [P, NK], U8), m.sb("mask", [P, NK]), m.sb("mask_bias", [P, NK], F32R), m.sb("fresh", [P, 1])
        w_kv, b_kv = m.sb("w_kv", [P, 2 * P]), m.sb("b_kv", [P, 2 * P])
        rows, turned = m.sb("rows", [P, U0, P]), m.sb("turned", [P, U0, P])
        kv = m.sb("kv", [P, U0, 2 * P])
        rotated = m.sb("rotated", [P, U0, P])
        part = [m.sb(f"part{n}", [P, U0, H0, D0 // 2]) for n in range(4)]
        squares, norms, best = m.sb("squares", [P, U0, P]), m.sb("norms", [P, U0, H0]), m.sb("best", [P, U0, H0])
        packed = m.sb("packed", [P, U0, NG * G0, ROW], F32R)
        s_load, s_rows = m.sem("loaded"), [m.sem(f"rows_loaded{n}") for n in range(U0)]
        s_turn, s_turned, s_kv, s_kv_kept, s_packed, s_keys, s_keys_kept = (m.sem(n) for n in (
            "rows_turned", "turned_kept", "kv_projected", "kv_kept", "packed", "keys_turned", "keys_kept"))
        s_vec, s_pool, s_rot, s_copied, s_mask, s_norm, s_all, s_bound = (m.sem(n) for n in (
            "vector_step", "pool_step", "rotated", "high_copied", "mask", "norms", "bound_of_all", "bound_root"))
        s_prod = m.sem("products")
        ctx = a["ctx_1024"][0]
        ident = kept["ident"]

        with nc.Block() as block:
            @block.sync
            def _(sp):
                mask_rows = a["mask_BxS2_bf1"][0]
                sp.dma_start(rope[:, :, :, :], a["rope_k"]).then_inc(s_load, 16)
                sp.dma_start(w_kv[:, :], a["L0_xattn_Wkv"]).then_inc(s_load, 16)
                sp.dma_start(b_kv[:, :], spread(a["L0_xattn_bkv"])).then_inc(s_load, 16)
                sp.dma_start(fresh[:, :], a["fresh"]).then_inc(s_load, 16)
                sp.dma_start(mask_u8[:, 0:NK - 1], mask_rows[0:(NK - 1) * P].rearrange("(t p) -> p t", p=P)).then_inc(s_load, 16)
                sp.dma_start(mask_u8[:, NK - 1:NK], columns(mask_rows[LAST:LC])).then_inc(s_load, 16)
                for t in range(NK):
                    if t >= U0:
                        sp.wait_ge(s_turn, t // U0)
                    first = min(t * P, LAST)
                    sp.dma_start(rows[:, t % U0, :], ctx[first:first + P, :]).then_inc(s_rows[t % U0], 16)
                sp.wait_ge(s_load, 6 * 16)

            @block.tensor
            def _(pe):
                def project(i):
                    for n in range(U0):
                        pe.wait_ge(s_rows[n], 16 * i + 16)
                        last = nc.tensor.transpose(ps[:, 0, n * P:(n + 1) * P], rows[:, n, :], ident[:, :])
                    last.then_inc(s_turn, 1)
                    pe.wait_ge(s_turned, i + 1)
                    for n in range(U0):
                        last = nc.tensor.matmul(ps[:, 1 + n, 0:2 * P], turned[:, n, :], w_kv[:, :], start=True, stop=True)
                    last.then_inc(s_kv, 1)

                def turn_keys(i):
                    for n in range(U0):
                        for g in range(NG):
                            last = nc.tensor.transpose(ps[:, 4 + n, g * P:(g + 1) * P],
                                                       packed[:, n, g * G0:(g + 1) * G0, :].bitcast(F32).rearrange("p h r -> p (h r)"),
                                                       ident[:, :])
                        last.then_inc(s_keys, 1)

                pe.wait_ge(s_load, 6 * 16)
                project(0)
                with pe.Fori(0, NI - 1) as i:
                    pe.wait_ge(s_kv_kept, i + 1)
                    project(i + 1)
                    pe.wait_ge(s_packed, i + 1)
                    turn_keys(i)
                pe.wait_ge(s_packed, NI)
                pe.wait_ge(s_keys_kept, (NI - 1) * U0)
                turn_keys(NI - 1)

            @block.scalar
            def _(act):
                def keep_turned(i):
                    act.wait_ge(s_turn, i + 1)
                    nc.scalar.activation(turned[:, :, :].rearrange("p n c -> p (n c)"), ps[:, 0, 0:U0 * P], ACT.Copy).then_inc(s_turned, 1)

                def keep_keys(i):
                    for n in range(U0):
                        act.wait_ge(s_keys, i * U0 + n + 2)
                        nc.scalar.activation(key_rows[:, :, bass.ds(i * (U0 * P) + n * P, P)],
                                             ps[:, 4 + n, :].rearrange("p (g c) -> p g c", g=NG), ACT.Copy).then_inc(s_keys_kept, 1)

                keep_turned(0)
                with act.Fori(0, NI - 1) as i:
                    keep_turned(i + 1)
                    keep_keys(i)
                keep_keys(NI - 1)
                act.wait_ge(s_all, 1)
                nc.scalar.activation(key_bound[:, :], key_bound[:, :], ACT.Sqrt).then_inc(s_bound, 1)

            @block.gpsimd
            def _(pool):
                with pool.Fori(0, NI) as i:
                    pool.wait_ge(s_kv_kept, i + 1)
                    even, odd = (kv[:, :, j:P:2].rearrange("p n (h d) -> p n h d", h=H0) for j in (0, 1))
                    cos, sin = (rope[:, bass.ds(i * U0, U0), j, :].unsqueeze(2).to_broadcast([P, U0, H0, D0 // 2]) for j in (0, 1))
                    nc.gpsimd.tensor_tensor(part[2][:, :, :, :], even, sin, ALU.mult).then_inc(s_pool, 1)
                    nc.gpsimd.tensor_tensor(part[3][:, :, :, :], odd, cos, ALU.mult).then_inc(s_pool, 1)
                    pool.wait_ge(s_pool, i * 2 + 2)
                    nc.gpsimd.tensor_tensor(rotated[:, :, 1:P:2].rearrange("p n (h d) -> p n h d", h=H0),
                                            part[2][:, :, :, :], part[3][:, :, :, :], ALU.add).then_inc(s_rot, 1)
                pool.wait_ge(s_norm, 1)
                nc.gpsimd.partition_all_reduce(key_bound[:, :], best[:, 0, :], P, bass.bass_isa.ReduceOp.max).then_inc(s_all, 1)

            @block.vector
            def _(dve):
                step = stepper(dve)
                step(nc.vector.memset(packed[:, :, :, :].bitcast(F32), 0.0), s_keys)
                step(nc.vector.memset(packed[:, :, :, 3 * D0:3 * D0 + 2].bitcast(F32), 1.0), s_mask)
                step(nc.vector.memset(best[:, :, :], 0.0), s_mask)
                dve.wait_ge(s_load, 6 * 16)
                step(nc.vector.tensor_copy(mask[:, :], mask_u8[:, :]), s_mask)
                step(nc.vector.tensor_scalar(mask[:, NK - 1:NK], mask[:, NK - 1:NK], fresh[:, 0:1], None, ALU.mult), s_mask)
                step(nc.vector.tensor_scalar(mask_bias[:, :], mask[:, :], -MASKED, MASKED, ALU.mult, ALU.add), s_mask)
                with dve.Fori(0, NI) as i:
                    tiles = bass.ds(i * U0, U0)
                    dve.wait_ge(s_kv, i + 1)
                    nc.vector.tensor_tensor(kv[:, :, :], ps[:, 1:1 + U0, 0:2 * P], b_kv[:, :].unsqueeze(1).to_broadcast([P, U0, 2 * P]),
                                            ALU.add).then_inc(s_kv_kept, 1)
                    dve.wait_ge(s_kv_kept, i + 1)
                    even, odd = (kv[:, :, j:P:2].rearrange("p n (h d) -> p n h d", h=H0) for j in (0, 1))
                    cos, sin = (rope[:, tiles, j, :].unsqueeze(2).to_broadcast([P, U0, H0, D0 // 2]) for j in (0, 1))
                    nc.vector.tensor_tensor(part[0][:, :, :, :], even, cos, ALU.mult).then_inc(s_prod, 1)
                    nc.vector.tensor_tensor(part[1][:, :, :, :], odd, sin, ALU.mult).then_inc(s_prod, 1)
                    dve.wait_ge(s_prod, i * 2 + 2)
                    nc.vector.tensor_tensor(rotated[:, :, 0:P:2].rearrange("p n (h d) -> p n h d", h=H0),
                                            part[0][:, :, :, :], part[1][:, :, :, :], ALU.subtract).then_inc(s_vec, 1)
                    weight = mask[:, tiles].unsqueeze(2).to_broadcast([P, U0, P]).rearrange("p n (h d) -> p n h d", h=H0)
                    nc.vector.tensor_tensor(values[:, tiles, :, 0:D0], kv[:, :, P:2 * P].rearrange("p n (h d) -> p n h d", h=H0),
                                            weight, ALU.mult).then_inc(s_vec, 1)
                    nc.vector.tensor_copy(values[:, tiles, :, D0], mask[:, tiles].unsqueeze(2).to_broadcast([P, U0, H0])).then_inc(s_vec, 1)
                    dve.wait_ge(s_vec, i * 9 + 3)
                    dve.wait_ge(s_rot, i + 1)
                    heads = rotated[:, :, :].rearrange("p n (h d) -> p (n h) d", h=H0)
                    rows_of = packed[:, :, :, :].rearrange("p n h r -> p (n h) r")

                    dve.wait_ge(s_keys, i * U0 + 1)
                    nc.vector.tensor_copy(rows_of[:, :, 0:D0], heads).then_inc(s_vec, 1)
                    dve.wait_ge(s_vec, i * 9 + 4)
                    nc.vector.tensor_copy(rows_of[:, :, D0:2 * D0], heads).then_inc(s_vec, 1)
                    nc.vector.tensor_tensor(rows_of[:, :, 2 * D0:3 * D0], heads, rows_of[:, :, 0:D0].bitcast(F32), ALU.subtract).then_inc(s_vec, 1)
                    nc.vector.tensor_copy(packed[:, :, :, 3 * D0 + 2], mask_bias[:, tiles].bitcast(F32).unsqueeze(2).to_broadcast([P, U0, H0])).then_inc(s_packed, 1)
                    nc.vector.tensor_tensor(squares[:, :, :], rotated[:, :, :], rotated[:, :, :], ALU.mult).then_inc(s_vec, 1)
                    dve.wait_ge(s_vec, i * 9 + 7)
                    nc.vector.tensor_reduce(norms[:, :, :], squares[:, :, :].rearrange("p n (h d) -> p n h d", h=H0), AX.X, ALU.add).then_inc(s_vec, 1)
                    dve.wait_ge(s_vec, i * 9 + 8)
                    nc.vector.tensor_tensor(best[:, :, :], best[:, :, :], norms[:, :, :], ALU.max).then_inc(s_vec, 1)
                    dve.wait_ge(s_vec, i * 9 + 9)
                nc.vector.tensor_tensor(best[:, 0, :], best[:, 0, :], best[:, 1, :], ALU.max).then_inc(s_vec, 1)
                dve.wait_ge(s_vec, NI * 9 + 1)
                nc.vector.tensor_tensor(best[:, 0, :], best[:, 0, :], best[:, 2, :], ALU.max).then_inc(s_norm, 1)


def cross_attention(nc, kept, ps, a):
    with ExitStack() as stack:
        context_keys(nc, kept, ps, a, stack)
        key_rows, values, key_bound, x, ident = (kept[n] for n in ("key_rows", "values", "key_bound", "x", "ident"))
        m = Memory(nc, stack, "att")
        scaled = m.sb("scaled", [P, NT, P])
        guard = m.sb("guard", [P, NT, H0])
        attended = scaled
        flag = m.sb("flag", [P, 2])
        with ExitStack() as own:
            m = Memory(nc, own, "qry")
            w_q, b_q, rope = m.sb("w_q", [P, P]), m.sb("b_q", [P, P]), m.sb("rope", [P, NT, 2, D0 // 2])
            stats, moments, normed, xn = m.sb("stats", [P, NT, 6]), m.sb("moments", [P, NT, 2]), m.sb("normed", [P, NT, P]), m.sb("xn", [P, T])
            q, squares = m.sb("q", [P, NT, P]), m.sb("squares", [P, NT, P])
            part = [m.sb(f"part{n}", [P, NT, H0, D0 // 2]) for n in range(4)]
            s_load, s_vec, s_eps, s_root, s_norm, s_turned, s_xn_a, s_xn_v, s_proj, s_sq, s_len, s_top, s_all = (m.sem(n) for n in (
                "loaded", "vector_step", "variance", "root", "normed", "turned", "xn_scalar", "xn_vector", "projected", "squares", "lengths", "top", "top_of_all"))
            bank = ps[:, :, :].rearrange("p b c -> p (b c)")
            with nc.Block() as block:
                @block.sync
                def _(sp):
                    sp.dma_start(w_q[:, :], a["L0_xattn_Wq"]).then_inc(s_load, 16)
                    sp.dma_start(b_q[:, :], spread(a["L0_xattn_bq"])).then_inc(s_load, 16)
                    sp.dma_start(rope[:, :, :, :], a["rope_q"]).then_inc(s_load, 16)
                    sp.wait_ge(s_load, 3 * 16)

                @block.scalar
                def _(act):
                    root(nc, act, moments, s_eps, s_root)
                    act.wait_ge(s_turned, 1)
                    nc.scalar.activation(xn[:, 0:HALF], bank[:, 0:HALF], ACT.Copy).then_inc(s_xn_a, 1)
                    act.wait_ge(s_sq, 1)
                    nc.scalar.activation(guard[:, :, :], guard[:, :, :], ACT.Sqrt).then_inc(s_len, 1)

                @block.tensor
                def _(pe):
                    pe.wait_ge(s_norm, NT)
                    transpose_tiles(nc, pe, bank, normed, ident, s_turned)
                    pe.wait_ge(s_load, 3 * 16)
                    pe.wait_ge(s_xn_a, 1)
                    pe.wait_ge(s_xn_v, 1)
                    for t in range(NT):
                        last = nc.tensor.matmul(bank[:, T + t * P:T + (t + 1) * P], xn[:, t * P:(t + 1) * P], w_q[:, :], start=True, stop=True)
                    last.then_inc(s_proj, 1)

                @block.vector
                def _(dve):
                    step = stepper(dve)
                    layer_norm(nc, dve, step, s_vec, stats, moments, x, normed, s_eps, s_root, s_norm)
                    dve.wait_ge(s_turned, 2)
                    step(nc.vector.tensor_copy(xn[:, HALF:T], bank[:, HALF:T]), s_xn_v)
                    dve.wait_ge(s_load, 3 * 16)
                    dve.wait_ge(s_proj, 1)
                    step(nc.vector.tensor_tensor(q[:, :, :], bank[:, T:2 * T].rearrange("p (t c) -> p t c", c=P),
                                                 b_q[:, :].unsqueeze(1).to_broadcast([P, NT, P]), ALU.add), s_vec)
                    even, odd = (q[:, :, j:P:2].rearrange("p n (h d) -> p n h d", h=H0) for j in (0, 1))
                    cos, sin = (rope[:, :, j, :].unsqueeze(2).to_broadcast([P, NT, H0, D0 // 2]) for j in (0, 1))
                    for n, (u, w) in enumerate(((even, cos), (odd, sin), (even, sin), (odd, cos))):
                        step(nc.vector.tensor_tensor(part[n][:, :, :, :], u, w, ALU.mult), s_vec, wait=n == 3)
                    for n, op in ((0, ALU.subtract), (1, ALU.add)):
                        step(nc.vector.tensor_tensor(q[:, :, n:P:2].rearrange("p n (h d) -> p n h d", h=H0),
                                                     part[2 * n][:, :, :, :], part[2 * n + 1][:, :, :, :], op), s_vec)
                    step(nc.vector.tensor_scalar(scaled[:, :, :], q[:, :, :], D0 ** -1.0, None, ALU.mult), s_vec)
                    step(nc.vector.tensor_tensor(squares[:, :, :], scaled[:, :, :], scaled[:, :, :], ALU.mult), s_vec)
                    step(nc.vector.tensor_reduce(guard[:, :, :], squares[:, :, :].rearrange("p n (h d) -> p n h d", h=H0), AX.X, ALU.add), s_sq)
                    dve.wait_ge(s_len, 1)
                    step(nc.vector.tensor_tensor(guard[:, :, :], guard[:, :, :], key_bound[:, :].unsqueeze(1).to_broadcast([P, NT, H0]), ALU.mult), s_vec)
                    step(nc.vector.tensor_reduce(flag[:, 0:1], guard[:, :, :], AX.XY, ALU.max), s_top)

                @block.gpsimd
                def _(pool):
                    pool.wait_ge(s_top, 1)
                    nc.gpsimd.partition_all_reduce(flag[:, 1:2], flag[:, 0:1], P, bass.bass_isa.ReduceOp.max).then_inc(s_all, 1)

        attend(nc, kept, ps, a, scaled, guard, attended, flag)

        with ExitStack() as own:
            m = Memory(nc, own, "prj")
            turned, w_out, b_out = m.sb("turned", [P, T]), m.sb("w_out", [P, P]), m.sb("b_out", [P, P])
            s_load = m.sem("loaded")
            s_turned, s_a, s_v, s_proj, s_vec = (m.sem(n) for n in ("turned", "kept_scalar", "kept_vector", "projected", "vector_step"))
            bank = ps[:, :, :].rearrange("p b c -> p (b c)")
            with nc.Block() as block:
                @block.sync
                def _(sp):
                    sp.dma_start(w_out[:, :], a["L0_xattn_Wo"]).then_inc(s_load, 16)
                    sp.dma_start(b_out[:, :], spread(a["L0_xattn_bo"])).then_inc(s_load, 16)
                    sp.wait_ge(s_load, 2 * 16)

                @block.tensor
                def _(pe):
                    transpose_tiles(nc, pe, bank, attended, ident, s_turned)
                    pe.wait_ge(s_load, 2 * 16)
                    pe.wait_ge(s_a, 1)
                    pe.wait_ge(s_v, 1)
                    for t in range(NT):
                        last = nc.tensor.matmul(bank[:, T + t * P:T + (t + 1) * P], turned[:, t * P:(t + 1) * P], w_out[:, :], start=True, stop=True)
                    last.then_inc(s_proj, 1)

                @block.scalar
                def _(act):
                    act.wait_ge(s_turned, 1)
                    nc.scalar.activation(turned[:, 0:HALF], bank[:, 0:HALF], ACT.Copy).then_inc(s_a, 1)

                @block.vector
                def _(dve):
                    step = stepper(dve)
                    dve.wait_ge(s_load, 2 * 16)
                    step(nc.vector.tensor_tensor(x[:, :, :], x[:, :, :], b_out[:, :].unsqueeze(1).to_broadcast([P, NT, P]), ALU.add), s_vec)
                    dve.wait_ge(s_turned, 2)
                    step(nc.vector.tensor_copy(turned[:, HALF:T], bank[:, HALF:T]), s_v)
                    dve.wait_ge(s_proj, 1)
                    step(nc.vector.tensor_tensor(x[:, :, :], bank[:, T:2 * T].rearrange("p (t c) -> p t c", c=P), x[:, :, :], ALU.add), s_vec)


def attend(nc, kept, ps, a, scaled, guard, attended, flag):
    key_rows, values, ident = kept["key_rows"], kept["values"], kept["ident"]
    NP = U0 * G0
    BODY = U0 * G0
    SG = NK * G0
    AHEAD = 7
    with ExitStack() as own:
        m = Memory(nc, own, "loop")
        head_rows = m.sb("head_rows", [P, G0])
        query_rows = m.sb("query_rows", [P, NG, T], F32R)
        key_tile = [m.sb(f"key_tile{n}", [P, G0, P], F32R) for n in range(U0)]
        value_tile = [m.sb(f"value_tile{n}", [P, G0, ROW]) for n in range(U0)]
        exps = [scaled[:, :, :].rearrange("p t c -> p (t c)")] + [m.sb(f"exps{n}", [P, T])[:, :] for n in range(1, NP)]
        packed = exps[NP - 1].rearrange("p (t h r) -> p t h r", h=G0, r=ROW).bitcast(F32R)
        sums = [values[:, 0:T // ROW, g * G0:(g + 1) * G0, 0:D0] for g in range(NG)]
        inverse = m.sb("inverse", [P, NT, G0])
        zero = m.sb("zero", [P, 1])
        row_max, chunk_max, new_guard = m.sb("row_max", [P, NT, G0]), m.sb("chunk_max", [P, NT, G0]), m.sb("new_guard", [P, NT, G0])
        s_load, s_set, s_constant, s_high, s_packed, s_turned, s_queries = (m.sem(n) for n in (
            "loaded", "set", "constant_rows", "high", "packed", "queries_turned", "queries"))
        s_key, s_value, s_score, s_exp, s_weighted, s_open = (m.sem(n) for n in ("key_tile", "value_tile", "scores", "exps", "weighted", "opened"))
        s_closed, s_sums, s_straight, s_back, s_inv, s_norm = (m.sem(n) for n in ("closed", "sums", "sums_straight", "sums_turned", "inverse", "normalised"))
        x_alone, x_scores, x_max, x_pack, x_packed, x_turned, x_step = (m.sem(n) for n in (
            "exact_alone", "exact_scores", "exact_max", "exact_high", "exact_packed", "exact_turned", "exact_step"))
        CHUNK = U0 * P
        two_banks = ps[:, 0:2, :].rearrange("p b c -> p (b c)")

        def turn_queries(semaphore):
            for t in range(NT):
                last = nc.tensor.transpose(ps[:, t // 4, (t % 4) * P:(t % 4 + 1) * P],
                                           packed[:, t, :, :].bitcast(F32).rearrange("p h r -> p (h r)"), ident[:, :])
            last.then_inc(semaphore, 1)

        with nc.Block() as block:
            @block.sync
            def _(sp):
                sp.dma_start(head_rows[:, :], a["head_rows"]).then_inc(s_load, 16)
                sp.wait_ge(s_load, 16)

            @block.tensor
            def _(pe):
                def scores(g, i, c):
                    if not (isinstance(g, int) and g == 0 and isinstance(i, int) and i == 0 and c < 3):
                        pe.wait_ge(s_exp, g * SG + i * BODY + (c - 2))
                    if c % G0 == 0:
                        pe.wait_ge(s_key, g * NK + i * U0 + (c // G0 + 1))
                    for b in range(2):
                        last = nc.tensor.matmul(ps[:, 2 * (c % 3) + b, :], key_tile[c // G0 % U0][:, c % G0, :],
                                                query_rows[:, g, b * HALF:(b + 1) * HALF], start=True, stop=True)
                    last.then_inc(s_score, 1)

                def weigh(g, i, n, b):
                    if b == 0:
                        pe.wait_ge(s_value, g * NK + i * U0 + (n + 1))
                        pe.wait_ge(s_exp, g * SG + i * BODY + G0 * (n + 1))
                    for h in range(G0):
                        last = nc.tensor.matmul(ps[h * ROW:(h + 1) * ROW, 6 + b, :], value_tile[n][:, h, :],
                                                exps[n * G0 + h][:, b * HALF:(b + 1) * HALF], start=False, stop=False,
                                                skip_group_check=True)
                    if b:
                        last.then_inc(s_weighted, 1)

                def zeros(b, opening):
                    return nc.tensor.matmul(ps[:, 6 + b, :], ident[:, :], zero[:, :].to_broadcast([P, HALF]), start=opening, stop=not opening,
                                            skip_group_check=True)

                def body(g, i, last_of_group=False, last=False):
                    for n in range(U0):
                        for b in range(2):
                            weigh(g, i, n, b)
                            if last_of_group and n == U0 - 1 and b:
                                for bank in range(2):
                                    closed = zeros(bank, False)
                                closed.then_inc(s_closed, 1)
                            for step in range(n * G0 + AHEAD + 2 * b, n * G0 + AHEAD + 2 * b + 2):
                                if step < BODY:
                                    scores(g, i, step)
                                elif not last_of_group:
                                    scores(g, i + 1, step - BODY)
                                elif not last:
                                    scores(g + 1, 0, step - BODY)

                def open_sums():
                    for bank in range(2):
                        opened = zeros(bank, True)
                    opened.then_inc(s_open, 1)

                def group(g, last=False):
                    with pe.Fori(0, NI - 1) as i:
                        body(g, i)
                    body(g, NI - 1, last_of_group=True, last=last)

                pe.wait_ge(s_load, 16)
                bits = nc.tensor.value_load(flag[0:1, 1:2].bitcast(I32))
                pe.wait_ge(s_set, 4)
                with pe.Fori(0, NG) as g:
                    pe.wait_ge(s_packed, g * 3 + 3)
                    turn_queries(s_turned)
                    with pe.If(bits > SAFE_BITS):
                        with pe.Fori(0, NI) as i:
                            for n in range(NT * G0):
                                if n % G0 == 0:
                                    pe.wait_ge(x_alone, (g * NI + i) * NT + (n // G0 + 1))
                                if n >= 6:
                                    pe.wait_ge(x_max, (g * NI + i) * (NT * G0) + (n - 5))
                                nc.tensor.matmul(ps[:, n % 6, 0:CHUNK], key_tile[n // G0 % 2][:, n % G0, :],
                                                 key_rows[:, g, bass.ds(i * CHUNK, CHUNK)], start=True, stop=True).then_inc(x_scores, 1)
                            pe.wait_ge(x_max, (g * NI + i + 1) * (NT * G0))
                        pe.wait_ge(x_packed, g + 1)
                        turn_queries(x_turned)
                for c in range(AHEAD):
                    scores(0, 0, c)
                open_sums()
                with pe.Fori(0, NG - 1) as g:
                    group(g)
                    pe.wait_ge(s_sums, g + 1)
                    open_sums()
                group(NG - 1, last=True)
                for g in range(NG):
                    pe.wait_ge(s_straight, g + 1)
                    for t in range(NT):
                        last = nc.tensor.transpose(ps[:, 2 * g + t // 4, (t % 4) * P:(t % 4 + 1) * P],
                                                   exps[1 + g][:, t * P:(t + 1) * P], ident[:, :])
                    last.then_inc(s_back, 1)

            @block.scalar
            def _(act):
                def body(g, i, first=False):
                    for c in range(BODY):
                        act.wait_ge(s_score, g * SG + i * BODY + (c + 1))
                        if c % G0 == 0 and not first:
                            act.wait_ge(s_weighted, g * NK + i * U0 + (c // G0 - 2))
                        nc.scalar.activation(exps[c], ps[:, 2 * (c % 3):2 * (c % 3) + 2, :].rearrange("p b c -> p (b c)"),
                                             ACT.Exp).then_inc(s_exp, 1)

                body(0, 0, first=True)
                with act.Fori(1, NI) as i:
                    body(0, i)
                with act.Fori(1, NG) as g:
                    with act.Fori(0, NI) as i:
                        body(g, i)
                act.wait_ge(s_weighted, NG * NK)
                for g in range(NG):
                    act.wait_ge(s_sums, g + 1)
                    nc.scalar.activation(exps[1 + g].rearrange("p (n h d) -> p n h d", h=G0, d=D0), sums[g], ACT.Copy).then_inc(s_straight, 1)

            @block.vector
            def _(dve):
                step = stepper(dve)
                for tile in value_tile:
                    step(nc.vector.memset(tile[:, :, :], 0.0), s_set, wait=False)
                step(nc.vector.memset(zero[:, :], 0.0), s_set)
                step(nc.vector.memset(packed[:, :, :, 3 * D0 + 3:ROW].bitcast(F32), 0.0), s_constant)
                step(nc.vector.memset(packed[:, :, :, 3 * D0 + 2:3 * D0 + 3].bitcast(F32), 1.0), s_constant)
                dve.wait_ge(s_load, 16)
                bits = nc.vector.value_load(flag[0:1, 1:2].bitcast(I32))

                with dve.Fori(0, NG) as g:
                    heads = scaled[:, :, bass.ds(g * ROW, ROW)].rearrange("p t (h d) -> p t h d", h=G0)
                    guards = guard[:, :, bass.ds(g * G0, G0)]
                    high = packed[:, :, :, 0:D0]
                    nc.vector.tensor_copy(high, heads).then_inc(s_high, 1)
                    nc.vector.tensor_scalar(packed[:, :, :, 3 * D0], guards, -1.0, None, ALU.mult).then_inc(s_high, 1)
                    nc.vector.tensor_copy(packed[:, :, :, 2 * D0:3 * D0], heads).then_inc(s_packed, 1)
                    dve.wait_ge(s_high, g * 2 + 2)
                    nc.vector.tensor_tensor(packed[:, :, :, D0:2 * D0], heads, high.bitcast(F32), ALU.subtract).then_inc(s_packed, 1)
                    nc.vector.scalar_tensor_tensor(packed[:, :, :, 3 * D0 + 1], guards, -1.0, packed[:, :, :, 3 * D0].bitcast(F32),
                                                   ALU.mult, ALU.subtract).then_inc(s_packed, 1)
                    dve.wait_ge(s_turned, g + 1)
                    nc.vector.tensor_scalar(query_rows[:, g, :], two_banks, 1.0, None, ALU.mult).then_inc(s_queries, 1)
                    with dve.If(bits > SAFE_BITS):
                        dve.wait_ge(s_queries, g + 1)

                        def stage_queries(t):
                            nc.vector.tensor_tensor(key_tile[t % 2][:, :, :],
                                                    query_rows[:, g, t * P:(t + 1) * P].bitcast(F32).unsqueeze(1).to_broadcast([P, G0, P]),
                                                    head_rows[:, :].unsqueeze(2).to_broadcast([P, G0, P]), ALU.mult).then_inc(x_alone, 1)

                        nc.vector.memset(row_max[:, :, :], MASKED).then_inc(x_step, 1)
                        with dve.Fori(0, NI) as i:
                            stage_queries(0)
                            for n in range(NT * G0):
                                if n % G0 == 0 and n // G0 + 1 < NT:
                                    stage_queries(n // G0 + 1)
                                dve.wait_ge(x_scores, (g * NI + i) * (NT * G0) + (n + 1))
                                nc.vector.tensor_reduce(chunk_max[:, n // G0, n % G0:n % G0 + 1], ps[:, n % 6, 0:CHUNK], AX.X, ALU.max).then_inc(x_max, 1)
                            dve.wait_ge(x_max, (g * NI + i + 1) * (NT * G0))
                            dve.wait_ge(x_step, g * (NI + 3) + i + 1)
                            nc.vector.tensor_tensor(row_max[:, :, :], row_max[:, :, :], chunk_max[:, :, :], ALU.max).then_inc(x_step, 1)
                            dve.wait_ge(x_step, g * (NI + 3) + i + 2)
                        nc.vector.tensor_tensor(new_guard[:, :, :], row_max[:, :, :], guards, ALU.add).then_inc(x_step, 1)
                        dve.wait_ge(x_step, g * (NI + 3) + NI + 2)
                        nc.vector.tensor_scalar(packed[:, :, :, 3 * D0], new_guard[:, :, :], -1.0, None, ALU.mult).then_inc(x_pack, 1)
                        dve.wait_ge(x_pack, g + 1)
                        nc.vector.scalar_tensor_tensor(packed[:, :, :, 3 * D0 + 1], new_guard[:, :, :], -1.0, packed[:, :, :, 3 * D0].bitcast(F32),
                                                       ALU.mult, ALU.subtract).then_inc(x_packed, 1)
                        dve.wait_ge(x_turned, g + 1)
                        nc.vector.tensor_scalar(query_rows[:, g, :], two_banks, 1.0, None, ALU.mult).then_inc(x_step, 1)

                dve.wait_ge(s_queries, NG)

                def stage_keys(g, i, n):
                    nc.vector.tensor_tensor(key_tile[n][:, :, :], key_rows[:, g, bass.ds(i * CHUNK + n * P, P)].bitcast(F32).unsqueeze(1).to_broadcast([P, G0, P]),
                                            head_rows[:, :].unsqueeze(2).to_broadcast([P, G0, P]), ALU.mult).then_inc(s_key, 1)

                def stage_values(g, i, n):
                    nc.vector.tensor_scalar(value_tile[n][:, :, 0:D0 + 1], values[:, i * U0 + n, bass.ds(g * G0, G0), :], 1.0, None, ALU.mult).then_inc(s_value, 1)

                def body(g, i, last_of_group=False):
                    following = (g + 1, 0) if last_of_group else (g, i + 1)
                    for n in range(U0):
                        dve.wait_ge(s_score, g * SG + i * BODY + G0 * (n + 1))
                        stage_keys(*following, n)
                        dve.wait_ge(s_weighted, g * NK + i * U0 + (n + 1))
                        stage_values(*following, n)

                def keep_sums(g):
                    dve.wait_ge(s_closed, g + 1)
                    for h in range(G0):
                        kept_sums = nc.vector.tensor_scalar(values[:, 0:T // ROW, bass.ds(g * G0 + h, 1), 0:D0].rearrange("p n a d -> p n (a d)"),
                                                            ps[:, 6:8, :].rearrange("p b (n h d) -> p (b n) h d", h=G0, d=D0)[:, :, h, :],
                                                            1.0, None, ALU.mult)
                    kept_sums.then_inc(s_sums, 1)

                for n in range(U0):
                    stage_keys(0, 0, n)
                    stage_values(0, 0, n)
                with dve.Fori(0, NG - 1) as g:
                    with dve.Fori(0, NI - 1) as i:
                        body(g, i)
                    body(g, NI - 1, last_of_group=True)
                    keep_sums(g)
                with dve.Fori(0, NI - 1) as i:
                    body(NG - 1, i)
                keep_sums(NG - 1)
                for g in range(NG):
                    dve.wait_ge(s_back, g + 1)
                    back = ps[:, 2 * g:2 * g + 2, :].rearrange("p b (t h r) -> p (b t) h r", h=G0, r=ROW)
                    if g:
                        dve.wait_ge(s_norm, g)
                    nc.vector.reciprocal(inverse[:, :, :], back[:, :, :, D0]).then_inc(s_inv, 1)
                    dve.wait_ge(s_inv, g + 1)
                    nc.vector.tensor_tensor(attended[:, :, g * ROW:(g + 1) * ROW].rearrange("p t (h d) -> p t h d", h=G0), back[:, :, :, 0:D0],
                                            inverse[:, :, :].unsqueeze(3).to_broadcast([P, NT, G0, D0]), ALU.mult).then_inc(s_norm, 1)


def route_top2(nc, dve, step, s_vec, s_exp_in, s_exp_out, m, logits, order, weights):
    E = order.shape[1]
    peak, prob, total = m["peak"], m["prob"], m["total"]
    larger, equal, rank = m["larger"], m["equal"], m["rank"]
    step(nc.vector.tensor_reduce(peak[:, :], logits, AX.X, ALU.max), s_vec)
    step(nc.vector.tensor_tensor(prob[:, :, :], logits, peak[:, :].unsqueeze(2).to_broadcast([P, NT, E]), ALU.subtract), s_exp_in)
    dve.wait_ge(s_exp_out, 1)
    step(nc.vector.tensor_reduce(total[:, :], prob[:, :, :], AX.X, ALU.add), s_vec)
    step(nc.vector.reciprocal(total[:, :], total[:, :]), s_vec)
    step(nc.vector.tensor_tensor(prob[:, :, :], prob[:, :, :], total[:, :].unsqueeze(2).to_broadcast([P, NT, E]), ALU.mult), s_vec)
    select(nc, step, s_vec, prob, order, larger, equal, rank, 2)
    step(nc.vector.tensor_tensor(weights[:, :, :], prob[:, :, :], rank[:, :, :], ALU.mult), s_vec)
    step(nc.vector.tensor_reduce(total[:, :], weights[:, :, :], AX.X, ALU.add), s_vec)
    step(nc.vector.reciprocal(total[:, :], total[:, :]), s_vec)
    step(nc.vector.tensor_tensor(weights[:, :, :], weights[:, :, :], total[:, :].unsqueeze(2).to_broadcast([P, NT, E]), ALU.mult), s_vec)


def select(nc, step, s_vec, values, order, larger, equal, rank, top):
    E = order.shape[1]
    for t in range(NT):
        other = values[:, t, :].unsqueeze(1).to_broadcast([P, E, E])
        mine = values[:, t, :].unsqueeze(2).to_broadcast([P, E, E])
        step(nc.vector.tensor_tensor(larger[:, t, :, :], other, mine, ALU.is_gt), s_vec, wait=False)
        step(nc.vector.tensor_tensor(equal[:, t, :, :], other, mine, ALU.is_equal), s_vec, wait=t == NT - 1)
    step(nc.vector.tensor_tensor(equal[:, :, :, :].rearrange("p t e f -> p t (e f)"), equal[:, :, :, :].rearrange("p t e f -> p t (e f)"),
                                 order[:, :, :].rearrange("p e f -> p (e f)").unsqueeze(1).to_broadcast([P, NT, E * E]), ALU.mult), s_vec)
    step(nc.vector.tensor_tensor(larger[:, :, :, :], larger[:, :, :, :], equal[:, :, :, :], ALU.add), s_vec)
    step(nc.vector.tensor_reduce(rank[:, :, :], larger[:, :, :, :], AX.X, ALU.add), s_vec)
    step(nc.vector.tensor_scalar(rank[:, :, :], rank[:, :, :], float(top), None, ALU.is_lt), s_vec)


def mixture(nc, kept, ps, a, layer):
    E = 32 if layer else 8
    HID = 64 if layer else 176
    ROUTED = E * HID // P
    SHARED = 1 if layer else 3
    NH = ROUTED + SHARED
    rows_of = [P] * NH
    if not layer:
        rows_of[-1] = 2 * HID - 2 * P
    x, ident = kept["x"], kept["ident"]
    bank = ps[:, :, :].rearrange("p b c -> p (b c)")
    with ExitStack() as stack:
        m = Memory(nc, stack, f"mix{layer}")
        w_gate, w_up, w_down = (m.sb(n, [P, NH, P]) for n in ("w_gate", "w_up", "w_down"))
        xn = m.sb("xn", [P, T])
        picks = m.sb("picks", [P, ROUTED, P], F32R)
        route_rows = m.sb("route_rows", [P, T], F32R)
        with ExitStack() as own:
            b = Memory(nc, own, f"mixb{layer}")
            picks_in = b.sb("picks_in", [P, ROUTED, P])
            router, order = b.sb("router", [P, E]), b.sb("order", [P, 8 if not layer else 4, 8 if not layer else 4])
            raw = b.sb("raw", [P, 3, ROUTED + SHARED, P]) if layer else None
            router_raw, router_bias = (b.sb("router_raw", [E, P]), b.sb("router_bias", [P, E])) if layer else (None, None)
            stats, moments, normed = b.sb("stats", [P, NT, 6]), b.sb("moments", [P, NT, 2]), b.sb("normed", [P, NT, P])
            packed = b.sb("packed", [P, NT, P], F32R)
            weights = b.sb("weights", [P, NT, E])
            R = order.shape[1]
            scratch = {n: b.sb(n, s) for n, s in {"peak": [P, NT], "total": [P, NT], "prob": [P, NT, E], "larger": [P, NT, R, R],
                                                  "equal": [P, NT, R, R], "rank": [P, NT, R], "choice": [P, NT, E], "best": [P, NT, 4, 8],
                                                  "top": [P, NT, 8], "left": [P, NT, E], "groups": [P, NT, 4]}.items()}
            s_load, s_late, s_vec, s_eps, s_root, s_norm, s_turned, s_xn_a, s_xn_v, s_logit, s_exp_in, s_exp_out = (b.sem(n) for n in (
                "loaded", "weights_loaded", "vector_step", "variance", "root", "normed", "turned", "xn_scalar", "xn_vector", "logits", "exp_input", "exps"))
            s_packed, s_routes, s_kept, s_w_turned, s_w_kept, s_router = (b.sem(n) for n in (
                "packed", "routes_turned", "routes_kept", "weights_turned", "weights_kept", "router_kept"))

            with nc.Block() as block:
                @block.sync
                def _(sp):
                    if layer:
                        loads = [(router_raw[:, :], a["L1_ffn_gate_w"]), (router_bias[:, :], spread(a["L1_ffn_gate_bias"])),
                                 (order[:, :, :], a["order4"])]
                        late = [(raw[:, 0, 0:ROUTED, :], a["L1_ffn_expert_gate"].rearrange("e i h -> (e i) h").rearrange("(n p) h -> p n h", p=P)),
                                (raw[:, 1, 0:ROUTED, :], a["L1_ffn_expert_up"].rearrange("e i h -> (e i) h").rearrange("(n p) h -> p n h", p=P)),
                                (raw[:, 2, 0:ROUTED, :].rearrange("p n (e i) -> p (n e) i", e=2), a["L1_ffn_expert_down"].rearrange("e h i -> h e i")),
                                (raw[:, 0, ROUTED, :], a["L1_ffn_shared_gate"]), (raw[:, 1, ROUTED, :], a["L1_ffn_shared_up"]),
                                (raw[:, 2, ROUTED, :], a["L1_ffn_shared_down"])]
                    else:
                        loads = [(router[:, :], a["L0_ffn_gate_w"]), (order[:, :, :], a["order8"])]
                        late = []
                        for w, name in ((w_gate, "gate"), (w_up, "up")):
                            flat = w[:, :, :].rearrange("p n c -> p (n c)")
                            late.append((flat[:, 0:E * HID].rearrange("p (e f) -> p e f", e=E), a[f"L0_ffn_exp_{name}"].rearrange("e d f -> d e f")))
                            late.append((flat[:, E * HID:(E + 2) * HID].rearrange("p (e f) -> p e f", e=2), a[f"L0_ffn_sh_{name}"].rearrange("e d f -> d e f")))
                        late.append((w_down[:, 0:ROUTED, :], a["L0_ffn_exp_down"].rearrange("e f d -> (e f) d").rearrange("(n p) d -> p n d", p=P)))
                        shared = a["L0_ffn_sh_down"].rearrange("e f d -> (e f) d")
                        late.append((w_down[:, ROUTED:ROUTED + 2, :], shared[0:2 * P, :].rearrange("(n p) d -> p n d", p=P)))
                        late.append((w_down[0:rows_of[-1], NH - 1, :], shared[2 * P:2 * HID, :]))
                    late.append((picks_in[:, :, :], a[f"picks{layer}"]))
                    for dst, src in loads:
                        sp.dma_start(dst, src).then_inc(s_load, 16)
                    for dst, src in late:
                        sp.dma_start(dst, src).then_inc(s_late, 16)
                    sp.wait_ge(s_load, len(loads) * 16)
                    sp.wait_ge(s_late, len(late) * 16)

                n_loads, n_late = (3, 7) if layer else (2, 8)

                @block.tensor
                def _(pe):
                    pe.wait_ge(s_load, n_loads * 16)
                    if layer:
                        nc.tensor.transpose(ps[:, 3, 0:E], router_raw[:, :], ident[0:E, 0:E]).then_inc(s_w_turned, 1)
                    pe.wait_ge(s_norm, NT)
                    transpose_tiles(nc, pe, bank, normed, ident, s_turned)
                    pe.wait_ge(s_xn_a, 1)
                    pe.wait_ge(s_xn_v, 1)
                    if layer:
                        pe.wait_ge(s_router, 1)
                    for t in range(NT):
                        last = nc.tensor.matmul(ps[:, 2, t * E:(t + 1) * E], xn[:, t * P:(t + 1) * P], router[:, :], start=True, stop=True)
                    last.then_inc(s_logit, 1)
                    if layer:
                        pe.wait_ge(s_late, n_late * 16)
                        for n in range(3 * NH):
                            if n >= 4:
                                pe.wait_ge(s_w_kept, n - 3)
                            nc.tensor.transpose(ps[:, 4 + n % 4, 0:P], raw[:, n // NH, n % NH, :], ident[:, :]).then_inc(s_w_turned, 1)
                    pe.wait_ge(s_packed, 1)
                    for t in range(NT):
                        last = nc.tensor.transpose(ps[:, t // 4, (t % 4) * P:(t % 4 + 1) * P], packed[:, t, :].bitcast(F32), ident[:, :])
                    last.then_inc(s_routes, 1)

                @block.scalar
                def _(act):
                    root(nc, act, moments, s_eps, s_root)
                    act.wait_ge(s_turned, 1)
                    nc.scalar.activation(xn[:, 0:HALF], bank[:, 0:HALF], ACT.Copy).then_inc(s_xn_a, 1)
                    if layer:
                        act.wait_ge(s_w_turned, 1)
                        nc.scalar.activation(router[:, :], ps[:, 3, 0:E], ACT.Copy).then_inc(s_router, 1)
                    act.wait_ge(s_exp_in, 1)
                    prob = scratch["prob"]
                    if layer:
                        nc.scalar.activation(prob[:, :, :], ps[:, 2, 0:NT * E].rearrange("p (t e) -> p t e", e=E), ACT.Sigmoid).then_inc(s_exp_out, 1)
                        for n in range(3 * NH):
                            act.wait_ge(s_w_turned, n + 2)
                            nc.scalar.activation((w_gate, w_up, w_down)[n // NH][:, n % NH, :], ps[:, 4 + n % 4, 0:P], ACT.Copy).then_inc(s_w_kept, 1)
                    else:
                        nc.scalar.activation(prob[:, :, :], prob[:, :, :], ACT.Exp).then_inc(s_exp_out, 1)

                @block.vector
                def _(dve):
                    step = stepper(dve)
                    step(nc.vector.memset(packed[:, :, :].bitcast(F32), 0.0), s_vec)
                    layer_norm(nc, dve, step, s_vec, stats, moments, x, normed, s_eps, s_root, s_norm)
                    dve.wait_ge(s_turned, 2)
                    step(nc.vector.tensor_copy(xn[:, HALF:T], bank[:, HALF:T]), s_xn_v)
                    dve.wait_ge(s_load, n_loads * 16)
                    dve.wait_ge(s_logit, 1)
                    if layer:
                        step(nc.vector.memset(scratch["peak"][:, :], 0.0), s_exp_in)
                        dve.wait_ge(s_exp_out, 1)
                        route_groups(nc, dve, step, s_vec, scratch, router_bias, order, weights)
                    else:
                        logits = ps[:, 2, 0:NT * E].rearrange("p (t e) -> p t e", e=E)
                        route_top2(nc, dve, step, s_vec, s_exp_in, s_exp_out, scratch, logits, order, weights)
                    step(nc.vector.tensor_copy(packed[:, :, 0:E], weights[:, :, :]), s_vec)
                    step(nc.vector.tensor_tensor(packed[:, :, 32:32 + E], weights[:, :, :], packed[:, :, 0:E].bitcast(F32), ALU.subtract), s_packed)
                    dve.wait_ge(s_late, n_late * 16)
                    step(nc.vector.tensor_copy(picks[:, :, :], picks_in[:, :, :]), s_vec)
                    dve.wait_ge(s_routes, 1)
                    step(nc.vector.tensor_copy(route_rows[:, :], bank[:, 0:T]), s_kept)

        with ExitStack() as own:
            b = Memory(nc, own, f"mixc{layer}")
            silu = [b.sb(f"silu{n}", [P, T]) for n in range(2)]
            hidden = [b.sb(f"hidden{n}", [P, T]) for n in range(2)]
            zero = b.sb("zero", [P, P])
            s_zero, s_gate, s_up, s_route, s_silu, s_prod, s_hidden, s_down, s_end = (b.sem(n) for n in (
                "zero", "gate", "up", "route", "silu", "product", "hidden", "down", "end"))
            with nc.Block() as block:
                @block.tensor
                def _(pe):
                    def down(n):
                        k = rows_of[n]
                        pe.wait_ge(s_hidden, n + 1)
                        for t in range(NT):
                            last = nc.tensor.matmul(bank[:, 6 * HALF + t * P:6 * HALF + (t + 1) * P], hidden[n % 2][0:k, t * P:(t + 1) * P],
                                                    w_down[0:k, n, :], start=False, stop=n == NH - 1 and t % 4 == 3, skip_group_check=True)
                        last.then_inc(s_down, 1)

                    pe.wait_ge(s_zero, 1)
                    for c in range(2):
                        nc.tensor.matmul(ps[:, 6 + c, :], zero[:, :], zero[:, 0:1].to_broadcast([P, HALF]), start=True, stop=False, skip_group_check=True)
                    for n in range(NH):
                        k = rows_of[n]
                        if n:
                            pe.wait_ge(s_silu, n)
                        for c in range(2):
                            last = nc.tensor.matmul(ps[0:k, c, :], w_gate[:, n, 0:k], xn[:, c * HALF:(c + 1) * HALF], start=True, stop=True)
                        last.then_inc(s_gate, 1)
                        if n:
                            pe.wait_ge(s_prod, n)
                        for c in range(2):
                            last = nc.tensor.matmul(ps[0:k, 2 + c, :], w_up[:, n, 0:k], xn[:, c * HALF:(c + 1) * HALF], start=True, stop=True)
                        last.then_inc(s_up, 1)
                        if n < ROUTED:
                            if n:
                                pe.wait_ge(s_hidden, n)
                            for c in range(2):
                                last = nc.tensor.matmul(ps[:, 4 + c, :], picks[:, n, :], route_rows[:, c * HALF:(c + 1) * HALF], start=True, stop=True)
                            last.then_inc(s_route, 1)
                        if n:
                            down(n - 1)
                    down(NH - 1)

                @block.scalar
                def _(act):
                    for n in range(NH):
                        k = rows_of[n]
                        act.wait_ge(s_gate, n + 1)
                        if n >= 2:
                            act.wait_ge(s_prod, n - 1)
                        nc.scalar.activation(silu[n % 2][0:k, :], bank[0:k, 0:T], ACT.Silu).then_inc(s_silu, 1)

                @block.vector
                def _(dve):
                    nc.vector.memset(zero[:, :], 0.0).then_inc(s_zero, 1)
                    for n in range(NH):
                        k = rows_of[n]
                        dve.wait_ge(s_silu, n + 1)
                        dve.wait_ge(s_up, n + 1)
                        if n < ROUTED:
                            nc.vector.tensor_tensor(silu[n % 2][0:k, :], silu[n % 2][0:k, :], bank[0:k, T:2 * T], ALU.mult).then_inc(s_prod, 1)
                            dve.wait_ge(s_prod, n + 1)
                            dve.wait_ge(s_route, n + 1)
                        if n >= 2:
                            dve.wait_ge(s_down, n - 1)
                        if n < ROUTED:
                            nc.vector.tensor_tensor(hidden[n % 2][0:k, :], silu[n % 2][0:k, :], bank[0:k, 2 * T:3 * T], ALU.mult).then_inc(s_hidden, 1)
                        else:
                            nc.vector.tensor_tensor(hidden[n % 2][0:k, :], silu[n % 2][0:k, :], bank[0:k, T:2 * T], ALU.mult).then_inc(s_hidden, 1)
                            if n < NH - 1:
                                nc.vector.memset(zero[:, 0:1], 0.0).then_inc(s_prod, 1)
                    dve.wait_ge(s_down, NH)
                    nc.vector.tensor_tensor(x[:, :, :], x[:, :, :], bank[:, 3 * T:4 * T].rearrange("p (t c) -> p t c", c=P), ALU.add).then_inc(s_end, 1)
                    dve.wait_ge(s_end, 1)


def route_groups(nc, dve, step, s_vec, s, bias, order, weights):
    E, scores, choice = 32, s["prob"], s["choice"]
    step(nc.vector.tensor_tensor(choice[:, :, :], scores[:, :, :], bias[:, :].unsqueeze(1).to_broadcast([P, NT, E]), ALU.add), s_vec)
    for n in range(NT * 4):
        t, g = n // 4, n % 4
        step(nc.vector.max(s["best"][:, t, g, :], choice[:, t, g * 8:(g + 1) * 8]), s_vec, wait=n == NT * 4 - 1)
    step(nc.vector.tensor_tensor(s["groups"][:, :, :], s["best"][:, :, :, 0], s["best"][:, :, :, 1], ALU.add), s_vec)
    select(nc, step, s_vec, s["groups"], order, s["larger"], s["equal"], s["rank"], 2)
    step(nc.vector.tensor_tensor(choice[:, :, :].rearrange("p t (g e) -> p (t g) e", g=4), choice[:, :, :].rearrange("p t (g e) -> p (t g) e", g=4),
                                 s["rank"][:, :, :].rearrange("p t g -> p (t g)").unsqueeze(2).to_broadcast([P, NT * 4, 8]), ALU.mult), s_vec)
    for t in range(NT):
        step(nc.vector.max(s["top"][:, t, :], choice[:, t, :]), s_vec, wait=t == NT - 1)
    for t in range(NT):
        step(nc.vector.match_replace(s["left"][:, t, :], s["top"][:, t, :], choice[:, t, :], MASKED), s_vec, wait=t == NT - 1)
    step(nc.vector.tensor_scalar(s["left"][:, :, :], s["left"][:, :, :], MASKED, None, ALU.is_equal), s_vec)
    step(nc.vector.tensor_tensor(weights[:, :, :], scores[:, :, :], s["left"][:, :, :], ALU.mult), s_vec)
    step(nc.vector.tensor_reduce(s["total"][:, :], weights[:, :, :], AX.X, ALU.add), s_vec)
    step(nc.vector.tensor_scalar(s["total"][:, :], s["total"][:, :], 1e-20, None, ALU.add), s_vec)
    step(nc.vector.reciprocal(s["total"][:, :], s["total"][:, :]), s_vec)
    step(nc.vector.tensor_tensor(weights[:, :, :], weights[:, :, :], s["total"][:, :].unsqueeze(2).to_broadcast([P, NT, E]), ALU.mult), s_vec)
    step(nc.vector.tensor_scalar(weights[:, :, :], weights[:, :, :], 2.5, None, ALU.mult), s_vec)


def mixture0(nc, kept, ps, a):
    mixture(nc, kept, ps, a, 0)


def mixture1(nc, kept, ps, a):
    mixture(nc, kept, ps, a, 1)


def lstm_step(nc, kept, ps, a):
    x, ident = kept["x"], kept["ident"]
    bank = ps[:, :, :].rearrange("p b c -> p (b c)")
    with ExitStack() as stack:
        m = Memory(nc, stack, "lstm")
        w, bias = m.sb("w", [P, 4 * P]), m.sb("bias", [P, 4])
        stats, moments, normed, xn = m.sb("stats", [P, NT, 6]), m.sb("moments", [P, NT, 2]), m.sb("normed", [P, NT, P]), m.sb("xn", [P, T])
        gate_in, gate_out, cand = m.sb("gate_in", [P, T]), m.sb("gate_out", [P, T]), m.sb("cand", [P, T])
        s_load, s_vec, s_eps, s_root, s_norm, s_turned, s_xn_a, s_xn_v, s_gates, s_act, s_cell, s_tanh, s_h, s_back, s_x = (m.sem(n) for n in (
            "loaded", "vector_step", "variance", "root", "normed", "turned", "xn_scalar", "xn_vector", "gates", "activated", "cell", "tanh",
            "state", "state_turned", "x_done"))
        with nc.Block() as block:
            @block.sync
            def _(sp):
                sp.dma_start(w[:, :], a["L1_attn_w"]).then_inc(s_load, 16)
                sp.dma_start(bias[:, :], columns(a["L1_attn_bias"])).then_inc(s_load, 16)
                sp.wait_ge(s_load, 2 * 16)

            @block.tensor
            def _(pe):
                pe.wait_ge(s_load, 2 * 16)
                pe.wait_ge(s_norm, NT)
                transpose_tiles(nc, pe, bank, normed, ident, s_turned)
                pe.wait_ge(s_xn_a, 1)
                pe.wait_ge(s_xn_v, 1)
                for n, g in enumerate((0, 2, 3)):
                    for c in range(2):
                        last = nc.tensor.matmul(ps[:, 2 + 2 * n + c, :], w[:, g * P:(g + 1) * P], xn[:, c * HALF:(c + 1) * HALF], start=True, stop=True)
                    last.then_inc(s_gates, 1)
                pe.wait_ge(s_h, 1)
                for t in range(NT):
                    last = nc.tensor.transpose(bank[:, t * P:(t + 1) * P], cand[:, t * P:(t + 1) * P], ident[:, :])
                last.then_inc(s_back, 1)

            @block.scalar
            def _(act):
                root(nc, act, moments, s_eps, s_root)
                act.wait_ge(s_load, 2 * 16)
                act.wait_ge(s_turned, 1)
                nc.scalar.activation(xn[:, 0:HALF], bank[:, 0:HALF], ACT.Copy).then_inc(s_xn_a, 1)
                for n, (dst, g, f) in enumerate(((gate_in, 0, ACT.Sigmoid), (gate_out, 2, ACT.Sigmoid), (cand, 3, ACT.Tanh))):
                    act.wait_ge(s_gates, n + 1)
                    nc.scalar.activation(dst[:, :], bank[:, (n + 1) * T:(n + 2) * T], f, bias=bias[:, g:g + 1]).then_inc(s_act, 1)
                act.wait_ge(s_cell, 1)
                nc.scalar.activation(cand[:, :], cand[:, :], ACT.Tanh).then_inc(s_tanh, 1)

            @block.vector
            def _(dve):
                step = stepper(dve)
                layer_norm(nc, dve, step, s_vec, stats, moments, x, normed, s_eps, s_root, s_norm)
                dve.wait_ge(s_turned, 2)
                step(nc.vector.tensor_copy(xn[:, HALF:T], bank[:, HALF:T]), s_xn_v)
                dve.wait_ge(s_act, 3)
                step(nc.vector.tensor_tensor(cand[:, :], gate_in[:, :], cand[:, :], ALU.mult), s_cell)
                dve.wait_ge(s_tanh, 1)
                step(nc.vector.tensor_tensor(cand[:, :], gate_out[:, :], cand[:, :], ALU.mult), s_h)
                dve.wait_ge(s_back, 1)
                step(nc.vector.tensor_tensor(x[:, :, :], x[:, :, :], bank[:, 0:T].rearrange("p (t c) -> p t c", c=P), ALU.add), s_x)


def latent_attention(nc, kept, ps, a):
    H1 = 8
    NM, NL = NK, NT
    NZ = NM + NL
    x, ident = kept["x"], kept["ident"]
    bank = ps[:, :, :].rearrange("p b c -> p (b c)")
    with ExitStack() as stack:
        m = Memory(nc, stack, "lat")
        z_rows = [m.sb(f"z_rows_{n}", [P, NZ, P], F32R) for n in ("high", "low")]
        z_cols = [m.sb(f"z_cols_{n}", [P, NZ * P], F32R) for n in ("high", "low")]
        mix = m.sb("mix", [P, 2 * P])
        latents = m.sb("latents", [P, T])

        with ExitStack() as own:
            b = Memory(nc, own, "zed")
            z = b.sb("z", [P, NM, P])
            stats, moments, shift = b.sb("stats", [P, NM, 6]), b.sb("moments", [P, NM, 2]), b.sb("shift", [P, NM])
            fresh, norms = b.sb("fresh", [P, 1]), b.sb("norms", [P, 4])
            lstats, lmoments = b.sb("lstats", [P, NT, 6]), b.sb("lmoments", [P, NT, 2])
            lmoments2, normed, normed2 = b.sb("lmoments2", [P, NT, 2]), b.sb("normed", [P, NT, P]), b.sb("normed2", [P, NT, P])
            s_load, s_rows = b.sem("loaded"), [b.sem(f"rows_loaded{n}") for n in range(3)]
            s_vec, s_stat, s_var, s_root, s_shift, s_z, s_high, s_low, s_turned, s_chigh, s_clow = (b.sem(n) for n in (
                "vector_step", "statistics", "variance", "root", "shift", "z", "rows_high", "rows_low", "turned", "columns_high", "columns_low"))
            s_eps1, s_root1, s_norm1, s_eps2, s_root2, s_norm2, s_lturned, s_mix = (b.sem(n) for n in (
                "eps1", "root1", "norm1", "eps2", "root2", "norm2", "latents_turned", "mix"))
            ctx = a["ctx_1024"][0]
            parts = ((0, NM // 2), (NM // 2, NM - 1))
            PAIRS = (NI - 2) // 2

            with nc.Block() as block:
                @block.sync
                def _(sp):
                    for n, (lo, hi) in enumerate(parts):
                        sp.dma_start(z[:, lo:hi, :], ctx[lo * P:hi * P, :].rearrange("(t p) c -> p t c", p=P)).then_inc(s_rows[n], 16)
                    sp.dma_start(z[:, NM - 1, :], ctx[LAST:LC, :]).then_inc(s_rows[2], 16)
                    sp.dma_start(fresh[:, :], a["fresh"]).then_inc(s_load, 16)
                    for n, name in enumerate(("gamma_media", "beta_media", "gamma_lat", "beta_lat")):
                        sp.dma_start(norms[:, n:n + 1], columns(a[f"L1_xattn_{name}"])).then_inc(s_load, 16)
                    sp.wait_ge(s_load, 5 * 16)

                @block.scalar
                def _(act):
                    def norm(j):
                        for n in range(U0):
                            t = j * U0 + n
                            row = z[:, bass.ds(t, 1), :].rearrange("p a c -> p (a c)")
                            nc.scalar.activation(row, row, ACT.Identity, bias=shift[:, bass.ds(t, 1)], scale=moments[:, bass.ds(t, 1), 1]).then_inc(s_z, 1)

                    def high(j, k):
                        act.wait_ge(s_turned, j + 1)
                        nc.scalar.activation(z_cols[0][:, bass.ds(j * (U0 * P), U0 * P)], ps[:, k, 0:U0 * P], ACT.Copy).then_inc(s_chigh, 1)

                    root(nc, act, lmoments, s_eps1, s_root1)
                    root(nc, act, lmoments2, s_eps2, s_root2)
                    act.wait_ge(s_var, 1)
                    nc.scalar.activation(moments[:, :, 1], moments[:, :, 1], ACT.Sqrt).then_inc(s_root, 1)
                    act.wait_ge(s_shift, 1)
                    norm(0)
                    norm(1)
                    with act.Fori(0, PAIRS) as i:
                        for k in range(2):
                            high(i * 2 + k, k)
                            norm(i * 2 + (k + 2))
                    high(NI - 3, 0)
                    norm(NI - 1)
                    high(NI - 2, 1)
                    high(NI - 1, 0)

                @block.tensor
                def _(pe):
                    def turn(j, k):
                        pe.wait_ge(s_z, j * U0 + U0)
                        for n in range(U0):
                            last = nc.tensor.transpose(ps[:, k, n * P:(n + 1) * P], z[:, j * U0 + n, :], ident[:, :])
                        last.then_inc(s_turned, 1)

                    pe.wait_ge(s_norm2, NT)
                    for t in range(NT):
                        last = nc.tensor.transpose(ps[:, 2 + t // 4, (t % 4) * P:(t % 4 + 1) * P], normed2[:, t, :], ident[:, :])
                        if t % 4 == 3:
                            last.then_inc(s_lturned, 1)
                    for j in range(NI):
                        if j >= 2:
                            pe.wait_ge(s_clow, j - 1)
                        turn(j, j % 2)

                @block.vector
                def _(dve):
                    step = stepper(dve)

                    def split_rows(j):
                        dve.wait_ge(s_z, j * U0 + U0)
                        tiles = bass.ds(j * U0, U0)
                        nc.vector.tensor_scalar(z_rows[0][:, tiles, :], z[:, tiles, :], 1.0, None, ALU.mult).then_inc(s_high, 1)
                        dve.wait_ge(s_high, j + 1)
                        nc.vector.tensor_tensor(z_rows[1][:, tiles, :], z[:, tiles, :], z_rows[0][:, tiles, :].bitcast(F32), ALU.subtract).then_inc(s_low, 1)

                    def split_columns(j, k):
                        dve.wait_ge(s_chigh, j + 1)
                        cols = bass.ds(j * (U0 * P), U0 * P)
                        nc.vector.tensor_tensor(z_cols[1][:, cols], ps[:, k, 0:U0 * P], z_cols[0][:, cols].bitcast(F32), ALU.subtract).then_inc(s_clow, 1)

                    layer_norm(nc, dve, step, s_vec, lstats, lmoments, x, normed, s_eps1, s_root1, s_norm1)
                    layer_norm(nc, dve, step, s_vec, lstats, lmoments2, normed, normed2, s_eps2, s_root2, s_norm2)
                    for n in range(3):
                        dve.wait_ge(s_rows[n], 16)
                    for t in range(NM):
                        step(nc.vector.bn_stats(stats[:, t, :], z[:, t, :]), s_stat, wait=t == NM - 1)
                    for t in range(NM):
                        step(nc.vector.bn_aggr(moments[:, t, :], stats[:, t, :]), s_stat, wait=t == NM - 1)
                    step(nc.vector.tensor_scalar(moments[:, :, 1], moments[:, :, 1], LN_EPS, None, ALU.add), s_var)
                    dve.wait_ge(s_root, 1)
                    step(nc.vector.reciprocal(moments[:, :, 1], moments[:, :, 1]), s_vec)
                    step(nc.vector.scalar_tensor_tensor(shift[:, :], moments[:, :, 0], -1.0, moments[:, :, 1], ALU.mult, ALU.mult), s_vec)
                    step(nc.vector.tensor_scalar(shift[:, :], shift[:, :], 1.0, None, ALU.add), s_shift)
                    split_rows(0)
                    with dve.Fori(0, (NI - 1) // 2) as i:
                        for k in range(2):
                            split_rows(i * 2 + (k + 1))
                            split_columns(i * 2 + k, k)
                    split_columns(NI - 1, 0)
                    dve.wait_ge(s_load, 5 * 16)
                    dve.wait_ge(s_low, NI)
                    for part in z_rows:
                        step(nc.vector.tensor_scalar(part[:, NM - 1, :], part[:, NM - 1, :].bitcast(F32), fresh[:, 0:1], None, ALU.mult), s_vec)
                    for n in range(2):
                        gain, offset = norms[:, 2 * n:2 * n + 1], norms[:, 2 * n + 1:2 * n + 2]
                        step(nc.vector.tensor_tensor(shift[:, n:n + 1], offset, gain, ALU.subtract), s_vec)
                        step(nc.vector.tensor_scalar(shift[:, n:n + 1], shift[:, n:n + 1], 1.0 / P, None, ALU.mult), s_vec)
                        step(nc.vector.tensor_scalar(mix[:, n * P:(n + 1) * P], ident[:, :], gain, shift[:, n:n + 1], ALU.mult, ALU.add), s_mix)
                    for c in range(2):
                        lo, hi = c * HALF, (c + 1) * HALF
                        dve.wait_ge(s_lturned, 2)
                        step(nc.vector.tensor_scalar(latents[:, lo:hi], ps[:, 2 + c, :], norms[:, 2:3], norms[:, 3:4], ALU.mult, ALU.add), s_vec)
                        step(nc.vector.tensor_scalar(normed[:, 4 * c:4 * c + 4, :].rearrange("p t c -> p (t c)"), ps[:, 2 + c, :], 1.0, None, ALU.add), s_vec)
                        step(nc.vector.tensor_copy(z_cols[0][:, NM * P + lo:NM * P + hi], normed[:, 4 * c:4 * c + 4, :].rearrange("p t c -> p (t c)")), s_vec)
                        step(nc.vector.tensor_tensor(z_cols[1][:, NM * P + lo:NM * P + hi], normed[:, 4 * c:4 * c + 4, :].rearrange("p t c -> p (t c)"),
                                                     z_cols[0][:, NM * P + lo:NM * P + hi].bitcast(F32), ALU.subtract), s_vec)
                    step(nc.vector.tensor_scalar(normed2[:, :, :], normed2[:, :, :], 1.0, None, ALU.add), s_vec)
                    step(nc.vector.tensor_copy(z_rows[0][:, NM:NZ, :], normed2[:, :, :]), s_vec)
                    step(nc.vector.tensor_tensor(z_rows[1][:, NM:NZ, :], normed2[:, :, :], z_rows[0][:, NM:NZ, :].bitcast(F32), ALU.subtract), s_vec)

        latent_heads(nc, kept, ps, a, z_rows, z_cols, mix, latents, H1, NM, NL)


def latent_heads(nc, kept, ps, a, z_rows, z_cols, mix, latents, H1, NM, NL):
    x, ident = kept["x"], kept["ident"]
    NZ = NM + NL
    REACH = 11.4
    ROUNDS = 3
    U_LATENTS, TAKE_LATENTS, FOLD_V, OUT_WEIGHTS, OUTPUTS, SCALE, ADD = 0, 1, 3, 5, (7, 8), 9, 10
    FOLD_K, QUERY, R_AT, BOUND, EXACT = 12, 14, (16, 24), 30, 32
    SUM, SQUARES = 2, 4
    TAKE_MEDIA, U_MEDIA = NM, NM + 2
    bank = ps[:, :, :].rearrange("p b c -> p (b c)")
    mid = bank[:, 6 * HALF:8 * HALF]
    with ExitStack() as own:
        b = Memory(nc, own, "hed")
        w_q, w_k, w_v, w_o = (b.sb(n, [P, P]) for n in ("w_q", "w_k", "w_v", "w_o"))
        biases = b.sb("biases", [P, 3, H1])
        b_o = b.sb("b_o", [P, P])
        k2, v2, w2 = (b.sb(n, [P, 2, P]) for n in ("k2", "v2", "w2"))
        q = b.sb("q", [P, T])
        r = [[b.sb(f"r_{g}_{part}", [P, T], F32R) for part in ("high", "low")] for g in ("media", "latents")]
        r_next = [[b.sb(f"r_next_{g}_{part}", [P, T], F32R) for part in ("high", "low")] for g in ("media", "latents")]
        squares = b.sb("squares", [P, T], F32R)
        ones_in, ones, mean = b.sb("ones_in", [P, P]), b.sb("ones", [P, P], F32R), b.sb("mean", [P, 1])
        peak = b.sb("peak", [P, 2, 2])
        twice, quotient = b.sb("twice", [P, 2]), b.sb("quotient", [P, 2])
        bound, minus, minus_next = b.sb("bound", [P, 1]), b.sb("minus", [P, 1]), b.sb("minus_next", [P, 1])
        exps = [b.sb(f"exps{n}", [P, T]) for n in range(2)]
        high = [b.sb(f"exps_high{n}", [P, T], F32R) for n in range(2)]
        low = [b.sb(f"exps_low{n}", [P, T], F32R) for n in range(2)]
        u = [b.sb(f"u_{g}", [P, T]) for g in ("media", "latents")]
        inverse = b.sb("inverse", [P, NT])
        row_max, chunk_max, spread_max = b.sb("row_max", [P, NT]), b.sb("chunk_max", [P, NT]), b.sb("spread_max", [P, P])
        s_bias, s_w_qk, s_w_vo, s_set, s_end = (b.sem(n) for n in ("biases_loaded", "w_q_k_loaded", "w_v_o_loaded", "set", "end"))
        s_fold_k, s_k2, s_q, s_q_kept, s_r, s_r_high, s_r_low, s_sq, s_bound_mm, s_peak, s_root, s_bound, s_ready = (b.sem(n) for n in (
            "keys_folded", "k2", "q", "q_kept", "r", "r_high", "r_low", "squares", "bound_sums", "peaks", "root", "bound_step", "ready"))
        s_take_low, s_take_high = ([b.sem(f"taken_{part}_{g}") for g in ("media", "latents")] for part in ("low", "high"))
        s_minus = b.sem("minus")
        s_score, s_exp, s_high, s_low, s_weighted = (b.sem(n) for n in ("scores", "exps", "exps_high", "exps_low", "weighted"))
        s_u_media, s_u_latents, s_fold_v, s_v2, s_w2, s_w2_kept, s_den, s_inv, s_y, s_scaled, s_added = (b.sem(n) for n in (
            "u_media", "u_latents", "values_folded", "v2", "w2", "w2_kept", "denominators", "inverse", "outputs", "outputs_scaled", "added"))
        x_score, x_max, x_row, x_spread, x_turned, x_fixed, x_done = (b.sem(n) for n in (
            "exact_scores", "exact_max", "exact_row", "exact_spread", "exact_turned", "exact_fixed", "exact_done"))
        XN = NI * NT + 2 * NT
        ROWS = NI + 3

        with nc.Block() as block:
            @block.sync
            def _(sp):
                for n, name in enumerate(("bq", "bk", "bv")):
                    src = a["L1_xattn_bq"] if n == 0 else a["L1_xattn_bkv"][(n - 1) * H1 * P:n * H1 * P]
                    sp.dma_start(biases[:, n, :], columns(src)).then_inc(s_bias, 16)
                sp.dma_start(b_o[:, :], spread(a["L1_xattn_bo"])).then_inc(s_bias, 16)

                def load_qk(h):
                    sp.dma_start(w_q[:, :], a["L1_xattn_Wq"][:, bass.ds(h * P, P)]).then_inc(s_w_qk, 16)
                    sp.dma_start(w_k[:, :], a["L1_xattn_Wkv"][:, bass.ds(h * P, P)]).then_inc(s_w_qk, 16)

                def load_vo(h):
                    sp.dma_start(w_v[:, :], a["L1_xattn_Wkv"][:, bass.ds(h * P + H1 * P, P)]).then_inc(s_w_vo, 16)
                    sp.dma_start(w_o[:, :], a["L1_xattn_Wo"][bass.ds(h * P, P), :]).then_inc(s_w_vo, 16)

                load_qk(0)
                load_vo(0)
                with sp.Fori(0, H1 - 1) as h:
                    sp.wait_ge(s_q, h + 1)
                    load_qk(h + 1)
                    sp.wait_ge(s_w2, h + 1)
                    load_vo(h + 1)
                sp.wait_ge(s_w_qk, H1 * 2 * 16)
                sp.wait_ge(s_w_vo, H1 * 2 * 16)
                sp.wait_ge(s_bias, 4 * 16)

            @block.tensor
            def _(pe):
                def scores(h, t):
                    if t >= 2:
                        pe.wait_ge(s_high, h * NZ + (t - 1))
                    elif t == 0 and not first_head(h):
                        pe.wait_ge(s_high, h * NZ)
                    if t in (0, NM):
                        pe.wait_ge(s_take_low[t >= NM], h + 1)
                        pe.wait_ge(s_take_high[t >= NM], h + 1)
                    group = r[t >= NM]
                    for c in range(2):
                        for n, (zp, rp) in enumerate(((0, 0), (0, 1), (1, 0))):
                            last = nc.tensor.matmul(ps[:, 2 * (t % 2) + c, :], z_cols[zp][:, t * P:(t + 1) * P], group[rp][:, c * HALF:(c + 1) * HALF],
                                                    start=n == 0, stop=n == 2)
                    last.then_inc(s_score, 1)

                def weigh(h, t):
                    if t == 0 and not first_head(h):
                        pe.wait_ge(s_u_media, h)
                    if t == NM and not first_head(h):
                        pe.wait_ge(s_added, h)
                    pe.wait_ge(s_low, h * NZ + (t + 1))
                    first, last_tile = (0, NM - 1) if t < NM else (NM, NZ - 1)
                    for c in range(2):
                        for n, (zp, e) in enumerate(((0, high), (0, low), (1, high))):
                            last = nc.tensor.matmul(ps[:, (4 if t < NM else 6) + c, :], z_rows[zp][:, t, :], e[t % 2][:, c * HALF:(c + 1) * HALF],
                                                    start=t == first and n == 0, stop=t == last_tile and n == 2)
                    last.then_inc(s_weighted, 1)

                def finish(h, at):
                    if at == U_LATENTS:
                        weigh(h, NZ - 1)
                    elif at == FOLD_V:
                        pe.wait_ge(s_w_vo, h * 32 + 32)
                        pe.wait_ge(s_u_latents, h + 1)
                        nc.tensor.matmul(ps[:, 6, 0:2 * P], w_v[:, :], mix[:, :], start=True, stop=True).then_inc(s_fold_v, 1)
                    elif at == OUT_WEIGHTS:
                        pe.wait_ge(s_v2, h + 1)
                        for g in range(2):
                            last = nc.tensor.matmul(ps[:, 6, g * P:(g + 1) * P], v2[:, g, :], w_o[:, :], start=True, stop=True)
                        last.then_inc(s_w2, 1)
                        pe.wait_ge(s_u_media, h + 1)
                        for t in range(NT):
                            for g in range(2):
                                last = nc.tensor.matmul(ps[:, 7, t:t + 1], u[g][:, t * P:(t + 1) * P], mean[:, :], start=g == 0, stop=g == 1)
                        last.then_inc(s_den, 1)
                    elif at in OUTPUTS:
                        if at == OUTPUTS[0]:
                            pe.wait_ge(s_w2_kept, h + 1)
                            pe.wait_ge(s_inv, h + 1)
                        c = OUTPUTS.index(at)
                        for t in range(4 * c, 4 * c + 4):
                            for g in range(2):
                                last = nc.tensor.matmul(mid[:, t * P:(t + 1) * P], u[g][:, t * P:(t + 1) * P], w2[:, g, :], start=g == 0, stop=g == 1)
                        last.then_inc(s_y, 1)

                def prepare(h, at):
                    if at == FOLD_K:
                        pe.wait_ge(s_w_qk, h * 32 + 32)
                        nc.tensor.matmul(ps[:, 6, 0:2 * P], w_k[:, :], mix[:, :], start=True, stop=True).then_inc(s_fold_k, 1)
                    elif at == QUERY:
                        pe.wait_ge(s_k2, h + 1)
                        for c in range(2):
                            last = nc.tensor.matmul(ps[:, 6 + c, :], w_q[:, :], latents[:, c * HALF:(c + 1) * HALF], start=True, stop=True)
                        last.then_inc(s_q, 1)
                    for g in range(2):
                        if at == R_AT[g]:
                            if g == 0:
                                pe.wait_ge(s_q_kept, h + 1)
                            else:
                                pe.wait_ge(s_peak, h * 4 + 2)
                            for c in range(2):
                                last = nc.tensor.matmul(ps[:, 6 + c, :], k2[:, g, :], q[:, c * HALF:(c + 1) * HALF], start=True, stop=True)
                            last.then_inc(s_r, 1)
                        elif at == R_AT[g] + SUM:
                            pe.wait_ge(s_r_low, h * 2 + (g + 1))
                            for c in range(2):
                                last = nc.tensor.matmul(ps[:, 6 + c, :], ones[:, :], r_next[g][0][:, c * HALF:(c + 1) * HALF], start=True, stop=True)
                            last.then_inc(s_bound_mm, 1)
                        elif at == R_AT[g] + SQUARES:
                            pe.wait_ge(s_sq, h * 2 + (g + 1))
                            pe.wait_ge(s_peak, h * 4 + (2 * g + 1))
                            for c in range(2):
                                last = nc.tensor.matmul(ps[:, 6 + c, :], ones[:, :], squares[:, c * HALF:(c + 1) * HALF], start=True, stop=True)
                            last.then_inc(s_bound_mm, 1)
                    if at == EXACT:
                        pe.wait_ge(s_ready, h + 1)
                        nc.tensor.matmul(ps[:, 6, 0:1], ident[:, :], bound[:, :], start=True, stop=True)
                        bits = nc.tensor.value_load(bound[0:1, 0:1].bitcast(I32))
                        with pe.If(bits > SAFE_BITS):
                            exact(h)

                def exact(h):
                    def block_scores(g, cols, n, base, width):
                        if n >= 2:
                            pe.wait_ge(x_max, h * XN + base + (n - 1))
                        for k, (rp, zp) in enumerate(((0, 0), (0, 1), (1, 0))):
                            last = nc.tensor.matmul(ps[:, 6 + n % 2, 0:width], r_next[g][rp][:, n % NT * P:(n % NT + 1) * P], z_cols[zp][:, cols],
                                                    start=k == 0, stop=k == 2)
                        last.then_inc(x_score, 1)

                    with pe.Fori(0, NI) as i:
                        pe.wait_ge(x_row, h * ROWS + i + 1)
                        for n in range(NT):
                            block_scores(0, bass.ds(i * (U0 * P), U0 * P), n, i * NT, U0 * P)
                    pe.wait_ge(x_row, h * ROWS + NI + 1)
                    for n in range(2 * NT):
                        block_scores(1, slice(NM * P + n // NT * HALF, NM * P + (n // NT + 1) * HALF), n, NI * NT, HALF)
                    for t in range(NT):
                        pe.wait_ge(x_spread, h * NT + (t + 1))
                        nc.tensor.matmul(mid[:, t * P:(t + 1) * P], spread_max[:, :], ident[:, :], start=True, stop=True).then_inc(x_turned, 1)
                    pe.wait_ge(x_done, h + 1)

                def head(h, before=True, after=True):
                    for t in range(NZ):
                        scores(h, t)
                        if t >= 2:
                            weigh(h, t - 2)
                        if before:
                            finish(h - 1, t)
                        if after:
                            prepare(h + 1, t)
                    weigh(h, NZ - 2)

                pe.wait_ge(s_set, 4)
                for at in range(NZ):
                    prepare(0, at)
                head(0, before=False)
                with pe.Fori(1, H1 - 1) as h:
                    head(h)
                head(H1 - 1, after=False)
                for at in range(NZ):
                    finish(H1 - 1, at)

            @block.scalar
            def _(act):
                def tile(h, t):
                    act.wait_ge(s_score, h * NZ + (t + 1))
                    if t >= 2:
                        act.wait_ge(s_low, h * NZ + (t - 1))
                    pair = bank[:, 2 * (t % 2) * HALF:(2 * (t % 2) + 2) * HALF]
                    nc.scalar.activation(exps[t % 2][:, :], pair, ACT.Exp, bias=minus[:, 0:1]).then_inc(s_exp, 1)
                    if t >= 2:
                        act.wait_ge(s_weighted, h * NZ + (t - 1))
                    elif t == 0 and not first_head(h):
                        act.wait_ge(s_weighted, h * NZ)
                    nc.scalar.activation(high[t % 2][:, :], pair, ACT.Exp, bias=minus[:, 0:1]).then_inc(s_high, 1)

                def finish(h, at):
                    if at == OUT_WEIGHTS:
                        act.wait_ge(s_w2, h + 1)
                        nc.scalar.activation(w2[:, :, :], ps[:, 6, 0:2 * P].rearrange("p (g c) -> p g c", g=2), ACT.Copy).then_inc(s_w2_kept, 1)

                def prepare(h, at):
                    for g in range(2):
                        if at == R_AT[g]:
                            act.wait_ge(s_r, h * 2 + (g + 1))
                            if not first_head(h):
                                act.wait_ge(s_take_high[g], h)
                            nc.scalar.activation(r_next[g][0][:, :], mid, ACT.Copy).then_inc(s_r_high, 1)
                        elif at == R_AT[g] + SUM:
                            act.wait_ge(s_r_high, h * 2 + (g + 1))
                            if g:
                                act.wait_ge(s_bound_mm, h * 4 + 2)
                            nc.scalar.activation(squares[:, :], r_next[g][0][:, :].bitcast(F32), ACT.Square).then_inc(s_sq, 1)

                def take(h, g):
                    act.wait_ge(s_take_low[g], h + 1)
                    nc.scalar.activation(r[g][0][:, :], r_next[g][0][:, :].bitcast(F32), ACT.Copy).then_inc(s_take_high[g], 1)

                def head(h, before=True, after=True):
                    if before:
                        act.wait_ge(s_high, h * NZ)
                    act.wait_ge(s_take_low[0], h + 1)
                    nc.scalar.activation(minus[:, :], minus_next[:, :], ACT.Copy).then_inc(s_minus, 1)
                    act.wait_ge(s_minus, h + 1)
                    if before:
                        act.wait_ge(s_low, h * NZ)
                    for t in range(NZ):
                        tile(h, t)
                        if t == TAKE_LATENTS:
                            take(h, 1)
                        if before:
                            finish(h - 1, t)
                        if after:
                            prepare(h + 1, t)
                            if t == TAKE_MEDIA:
                                take(h + 1, 0)
                        if t == U_MEDIA:
                            copy_media(h, before)

                def copy_media(h, before):
                    act.wait_ge(s_weighted, h * NZ + NM)
                    if before:
                        act.wait_ge(s_y, h * 2)
                    nc.scalar.activation(u[0][:, :], bank[:, 4 * HALF:6 * HALF], ACT.Copy).then_inc(s_u_media, 1)

                act.wait_ge(s_set, 4)
                for at in range(NZ):
                    prepare(0, at)
                take(0, 0)
                head(0, before=False)
                with act.Fori(1, H1 - 1) as h:
                    head(h)
                head(H1 - 1, after=False)
                for at in range(NZ):
                    finish(H1 - 1, at)

            @block.vector
            def _(dve):
                step = stepper(dve)

                def exact(h):
                    def maxima(base, done, width):
                        dve.wait_ge(x_row, h * ROWS + done)
                        for n in range(NT):
                            dve.wait_ge(x_score, h * XN + base + (n + 1))
                            nc.vector.tensor_reduce(chunk_max[:, n:n + 1], ps[:, 6 + n % 2, 0:width], AX.X, ALU.max).then_inc(x_max, 1)
                        dve.wait_ge(x_max, h * XN + base + NT)
                        nc.vector.tensor_tensor(row_max[:, :], row_max[:, :], chunk_max[:, :], ALU.max).then_inc(x_row, 1)

                    nc.vector.memset(row_max[:, :], MASKED).then_inc(x_row, 1)
                    with dve.Fori(0, NI) as i:
                        maxima(i * NT, i + 1, U0 * P)
                    for k in range(2):
                        maxima(NI * NT + k * NT, NI + 1 + k, HALF)
                    dve.wait_ge(x_row, h * ROWS + NI + 3)
                    for t in range(NT):
                        if t:
                            dve.wait_ge(x_turned, h * NT + t)
                        nc.vector.tensor_copy(spread_max[:, :], row_max[:, t:t + 1].to_broadcast([P, P])).then_inc(x_spread, 1)
                    dve.wait_ge(x_turned, h * NT + NT)
                    for g in range(2):
                        nc.vector.tensor_tensor(q[:, :], r_next[g][0][:, :].bitcast(F32), r_next[g][1][:, :].bitcast(F32), ALU.add).then_inc(x_fixed, 1)
                        dve.wait_ge(x_fixed, h * 8 + (4 * g + 1))
                        nc.vector.scalar_tensor_tensor(q[:, :], mid, -1.0 / P, q[:, :], ALU.mult, ALU.add).then_inc(x_fixed, 1)
                        dve.wait_ge(x_fixed, h * 8 + (4 * g + 2))
                        nc.vector.tensor_copy(r_next[g][0][:, :], q[:, :]).then_inc(x_fixed, 1)
                        dve.wait_ge(x_fixed, h * 8 + (4 * g + 3))
                        nc.vector.tensor_tensor(r_next[g][1][:, :], q[:, :], r_next[g][0][:, :].bitcast(F32), ALU.subtract).then_inc(x_fixed, 1)
                        dve.wait_ge(x_fixed, h * 8 + (4 * g + 4))
                    nc.vector.memset(minus_next[:, :], 0.0).then_inc(x_done, 1)

                def finish(h, at):
                    if at == U_LATENTS:
                        dve.wait_ge(s_weighted, h * NZ + NZ)
                        nc.vector.tensor_copy(u[1][:, :], mid).then_inc(s_u_latents, 1)
                    elif at == FOLD_V:
                        dve.wait_ge(s_fold_v, h + 1)
                        nc.vector.tensor_scalar(v2[:, :, :], ps[:, 6, 0:2 * P].rearrange("p (g c) -> p g c", g=2),
                                                biases[:, 2, bass.ds(h, 1)], None, ALU.add).then_inc(s_v2, 1)
                    elif at == OUT_WEIGHTS:
                        dve.wait_ge(s_den, h + 1)
                        nc.vector.reciprocal(inverse[:, :], ps[:, 7, 0:NT]).then_inc(s_inv, 1)
                    elif at == SCALE:
                        dve.wait_ge(s_y, h * 2 + 2)
                        nc.vector.tensor_tensor(q[:, :].rearrange("p (t c) -> p t c", c=P), mid.rearrange("p (t c) -> p t c", c=P),
                                                inverse[:, :].unsqueeze(2).to_broadcast([P, NT, P]), ALU.mult).then_inc(s_scaled, 1)
                    elif at == ADD:
                        dve.wait_ge(s_scaled, h + 1)
                        if not first_head(h):
                            dve.wait_ge(s_added, h)
                        nc.vector.tensor_tensor(x[:, :, :], x[:, :, :], q[:, :].rearrange("p (t c) -> p t c", c=P), ALU.add).then_inc(s_added, 1)

                def prepare(h, at):
                    if at == FOLD_K:
                        dve.wait_ge(s_fold_k, h + 1)
                        nc.vector.tensor_scalar(k2[:, :, :], ps[:, 6, 0:2 * P].rearrange("p (g c) -> p g c", g=2),
                                                biases[:, 1, bass.ds(h, 1)], None, ALU.add).then_inc(s_k2, 1)
                    elif at == QUERY:
                        dve.wait_ge(s_q, h + 1)
                        if not (first_head(h) or first_head(h - 1)):
                            dve.wait_ge(s_added, h - 1)
                        nc.vector.tensor_scalar(q[:, :], mid, biases[:, 0, bass.ds(h, 1)], float(P) ** -0.5, ALU.add, ALU.mult).then_inc(s_q_kept, 1)
                    for g in range(2):
                        if at == R_AT[g]:
                            dve.wait_ge(s_r_high, h * 2 + (g + 1))
                            if not first_head(h):
                                dve.wait_ge(s_take_low[g], h)
                            nc.vector.tensor_tensor(r_next[g][1][:, :], mid, r_next[g][0][:, :].bitcast(F32), ALU.subtract).then_inc(s_r_low, 1)
                        elif at == R_AT[g] + SUM:
                            dve.wait_ge(s_bound_mm, h * 4 + (2 * g + 1))
                            nc.vector.tensor_reduce(peak[:, g, 0:1], mid, AX.X, ALU.max, apply_absolute_value=True).then_inc(s_peak, 1)
                        elif at == R_AT[g] + SQUARES:
                            dve.wait_ge(s_bound_mm, h * 4 + (2 * g + 2))
                            nc.vector.tensor_reduce(peak[:, g, 1:2], mid, AX.X, ALU.max).then_inc(s_peak, 1)
                    if at == BOUND:
                        dve.wait_ge(s_peak, h * 4 + 4)
                        nc.vector.tensor_scalar(twice[:, :], peak[:, :, 1], 1.0, None, ALU.add).then_inc(s_root, 1)
                        for n in range(ROUNDS):
                            dve.wait_ge(s_root, h * (3 * ROUNDS + 1) + 3 * n + 1)
                            nc.vector.reciprocal(quotient[:, :], twice[:, :]).then_inc(s_root, 1)
                            dve.wait_ge(s_root, h * (3 * ROUNDS + 1) + 3 * n + 2)
                            nc.vector.scalar_tensor_tensor(quotient[:, :], quotient[:, :], 2.0, peak[:, :, 1], ALU.mult, ALU.mult).then_inc(s_root, 1)
                            dve.wait_ge(s_root, h * (3 * ROUNDS + 1) + 3 * n + 3)
                            nc.vector.scalar_tensor_tensor(twice[:, :], twice[:, :], 0.5, quotient[:, :], ALU.mult, ALU.add).then_inc(s_root, 1)
                        dve.wait_ge(s_root, (h + 1) * (3 * ROUNDS + 1))
                        nc.vector.scalar_tensor_tensor(peak[:, :, 0], twice[:, :], REACH / 2, peak[:, :, 0], ALU.mult, ALU.add).then_inc(s_bound, 1)
                        dve.wait_ge(s_bound, h * 2 + 1)
                        nc.vector.tensor_reduce(bound[:, :], peak[:, :, 0], AX.X, ALU.max).then_inc(s_bound, 1)
                        dve.wait_ge(s_bound, h * 2 + 2)
                        if not first_head(h):
                            dve.wait_ge(s_minus, h)
                        nc.vector.tensor_scalar(minus_next[:, :], bound[:, :], -1.0, None, ALU.mult).then_inc(s_ready, 1)
                    elif at == EXACT:
                        bits = nc.vector.value_load(bound[0:1, 0:1].bitcast(I32))
                        with dve.If(bits > SAFE_BITS):
                            exact(h)

                def take(h, g):
                    if not first_head(h):
                        dve.wait_ge(s_score, h * NZ if g else h * NZ - NL)
                    nc.vector.tensor_copy(r[g][1][:, :], r_next[g][1][:, :].bitcast(F32)).then_inc(s_take_low[g], 1)

                def head(h, before=True, after=True):
                    for t in range(NZ):
                        dve.wait_ge(s_high, h * NZ + (t + 1))
                        nc.vector.tensor_tensor(low[t % 2][:, :], exps[t % 2][:, :], high[t % 2][:, :].bitcast(F32), ALU.subtract).then_inc(s_low, 1)
                        if t == TAKE_LATENTS:
                            take(h, 1)
                        if before:
                            finish(h - 1, t)
                        if after:
                            prepare(h + 1, t)
                            if t == TAKE_MEDIA:
                                take(h + 1, 0)

                step(nc.vector.memset(ones_in[:, :], 1.0), s_set)
                step(nc.vector.tensor_copy(ones[:, :], ones_in[:, :]), s_set)
                step(nc.vector.memset(mean[:, :], 1.0 / P), s_set)
                dve.wait_ge(s_bias, 4 * 16)
                step(nc.vector.tensor_scalar(biases[:, 1:3, :], biases[:, 1:3, :], 1.0 / P, None, ALU.mult), s_set)
                for at in range(NZ):
                    prepare(0, at)
                take(0, 0)
                head(0, before=False)
                with dve.Fori(1, H1 - 1) as h:
                    head(h)
                head(H1 - 1, after=False)
                for at in range(NZ):
                    finish(H1 - 1, at)
                dve.wait_ge(s_added, H1)
                step(nc.vector.tensor_tensor(x[:, :, :], x[:, :, :], b_o[:, :].unsqueeze(1).to_broadcast([P, NT, P]), ALU.add), s_end)


def first_head(h):
    return isinstance(h, int) and h == 0


STAGES = [linear_attention, cross_attention, mixture0, lstm_step, latent_attention, mixture1]


def decoder(nc, a, out):
    with nc.allow_non_contiguous_dma(reason="columns of biases"):
        program(nc, a, out)


def program(nc, a, out):
    with ExitStack() as stack:
        kept = {
            "x": stack.enter_context(nc.sbuf_tensor("x", [P, NT, P], F32)),
            "ident": stack.enter_context(nc.sbuf_tensor("ident", [P, P], F32)),
        }
        ps = stack.enter_context(nc.psum_tensor("ps", [P, 8, HALF], F32))
        s_start = nc.alloc_semaphore("start_loaded")
        with nc.Block() as block:
            @block.sync
            def _(sp):
                sp.dma_start(kept["x"][:, :, :], a["x"][0].rearrange("(t p) c -> p t c", p=P)).then_inc(s_start, 16)
                sp.dma_start(kept["ident"][:, :], a["ident"]).then_inc(s_start, 16)
                sp.wait_ge(s_start, 2 * 16)
        for stage in STAGES:
            stage(nc, kept, ps, a)
            nc.clear_and_free_semaphores(list(Memory.taken))
            Memory.taken.clear()
            nc.all_engine_barrier()
        s_out = nc.alloc_semaphore("out_written")
        with nc.Block() as block:
            @block.sync
            def _(sp):
                sp.dma_start(out[0].rearrange("(t p) c -> p t c", p=P), kept["x"][:, :, :]).then_inc(s_out, 16)
                sp.wait_ge(s_out, 16)


def shape_constants():
    def angles(rows, length):
        inv_freq = np.float32(1.0) / np.float32(10000.0) ** (np.arange(0, D0, 2, dtype=np.float32) / np.float32(D0))
        pos = np.float32(10.0) * (np.arange(length, dtype=np.float32) / np.float32(length))
        ang = pos[rows][..., None] * inv_freq
        return np.stack([np.cos(ang), np.sin(ang)], axis=-2).astype(np.float32)

    def before(n):
        return np.broadcast_to(np.tril(np.ones((n, n), np.float32), -1), (P, n, n)).copy()

    def picks(experts, hidden):
        unit = np.arange(experts * hidden) // hidden
        rows = np.arange(P)[:, None]
        return ((rows == unit) | (rows == unit + 32)).astype(np.float32).reshape(P, -1, P)

    p = np.arange(P)
    keys = np.stack([t * P + p if t < NK - 1 else LAST + p for t in range(NK)], axis=1)
    return {
        "ident": np.eye(P, dtype=np.float32),
        "tri": np.triu(np.ones((P, P), np.float32)),
        "rope_q": angles(np.stack([t * P + p for t in range(NT)], axis=1), T),
        "rope_k": angles(keys, LC),
        "fresh": (p >= REPEATED).astype(np.float32)[:, None].copy(),
        "order8": before(8),
        "order4": before(4),
        "picks0": picks(8, 176),
        "picks1": picks(32, 64),
        "head_rows": (p[:, None] // ROW == np.arange(G0)[None, :]).astype(np.float32),
    }


def kernel(**inputs):
    import concourse.bacc as bacc
    from concourse.bass_utils import run_bass_kernel_spmd

    nc = bacc.Bacc("TRN2", target_bir_lowering=False, num_devices=1)
    arrays, aps = {}, {}
    for name, array in {**inputs, **shape_constants()}.items():
        array = np.ascontiguousarray(array)
        if array.dtype == np.bool_:
            array = array.view(np.uint8)
        arrays[f"in_{name}"] = array
        aps[name] = nc.dram_tensor(f"in_{name}", array.shape, mybir.dt.from_np(array.dtype), kind="ExternalInput").ap()
    out = nc.dram_tensor("out", (1, T, P), F32, kind="ExternalOutput").ap()
    decoder(nc, aps, out)
    result = run_bass_kernel_spmd(nc, [arrays], core_ids=[0])
    return result.results[0]["out"]
```

```python
from contextlib import ExitStack

import numpy as np
import concourse.bass as bass
from concourse import mybir

F32 = mybir.dt.float32
F32R = mybir.dt.float32r
I32 = mybir.dt.int32
U8 = mybir.dt.uint8
ALU = mybir.AluOpType
ACT = mybir.ActivationFunctionType
AX = mybir.AxisListType

P = 128
T = 1024
NT = T // P
HALF = 512
LC = 6404
NK = -(-LC // P)
LAST = LC - P
REPEATED = NK * P - LC
LN_EPS = 1e-5
DEN_EPS = 1e-6
H0, D0 = 16, 8
G0 = 4
NG = H0 // G0
ROW = 32
U0 = 3
NI = NK // U0
SAFE = 40.0
SAFE_BITS = int(np.float32(SAFE).view(np.int32))
MASKED = -1e30


def stepper(engine):
    done = {}

    def step(instruction, semaphore, wait=True):
        instruction.then_inc(semaphore, 1)
        done[semaphore.name] = done.get(semaphore.name, 0) + 1
        if wait:
            engine.wait_ge(semaphore, done[semaphore.name])

    return step


def layer_norm(nc, dve, step, s_chain, stats, moments, src, dst, eps_done, root_done, out_done, n=NT, first=0):
    for t in range(n):
        step(nc.vector.bn_stats(stats[:, t, :], src[:, t, :]), s_chain, wait=t == n - 1)
    for t in range(n):
        step(nc.vector.bn_aggr(moments[:, t, :], stats[:, t, :]), s_chain, wait=t == n - 1)
    step(nc.vector.tensor_scalar(moments[:, 0:n, 1], moments[:, 0:n, 1], LN_EPS, None, ALU.add), eps_done)
    dve.wait_ge(root_done, first + 1)
    step(nc.vector.reciprocal(moments[:, 0:n, 1], moments[:, 0:n, 1]), s_chain)
    for t in range(n):
        step(nc.vector.tensor_scalar(dst[:, t, :], src[:, t, :], moments[:, t, 0:1], moments[:, t, 1:2],
                                     ALU.subtract, ALU.mult), out_done, wait=t == n - 1)


def root(nc, act, moments, eps_done, root_done, n=NT, first=0):
    act.wait_ge(eps_done, first + 1)
    nc.scalar.activation(moments[:, 0:n, 1], moments[:, 0:n, 1], ACT.Sqrt).then_inc(root_done, 1)


def transpose_tiles(nc, pe, bank, src, ident, done):
    for t in range(NT):
        last = nc.tensor.transpose(bank[:, t * P:(t + 1) * P], src[:, t, :], ident[:, :])
        if t % 4 == 3:
            last.then_inc(done, 1)


def columns(ap, width=P):
    return ap.rearrange("(c p) -> p c", p=width)


def spread(ap):
    return ap.rearrange("(a n) -> a n", a=1).to_broadcast([P, ap.shape[0]])


class Memory:

    taken = []

    def __init__(self, nc, stack, stage):
        self.nc, self.stack, self.stage = nc, stack, stage

    def sb(self, name, shape, dtype=F32):
        return self.stack.enter_context(self.nc.sbuf_tensor(f"{self.stage}_{name}", shape, dtype))

    def sem(self, name):
        semaphore = self.nc.alloc_semaphore(f"{self.stage}_{name}")
        self.taken.append(semaphore)
        return semaphore


def linear_attention(nc, kept, ps, a):
    with ExitStack() as stack:
        m = Memory(nc, stack, "lin")
        qkv_w, gate_w = m.sb("qkv_w", [P, 3 * P]), m.sb("gate_w", [P, P])
        biases = m.sb("biases", [P, 6])
        v_bias = m.sb("v_bias", [P, P])
        stats, moments, moments2 = m.sb("stats", [P, NT, 6]), m.sb("moments", [P, NT, 2]), m.sb("moments2", [P, NT, 2])
        normed, normed2 = m.sb("normed", [P, NT, P]), m.sb("normed2", [P, NT, P])
        xn = m.sb("xn", [P, T])
        q, k, gate, small = (m.sb(n, [P, T]) for n in ("q", "k", "gate", "small"))
        small_k = m.sb("small_k", [P, T])
        v = m.sb("v", [P, NT, P + 1])
        scores = m.sb("scores", [P, NT, T])
        den = m.sb("den", [P, NT])
        s_load, s_x = m.sem("loaded"), m.sem("x_loaded")
        s_vec, s_eps, s_root, s_norm, s_norm2 = (m.sem(n) for n in ("vector_step", "variance", "root", "normed", "normed2"))
        s_eps2, s_root2 = m.sem("variance2"), m.sem("root2")
        s_turned, s_xn_a, s_xn_v = m.sem("turned"), m.sem("xn_scalar"), m.sem("xn_vector")
        s_proj, s_gate, s_pre, s_exp, s_qk, s_v = (m.sem(n) for n in ("projected", "gate", "pre_elu", "exps", "q_k", "v"))
        s_score, s_sc, s_sum, s_x2 = (m.sem(n) for n in ("scores", "scores_kept", "sums", "x_done"))
        s_cp = m.sem("scores_copied")
        x, ident, tri = kept["x"], kept["ident"], m.sb("tri", [P, P])
        bank = ps[:, :, :].rearrange("p b c -> p (b c)")
        pairs = [(s, c) for s in range(NT) for c in range(s // 4, 2)]

        with nc.Block() as block:
            @block.sync
            def _(sp):
                sp.dma_start(x[:, :, :], a["x"][0].rearrange("(t p) c -> p t c", p=P)).then_inc(s_x, 16)
                sp.dma_start(ident[:, :], a["ident"]).then_inc(s_load, 16)
                sp.dma_start(qkv_w[:, :], a["L0_attn_qkv_w"]).then_inc(s_load, 16)
                sp.dma_start(gate_w[:, :], a["L0_attn_gate_w"]).then_inc(s_load, 16)
                sp.dma_start(v_bias[:, :], spread(a["L0_attn_qkv_b"][2 * P:3 * P])).then_inc(s_load, 16)
                sp.dma_start(biases[:, 0:3], columns(a["L0_attn_qkv_b"])).then_inc(s_load, 16)
                sp.dma_start(biases[:, 3:4], columns(a["L0_attn_gate_b"])).then_inc(s_load, 16)
                sp.dma_start(biases[:, 4:5], columns(a["L0_attn_ln_g"])).then_inc(s_load, 16)
                sp.dma_start(biases[:, 5:6], columns(a["L0_attn_ln_b"])).then_inc(s_load, 16)
                sp.dma_start(tri[:, :], a["tri"]).then_inc(s_load, 16)
                sp.wait_ge(s_load, 9 * 16)

            @block.scalar
            def _(act):
                root(nc, act, moments, s_eps, s_root)
                root(nc, act, moments2, s_eps2, s_root2)
                act.wait_ge(s_load, 9 * 16)
                act.wait_ge(s_turned, 1)
                nc.scalar.activation(xn[:, 0:HALF], bank[:, 0:HALF], ACT.Identity, bias=biases[:, 5:6],
                                     scale=biases[:, 4:5]).then_inc(s_xn_a, 1)
                act.wait_ge(s_proj, 2)
                nc.scalar.activation(gate[:, :], bank[:, 2 * T:3 * T], ACT.Sigmoid, bias=biases[:, 3:4]).then_inc(s_gate, 1)
                act.wait_ge(s_pre, 1)
                nc.scalar.activation(small[:, :], small[:, :], ACT.Exp).then_inc(s_exp, 1)
                act.wait_ge(s_pre, 2)
                nc.scalar.activation(small_k[:, :], small_k[:, :], ACT.Exp).then_inc(s_exp, 1)
                for n, (s, c) in enumerate(pairs):
                    if c * 4 > s:
                        act.wait_ge(s_score, n + 1)
                        nc.scalar.activation(scores[:, s, c * HALF:(c + 1) * HALF], ps[:, n % 4, :], ACT.Copy).then_inc(s_cp, 1)

            @block.vector
            def _(dve):
                step = stepper(dve)
                step(nc.vector.memset(v[:, :, P:P + 1], 1.0), s_vec, wait=False)
                dve.wait_ge(s_x, 16)
                layer_norm(nc, dve, step, s_vec, stats, moments, x, normed, s_eps, s_root, s_norm)
                layer_norm(nc, dve, step, s_vec, stats, moments2, normed, normed2, s_eps2, s_root2, s_norm2)
                dve.wait_ge(s_load, 9 * 16)
                dve.wait_ge(s_turned, 2)
                step(nc.vector.tensor_scalar(xn[:, HALF:T], bank[:, HALF:T], biases[:, 4:5], biases[:, 5:6],
                                             ALU.mult, ALU.add), s_xn_v)
                dve.wait_ge(s_proj, 1)
                step(nc.vector.tensor_scalar(q[:, :], bank[:, T:2 * T], biases[:, 0:1], None, ALU.add), s_vec)
                step(nc.vector.tensor_scalar(small[:, :], q[:, :], 0.0, None, ALU.min), s_pre)
                dve.wait_ge(s_proj, 3)
                dve.wait_ge(s_gate, 1)
                step(nc.vector.scalar_tensor_tensor(k[:, :], bank[:, 3 * T:4 * T], biases[:, 1:2], gate[:, :],
                                                    ALU.add, ALU.mult), s_vec)
                step(nc.vector.tensor_scalar(small_k[:, :], k[:, :], 0.0, None, ALU.min), s_pre)
                dve.wait_ge(s_exp, 1)
                step(nc.vector.scalar_tensor_tensor(q[:, :], q[:, :], 0.0, small[:, :], ALU.max, ALU.add), s_qk)
                dve.wait_ge(s_exp, 2)
                step(nc.vector.scalar_tensor_tensor(k[:, :], k[:, :], 0.0, small_k[:, :], ALU.max, ALU.add), s_qk)
                dve.wait_ge(s_proj, 4)
                step(nc.vector.tensor_tensor(v[:, :, 0:P], bank[:, 0:T].rearrange("p (t c) -> p t c", c=P),
                                             v_bias[:, :].unsqueeze(1).to_broadcast([P, NT, P]), ALU.add), s_v)
                for n, (s, c) in enumerate(pairs):
                    if c * 4 > s:
                        continue
                    dve.wait_ge(s_score, n + 1)
                    d, e = s * P, (s + 1) * P
                    b = d - c * HALF
                    if e < (c + 1) * HALF:
                        step(nc.vector.tensor_copy(scores[:, s, e:(c + 1) * HALF], ps[:, n % 4, b + P:HALF]), s_vec, wait=False)
                    step(nc.vector.tensor_tensor(scores[:, s, d:e], ps[:, n % 4, b:b + P], tri[:, :], ALU.mult), s_sc)
                for t in range(NT):
                    dve.wait_ge(s_sum, t + 1)
                    sums = ps[:, 4 + t % 4, 0:P + 1]
                    step(nc.vector.tensor_scalar(den[:, t:t + 1], sums[:, P:P + 1], DEN_EPS, None, ALU.add), s_vec)
                    step(nc.vector.reciprocal(den[:, t:t + 1], den[:, t:t + 1]), s_vec)
                    step(nc.vector.scalar_tensor_tensor(x[:, t, :], sums[:, 0:P], den[:, t:t + 1], x[:, t, :],
                                                        ALU.mult, ALU.add), s_x2, wait=False)

            @block.tensor
            def _(pe):
                pe.wait_ge(s_load, 9 * 16)
                pe.wait_ge(s_norm2, NT)
                transpose_tiles(nc, pe, bank, normed2, ident, s_turned)
                pe.wait_ge(s_xn_a, 1)
                pe.wait_ge(s_xn_v, 1)
                for w, b in ((qkv_w[:, 0:P], 2), (gate_w[:, :], 4), (qkv_w[:, P:2 * P], 6)):
                    for c in range(2):
                        last = nc.tensor.matmul(ps[:, b + c, :], w, xn[:, c * HALF:(c + 1) * HALF], start=True, stop=True)
                    last.then_inc(s_proj, 1)
                for t in range(NT):
                    last = nc.tensor.matmul(bank[:, t * P:(t + 1) * P], xn[:, t * P:(t + 1) * P], qkv_w[:, 2 * P:3 * P],
                                            start=True, stop=True)
                last.then_inc(s_proj, 1)
                pe.wait_ge(s_qk, 2)
                pe.wait_ge(s_v, 1)
                diagonal = off = 0
                kept_by = []
                for s, c in pairs:
                    kept_by.append((diagonal, off))
                    diagonal, off = (diagonal, off + 1) if c * 4 > s else (diagonal + 1, off)
                kept_by.append((diagonal, off))
                for n, (s, c) in enumerate(pairs):
                    if n >= 4:
                        for semaphore, count in zip((s_sc, s_cp), kept_by[n - 3]):
                            if count:
                                pe.wait_ge(semaphore, count)
                    lo = max(s * P, c * HALF)
                    nc.tensor.matmul(ps[:, n % 4, lo - c * HALF:HALF], k[:, s * P:(s + 1) * P], q[:, lo:(c + 1) * HALF],
                                     start=True, stop=True).then_inc(s_score, 1)
                pe.wait_ge(s_sc, NT)
                pe.wait_ge(s_cp, len(pairs) - NT)
                for t in range(NT):
                    if t >= 4:
                        pe.wait_ge(s_x2, t - 3)
                    for s in range(t + 1):
                        last = nc.tensor.matmul(ps[:, 4 + t % 4, 0:P + 1], scores[:, s, t * P:(t + 1) * P], v[:, s, :],
                                                start=s == 0, stop=s == t)
                    last.then_inc(s_sum, 1)


def context_keys(nc, kept, ps, a, stack):
    m = Memory(nc, stack, "ctx")
    key_rows = m.sb("key_rows", [P, NG, NK * P], F32R)
    values = m.sb("values", [P, NK, H0, D0 + 1])
    key_bound = m.sb("key_bound", [P, H0])
    kept.update(key_rows=key_rows, values=values, key_bound=key_bound)
    with ExitStack() as own:
        m = Memory(nc, own, "ctxb")
        rope = m.sb("rope", [P, NK, 2, D0 // 2])
        mask_u8, mask, mask_bias, fresh = m.sb("mask_u8", [P, NK], U8), m.sb("mask", [P, NK]), m.sb("mask_bias", [P, NK], F32R), m.sb("fresh", [P, 1])
        w_kv, b_kv = m.sb("w_kv", [P, 2 * P]), m.sb("b_kv", [P, 2 * P])
        rows, kv, rotated, squares = ([m.sb(f"{name}{k}", [P, U0, width]) for k in range(2)] for name, width in (
            ("rows", P), ("kv", 2 * P), ("rotated", P), ("squares", P)))
        packed = [m.sb(f"packed{k}", [P, U0, NG * G0, ROW], F32R) for k in range(2)]
        turned = m.sb("turned", [P, U0, P])
        unit = m.sb("unit", [P, P], F32R)
        part = [m.sb(f"part{n}", [P, U0, H0, D0 // 2]) for n in range(4)]
        norms, best = m.sb("norms", [P, U0, H0]), m.sb("best", [P, U0, H0])
        s_load, s_rows = m.sem("loaded"), [m.sem(f"rows_loaded{k}") for k in range(2)]
        s_turn, s_turned, s_kv, s_kv_kept, s_keys, s_keys_kept = (m.sem(n) for n in (
            "rows_turned", "turned_kept", "kv_projected", "kv_kept", "keys_turned", "keys_kept"))
        s_prod, s_prod_odd, s_even, s_odd, s_values = (m.sem(n) for n in ("products", "products_odd", "even", "odd", "values"))
        s_ones, s_mask, s_high, s_second, s_low, s_packed = (m.sem(n) for n in ("packed_set", "mask", "keys_high", "keys_high_again", "keys_low", "mask_packed"))
        s_sq, s_norms, s_best, s_norm, s_all, s_bound = (m.sem(n) for n in ("squares", "norms", "best", "best_of_tiles", "bound_of_all", "bound_root"))
        s_weight = m.sem("value_mask")
        ctx = a["ctx_1024"][0]
        ident = kept["ident"]

        def steps(engine, each):
            for j in range(3):
                each(j, j % 2)
            with engine.Fori(0, (NI - 5) // 2) as i:
                each(i * 2 + 3, 1)
                each(i * 2 + 4, 0)
            for j in range(NI - 2, NI):
                each(j, j % 2)

        def later(j, n):
            return not isinstance(j, int) or j >= n

        def by_head(ap):
            return ap.rearrange("p n (h d) -> p n h d", h=H0)

        with nc.Block() as block:
            @block.sync
            def _(sp):
                mask_rows = a["mask_BxS2_bf1"][0]
                sp.dma_start(w_kv[:, :], a["L0_xattn_Wkv"]).then_inc(s_load, 16)
                sp.dma_start(rope[:, :, :, :], a["rope_k"]).then_inc(s_load, 16)
                sp.dma_start(b_kv[:, :], spread(a["L0_xattn_bkv"])).then_inc(s_load, 16)
                sp.dma_start(fresh[:, :], a["fresh"]).then_inc(s_load, 16)
                sp.dma_start(mask_u8[:, 0:NK - 1], mask_rows[0:(NK - 1) * P].rearrange("(t p) -> p t", p=P)).then_inc(s_load, 16)
                sp.dma_start(mask_u8[:, NK - 1:NK], columns(mask_rows[LAST:LC])).then_inc(s_load, 16)
                for j in range(NI):
                    if j >= 2:
                        sp.wait_ge(s_turn, j - 1)
                    if j < NI - 1:
                        sp.dma_start(rows[j % 2][:, :, :], ctx[j * U0 * P:(j + 1) * U0 * P, :].rearrange("(t p) c -> p t c", p=P)).then_inc(s_rows[j % 2], 16)
                    else:
                        sp.dma_start(rows[0][:, 0:U0 - 1, :], ctx[j * U0 * P:(NK - 1) * P, :].rearrange("(t p) c -> p t c", p=P)).then_inc(s_rows[0], 16)
                        sp.dma_start(rows[0][:, U0 - 1, :], ctx[LAST:LC, :]).then_inc(s_rows[0], 16)
                sp.wait_ge(s_load, 6 * 16)

            @block.tensor
            def _(pe):
                def turn_rows(j, k):
                    for n in range(U0):
                        last = nc.tensor.transpose(ps[:, 0, n * P:(n + 1) * P], rows[k][:, n, :], ident[:, :])
                    last.then_inc(s_turn, 1)

                def project(j):
                    if later(j, 1):
                        pe.wait_ge(s_kv_kept, j)
                    pe.wait_ge(s_turned, j + 1)
                    for n in range(U0):
                        last = nc.tensor.matmul(ps[:, 1 + n, 0:2 * P], turned[:, n, :], w_kv[:, :], start=True, stop=True)
                    last.then_inc(s_kv, 1)

                def turn_keys(j, k):
                    pe.wait_ge(s_second, j + 1)
                    pe.wait_ge(s_low, j + 1)
                    pe.wait_ge(s_packed, j + 1)
                    for n in range(U0):
                        if later(j, 1):
                            pe.wait_ge(s_keys_kept, j * U0 + (n - U0 + 1))
                        for g in range(NG):
                            last = nc.tensor.matmul(ps[:, 4 + n, g * P:(g + 1) * P],
                                                    packed[k][:, n, g * G0:(g + 1) * G0, :].rearrange("p h r -> p (h r)"),
                                                    unit[:, :], start=True, stop=True)
                        last.then_inc(s_keys, 1)

                def each(j, k):
                    project(j)
                    if isinstance(j, int):
                        if j + 1 < NI:
                            pe.wait_ge(s_rows[1 - k], 16 * ((j + 1) // 2 + 1 + (j + 1 == NI - 1)))
                            turn_rows(j + 1, 1 - k)
                    else:
                        pe.wait_ge(s_rows[1 - k], (j + (1 + k)) * 8 + 8)
                        turn_rows(j + 1, 1 - k)
                    if later(j, 2):
                        turn_keys(j - 2, k)

                pe.wait_ge(s_load, 6 * 16)
                pe.wait_ge(s_rows[0], 16)
                turn_rows(0, 0)
                steps(pe, each)
                turn_keys(NI - 2, 1)
                turn_keys(NI - 1, 0)

            @block.scalar
            def _(act):
                def keep_turned(j):
                    act.wait_ge(s_turn, j + 1)
                    nc.scalar.activation(turned[:, :, :].rearrange("p n c -> p (n c)"), ps[:, 0, 0:U0 * P], ACT.Copy).then_inc(s_turned, 1)

                def pack_again(j, k):
                    act.wait_ge(s_high, j + 1)
                    source = packed[k][:, :, :, 0:D0].bitcast(F32).rearrange("p n h d -> p (n h) d")
                    nc.scalar.activation(packed[k][:, :, :, D0:2 * D0].rearrange("p n h d -> p (n h) d"), source, ACT.Copy).then_inc(s_second, 1)
                    if later(j, 2):
                        act.wait_ge(s_norms, j - 1)
                    nc.scalar.activation(squares[k][:, :, :], rotated[k][:, :, :], ACT.Square).then_inc(s_sq, 1)

                def keep_keys(j):
                    for n in range(U0):
                        act.wait_ge(s_keys, j * U0 + (n + 1))
                        nc.scalar.activation(key_rows[:, :, bass.ds(j * (U0 * P) + n * P, P)],
                                             ps[:, 4 + n, :].rearrange("p (g c) -> p g c", g=NG), ACT.Copy).then_inc(s_keys_kept, 1)

                def each(j, k):
                    keep_turned(j)
                    if later(j, 2):
                        pack_again(j - 2, k)
                    if later(j, 3):
                        keep_keys(j - 3)

                act.wait_ge(s_ones, 6)
                steps(act, each)
                pack_again(NI - 2, 1)
                keep_keys(NI - 3)
                keep_keys(NI - 2)
                pack_again(NI - 1, 0)
                keep_keys(NI - 1)
                act.wait_ge(s_all, 1)
                nc.scalar.activation(key_bound[:, :], key_bound[:, :], ACT.Sqrt).then_inc(s_bound, 1)

            @block.gpsimd
            def _(pool):
                def each(j, k):
                    pool.wait_ge(s_kv_kept, j + 1)
                    if later(j, 1):
                        pool.wait_ge(s_odd, j)
                    even, odd = (by_head(kv[k][:, :, n:P:2]) for n in (0, 1))
                    cos, sin = (rope[:, bass.ds(j * U0, U0), n, :].unsqueeze(2).to_broadcast([P, U0, H0, D0 // 2]) for n in (0, 1))
                    nc.gpsimd.tensor_tensor(part[2][:, :, :, :], even, sin, ALU.mult).then_inc(s_prod_odd, 1)
                    nc.gpsimd.tensor_tensor(part[3][:, :, :, :], odd, cos, ALU.mult).then_inc(s_prod_odd, 1)
                    pool.wait_ge(s_prod_odd, j * 2 + 2)
                    if later(j, 2):
                        pool.wait_ge(s_low, j - 1)
                        pool.wait_ge(s_sq, j - 1)
                    nc.gpsimd.tensor_tensor(by_head(rotated[k][:, :, 1:P:2]), part[2][:, :, :, :], part[3][:, :, :, :], ALU.add).then_inc(s_odd, 1)
                    if not later(j, 1):
                        pool.wait_ge(s_mask, 3)
                    tiles = bass.ds(j * U0, U0)
                    nc.gpsimd.tensor_tensor(values[:, tiles, :, 0:D0], by_head(kv[k][:, :, P:2 * P]),
                                            by_head(mask[:, tiles].unsqueeze(2).to_broadcast([P, U0, P])), ALU.mult).then_inc(s_values, 1)

                steps(pool, each)
                pool.wait_ge(s_norm, 1)
                nc.gpsimd.partition_all_reduce(key_bound[:, :], best[:, 0, :], P, bass.bass_isa.ReduceOp.max).then_inc(s_all, 1)

            @block.vector
            def _(dve):
                step = stepper(dve)
                step(nc.vector.tensor_copy(unit[:, :], ident[:, :]), s_ones)
                step(nc.vector.memset(turned[:, :, :], 0.0), s_ones)
                for k in range(2):
                    flat = packed[k][:, :, :, :].rearrange("p n h r -> p (n h r)")
                    step(nc.vector.tensor_copy(flat, turned[:, 0, 0:1].to_broadcast([P, U0 * NG * G0 * ROW])), s_ones)
                    step(nc.vector.tensor_scalar(packed[k][:, :, :, 3 * D0:3 * D0 + 2], packed[k][:, :, :, 3 * D0:3 * D0 + 2].bitcast(F32), 1.0, None, ALU.add), s_ones)
                step(nc.vector.memset(best[:, :, :], 0.0), s_ones)
                dve.wait_ge(s_load, 6 * 16)
                step(nc.vector.tensor_copy(mask[:, :], mask_u8[:, :]), s_mask)
                step(nc.vector.tensor_scalar(mask[:, NK - 1:NK], mask[:, NK - 1:NK], fresh[:, 0:1], None, ALU.mult), s_mask)
                step(nc.vector.tensor_scalar(mask_bias[:, :], mask[:, :], -MASKED, MASKED, ALU.mult, ALU.add), s_mask)
                step(nc.vector.tensor_copy(values[:, :, :, D0], mask[:, :].unsqueeze(2).to_broadcast([P, NK, H0])), s_weight)

                def rotate(j, k):
                    dve.wait_ge(s_kv, j + 1)
                    if later(j, 2):
                        dve.wait_ge(s_values, j - 1)
                    nc.vector.tensor_tensor(kv[k][:, :, :], ps[:, 1:1 + U0, 0:2 * P], b_kv[:, :].unsqueeze(1).to_broadcast([P, U0, 2 * P]),
                                            ALU.add).then_inc(s_kv_kept, 1)
                    dve.wait_ge(s_kv_kept, j + 1)
                    even, odd = (by_head(kv[k][:, :, n:P:2]) for n in (0, 1))
                    cos, sin = (rope[:, bass.ds(j * U0, U0), n, :].unsqueeze(2).to_broadcast([P, U0, H0, D0 // 2]) for n in (0, 1))
                    nc.vector.tensor_tensor(part[0][:, :, :, :], even, cos, ALU.mult).then_inc(s_prod, 1)
                    nc.vector.tensor_tensor(part[1][:, :, :, :], odd, sin, ALU.mult).then_inc(s_prod, 1)
                    dve.wait_ge(s_prod, j * 2 + 2)
                    if later(j, 2):
                        dve.wait_ge(s_sq, j - 1)
                    nc.vector.tensor_tensor(by_head(rotated[k][:, :, 0:P:2]), part[0][:, :, :, :], part[1][:, :, :, :], ALU.subtract).then_inc(s_even, 1)

                def pack(j, k):
                    heads = rotated[k][:, :, :].rearrange("p n (h d) -> p (n h) d", h=H0)
                    rows_of = packed[k][:, :, :, :].rearrange("p n h r -> p (n h) r")
                    dve.wait_ge(s_even, j + 1)
                    dve.wait_ge(s_odd, j + 1)
                    if later(j, 2):
                        dve.wait_ge(s_keys, j * U0 - U0)
                    nc.vector.tensor_copy(rows_of[:, :, 0:D0], heads).then_inc(s_high, 1)
                    nc.vector.tensor_copy(packed[k][:, :, :, 3 * D0 + 2], mask_bias[:, bass.ds(j * U0, U0)].bitcast(F32).unsqueeze(2).to_broadcast([P, U0, H0])).then_inc(s_packed, 1)
                    dve.wait_ge(s_high, j + 1)
                    nc.vector.tensor_tensor(rows_of[:, :, 2 * D0:3 * D0], heads, rows_of[:, :, 0:D0].bitcast(F32), ALU.subtract).then_inc(s_low, 1)

                def measure(j, k):
                    dve.wait_ge(s_sq, j + 1)
                    if later(j, 1):
                        dve.wait_ge(s_best, j)
                    nc.vector.tensor_reduce(norms[:, :, :], by_head(squares[k][:, :, :]), AX.X, ALU.add).then_inc(s_norms, 1)
                    dve.wait_ge(s_norms, j + 1)
                    nc.vector.tensor_tensor(best[:, :, :], best[:, :, :], norms[:, :, :], ALU.max).then_inc(s_best, 1)

                def each(j, k):
                    rotate(j, k)
                    if later(j, 2):
                        measure(j - 2, k)
                    if later(j, 1):
                        pack(j - 1, 1 - k)

                steps(dve, each)
                measure(NI - 2, 1)
                pack(NI - 1, 0)
                measure(NI - 1, 0)
                dve.wait_ge(s_best, NI)
                nc.vector.tensor_tensor(best[:, 0, :], best[:, 0, :], best[:, 1, :], ALU.max).then_inc(s_best, 1)
                dve.wait_ge(s_best, NI + 1)
                nc.vector.tensor_tensor(best[:, 0, :], best[:, 0, :], best[:, 2, :], ALU.max).then_inc(s_norm, 1)


def cross_attention(nc, kept, ps, a):
    with ExitStack() as stack:
        context_keys(nc, kept, ps, a, stack)
        key_bound, x, ident = (kept[n] for n in ("key_bound", "x", "ident"))
        m = Memory(nc, stack, "att")
        scaled = m.sb("scaled", [P, NT, P])
        guard = m.sb("guard", [P, NT, H0])
        attended = scaled
        flag = m.sb("flag", [P, 2])
        with ExitStack() as own:
            m = Memory(nc, own, "qry")
            w_q, b_q, rope = m.sb("w_q", [P, P]), m.sb("b_q", [P, P]), m.sb("rope", [P, NT, 2, D0 // 2])
            stats, moments, normed, xn = m.sb("stats", [P, NT, 6]), m.sb("moments", [P, NT, 2]), m.sb("normed", [P, NT, P]), m.sb("xn", [P, T])
            q, squares = m.sb("q", [P, NT, P]), m.sb("squares", [P, NT, P])
            part = [m.sb(f"part{n}", [P, NT, H0, D0 // 2]) for n in range(4)]
            s_load, s_vec, s_eps, s_root, s_norm, s_turned, s_xn_a, s_xn_v, s_proj, s_sq, s_len, s_top, s_all = (m.sem(n) for n in (
                "loaded", "vector_step", "variance", "root", "normed", "turned", "xn_scalar", "xn_vector", "projected", "squares", "lengths", "top", "top_of_all"))
            bank = ps[:, :, :].rearrange("p b c -> p (b c)")
            with nc.Block() as block:
                @block.sync
                def _(sp):
                    sp.dma_start(w_q[:, :], a["L0_xattn_Wq"]).then_inc(s_load, 16)
                    sp.dma_start(b_q[:, :], spread(a["L0_xattn_bq"])).then_inc(s_load, 16)
                    sp.dma_start(rope[:, :, :, :], a["rope_q"]).then_inc(s_load, 16)
                    sp.wait_ge(s_load, 3 * 16)

                @block.scalar
                def _(act):
                    root(nc, act, moments, s_eps, s_root)
                    act.wait_ge(s_turned, 1)
                    nc.scalar.activation(xn[:, 0:HALF], bank[:, 0:HALF], ACT.Copy).then_inc(s_xn_a, 1)
                    act.wait_ge(s_sq, 1)
                    nc.scalar.activation(guard[:, :, :], guard[:, :, :], ACT.Sqrt).then_inc(s_len, 1)

                @block.tensor
                def _(pe):
                    pe.wait_ge(s_norm, NT)
                    transpose_tiles(nc, pe, bank, normed, ident, s_turned)
                    pe.wait_ge(s_load, 3 * 16)
                    pe.wait_ge(s_xn_a, 1)
                    pe.wait_ge(s_xn_v, 1)
                    for t in range(NT):
                        last = nc.tensor.matmul(bank[:, T + t * P:T + (t + 1) * P], xn[:, t * P:(t + 1) * P], w_q[:, :], start=True, stop=True)
                    last.then_inc(s_proj, 1)

                @block.vector
                def _(dve):
                    step = stepper(dve)
                    layer_norm(nc, dve, step, s_vec, stats, moments, x, normed, s_eps, s_root, s_norm)
                    dve.wait_ge(s_turned, 2)
                    step(nc.vector.tensor_copy(xn[:, HALF:T], bank[:, HALF:T]), s_xn_v)
                    dve.wait_ge(s_load, 3 * 16)
                    dve.wait_ge(s_proj, 1)
                    step(nc.vector.tensor_tensor(q[:, :, :], bank[:, T:2 * T].rearrange("p (t c) -> p t c", c=P),
                                                 b_q[:, :].unsqueeze(1).to_broadcast([P, NT, P]), ALU.add), s_vec)
                    even, odd = (q[:, :, j:P:2].rearrange("p n (h d) -> p n h d", h=H0) for j in (0, 1))
                    cos, sin = (rope[:, :, j, :].unsqueeze(2).to_broadcast([P, NT, H0, D0 // 2]) for j in (0, 1))
                    for n, (u, w) in enumerate(((even, cos), (odd, sin), (even, sin), (odd, cos))):
                        step(nc.vector.tensor_tensor(part[n][:, :, :, :], u, w, ALU.mult), s_vec, wait=n == 3)
                    for n, op in ((0, ALU.subtract), (1, ALU.add)):
                        step(nc.vector.tensor_tensor(q[:, :, n:P:2].rearrange("p n (h d) -> p n h d", h=H0),
                                                     part[2 * n][:, :, :, :], part[2 * n + 1][:, :, :, :], op), s_vec)
                    step(nc.vector.tensor_scalar(scaled[:, :, :], q[:, :, :], D0 ** -1.0, None, ALU.mult), s_vec)
                    step(nc.vector.tensor_tensor(squares[:, :, :], scaled[:, :, :], scaled[:, :, :], ALU.mult), s_vec)
                    step(nc.vector.tensor_reduce(guard[:, :, :], squares[:, :, :].rearrange("p n (h d) -> p n h d", h=H0), AX.X, ALU.add), s_sq)
                    dve.wait_ge(s_len, 1)
                    step(nc.vector.tensor_tensor(guard[:, :, :], guard[:, :, :], key_bound[:, :].unsqueeze(1).to_broadcast([P, NT, H0]), ALU.mult), s_vec)
                    step(nc.vector.tensor_reduce(flag[:, 0:1], guard[:, :, :], AX.XY, ALU.max), s_top)

                @block.gpsimd
                def _(pool):
                    pool.wait_ge(s_top, 1)
                    nc.gpsimd.partition_all_reduce(flag[:, 1:2], flag[:, 0:1], P, bass.bass_isa.ReduceOp.max).then_inc(s_all, 1)

        attend(nc, kept, ps, a, scaled, guard, attended, flag)

        with ExitStack() as own:
            m = Memory(nc, own, "prj")
            turned, w_out, b_out = m.sb("turned", [P, T]), m.sb("w_out", [P, P]), m.sb("b_out", [P, P])
            s_load = m.sem("loaded")
            s_turned, s_a, s_v, s_proj, s_vec = (m.sem(n) for n in ("turned", "kept_scalar", "kept_vector", "projected", "vector_step"))
            bank = ps[:, :, :].rearrange("p b c -> p (b c)")
            with nc.Block() as block:
                @block.sync
                def _(sp):
                    sp.dma_start(w_out[:, :], a["L0_xattn_Wo"]).then_inc(s_load, 16)
                    sp.dma_start(b_out[:, :], spread(a["L0_xattn_bo"])).then_inc(s_load, 16)
                    sp.wait_ge(s_load, 2 * 16)

                @block.tensor
                def _(pe):
                    transpose_tiles(nc, pe, bank, attended, ident, s_turned)
                    pe.wait_ge(s_load, 2 * 16)
                    pe.wait_ge(s_a, 1)
                    pe.wait_ge(s_v, 1)
                    for t in range(NT):
                        last = nc.tensor.matmul(bank[:, T + t * P:T + (t + 1) * P], turned[:, t * P:(t + 1) * P], w_out[:, :], start=True, stop=True)
                    last.then_inc(s_proj, 1)

                @block.scalar
                def _(act):
                    act.wait_ge(s_turned, 1)
                    nc.scalar.activation(turned[:, 0:HALF], bank[:, 0:HALF], ACT.Copy).then_inc(s_a, 1)

                @block.vector
                def _(dve):
                    step = stepper(dve)
                    dve.wait_ge(s_load, 2 * 16)
                    step(nc.vector.tensor_tensor(x[:, :, :], x[:, :, :], b_out[:, :].unsqueeze(1).to_broadcast([P, NT, P]), ALU.add), s_vec)
                    dve.wait_ge(s_turned, 2)
                    step(nc.vector.tensor_copy(turned[:, HALF:T], bank[:, HALF:T]), s_v)
                    dve.wait_ge(s_proj, 1)
                    step(nc.vector.tensor_tensor(x[:, :, :], bank[:, T:2 * T].rearrange("p (t c) -> p t c", c=P), x[:, :, :], ALU.add), s_vec)


def attend(nc, kept, ps, a, scaled, guard, attended, flag):
    key_rows, values, ident = kept["key_rows"], kept["values"], kept["ident"]
    NP = U0 * G0
    BODY = U0 * G0
    SG = NK * G0
    AHEAD = 7
    with ExitStack() as own:
        m = Memory(nc, own, "loop")
        head_rows = m.sb("head_rows", [P, G0])
        query_rows = m.sb("query_rows", [P, NG, T], F32R)
        key_tile = [m.sb(f"key_tile{n}", [P, G0, P], F32R) for n in range(U0)]
        value_tile = [m.sb(f"value_tile{n}", [P, G0, ROW]) for n in range(U0)]
        exps = [scaled[:, :, :].rearrange("p t c -> p (t c)")] + [m.sb(f"exps{n}", [P, T])[:, :] for n in range(1, NP)]
        packed = exps[NP - 1].rearrange("p (t h r) -> p t h r", h=G0, r=ROW).bitcast(F32R)
        sums = [values[:, 0:T // ROW, g * G0:(g + 1) * G0, 0:D0] for g in range(NG)]
        inverse = m.sb("inverse", [P, NT, G0])
        zero = m.sb("zero", [P, 1])
        row_max, chunk_max, new_guard = m.sb("row_max", [P, NT, G0]), m.sb("chunk_max", [P, NT, G0]), m.sb("new_guard", [P, NT, G0])
        s_load, s_set, s_constant, s_high, s_packed, s_turned, s_queries = (m.sem(n) for n in (
            "loaded", "set", "constant_rows", "high", "packed", "queries_turned", "queries"))
        s_key, s_value, s_score, s_exp, s_weighted, s_open = (m.sem(n) for n in ("key_tile", "value_tile", "scores", "exps", "weighted", "opened"))
        s_closed, s_sums, s_straight, s_back, s_inv, s_norm = (m.sem(n) for n in ("closed", "sums", "sums_straight", "sums_turned", "inverse", "normalised"))
        x_alone, x_scores, x_max, x_pack, x_packed, x_turned, x_step = (m.sem(n) for n in (
            "exact_alone", "exact_scores", "exact_max", "exact_high", "exact_packed", "exact_turned", "exact_step"))
        CHUNK = U0 * P
        two_banks = ps[:, 0:2, :].rearrange("p b c -> p (b c)")

        def turn_queries(semaphore):
            for t in range(NT):
                last = nc.tensor.transpose(ps[:, t // 4, (t % 4) * P:(t % 4 + 1) * P],
                                           packed[:, t, :, :].bitcast(F32).rearrange("p h r -> p (h r)"), ident[:, :])
            last.then_inc(semaphore, 1)

        with nc.Block() as block:
            @block.sync
            def _(sp):
                sp.dma_start(head_rows[:, :], a["head_rows"]).then_inc(s_load, 16)
                sp.wait_ge(s_load, 16)

            @block.tensor
            def _(pe):
                def scores(g, i, c):
                    if not (isinstance(g, int) and g == 0 and isinstance(i, int) and i == 0 and c < 3):
                        pe.wait_ge(s_exp, g * SG + i * BODY + (c - 2))
                    if c % G0 == 0:
                        pe.wait_ge(s_key, g * NK + i * U0 + (c // G0 + 1))
                    for b in range(2):
                        last = nc.tensor.matmul(ps[:, 2 * (c % 3) + b, :], key_tile[c // G0 % U0][:, c % G0, :],
                                                query_rows[:, g, b * HALF:(b + 1) * HALF], start=True, stop=True)
                    last.then_inc(s_score, 1)

                def weigh(g, i, n, b):
                    if b == 0:
                        pe.wait_ge(s_value, g * NK + i * U0 + (n + 1))
                        pe.wait_ge(s_exp, g * SG + i * BODY + G0 * (n + 1))
                    for h in range(G0):
                        last = nc.tensor.matmul(ps[h * ROW:(h + 1) * ROW, 6 + b, :], value_tile[n][:, h, :],
                                                exps[n * G0 + h][:, b * HALF:(b + 1) * HALF], start=False, stop=False,
                                                skip_group_check=True)
                    if b:
                        last.then_inc(s_weighted, 1)

                def zeros(b, opening):
                    return nc.tensor.matmul(ps[:, 6 + b, :], ident[:, :], zero[:, :].to_broadcast([P, HALF]), start=opening, stop=not opening,
                                            skip_group_check=True)

                def body(g, i, last_of_group=False, last=False):
                    for n in range(U0):
                        for b in range(2):
                            weigh(g, i, n, b)
                            if last_of_group and n == U0 - 1 and b:
                                for bank in range(2):
                                    closed = zeros(bank, False)
                                closed.then_inc(s_closed, 1)
                            for step in range(n * G0 + AHEAD + 2 * b, n * G0 + AHEAD + 2 * b + 2):
                                if step < BODY:
                                    scores(g, i, step)
                                elif not last_of_group:
                                    scores(g, i + 1, step - BODY)
                                elif not last:
                                    scores(g + 1, 0, step - BODY)

                def open_sums():
                    for bank in range(2):
                        opened = zeros(bank, True)
                    opened.then_inc(s_open, 1)

                def group(g, last=False):
                    with pe.Fori(0, NI - 1) as i:
                        body(g, i)
                    body(g, NI - 1, last_of_group=True, last=last)

                pe.wait_ge(s_load, 16)
                bits = nc.tensor.value_load(flag[0:1, 1:2].bitcast(I32))
                pe.wait_ge(s_set, 4)
                with pe.Fori(0, NG) as g:
                    pe.wait_ge(s_packed, g * 3 + 3)
                    turn_queries(s_turned)
                    with pe.If(bits > SAFE_BITS):
                        with pe.Fori(0, NI) as i:
                            for n in range(NT * G0):
                                if n % G0 == 0:
                                    pe.wait_ge(x_alone, (g * NI + i) * NT + (n // G0 + 1))
                                if n >= 6:
                                    pe.wait_ge(x_max, (g * NI + i) * (NT * G0) + (n - 5))
                                nc.tensor.matmul(ps[:, n % 6, 0:CHUNK], key_tile[n // G0 % 2][:, n % G0, :],
                                                 key_rows[:, g, bass.ds(i * CHUNK, CHUNK)], start=True, stop=True).then_inc(x_scores, 1)
                            pe.wait_ge(x_max, (g * NI + i + 1) * (NT * G0))
                        pe.wait_ge(x_packed, g + 1)
                        turn_queries(x_turned)
                for c in range(AHEAD):
                    scores(0, 0, c)
                open_sums()
                with pe.Fori(0, NG - 1) as g:
                    group(g)
                    pe.wait_ge(s_sums, g + 1)
                    open_sums()
                group(NG - 1, last=True)
                for g in range(NG):
                    pe.wait_ge(s_straight, g + 1)
                    for t in range(NT):
                        last = nc.tensor.transpose(ps[:, 2 * g + t // 4, (t % 4) * P:(t % 4 + 1) * P],
                                                   exps[1 + g][:, t * P:(t + 1) * P], ident[:, :])
                    last.then_inc(s_back, 1)

            @block.scalar
            def _(act):
                def body(g, i, first=False):
                    for c in range(BODY):
                        act.wait_ge(s_score, g * SG + i * BODY + (c + 1))
                        if c % G0 == 0 and not first:
                            act.wait_ge(s_weighted, g * NK + i * U0 + (c // G0 - 2))
                        nc.scalar.activation(exps[c], ps[:, 2 * (c % 3):2 * (c % 3) + 2, :].rearrange("p b c -> p (b c)"),
                                             ACT.Exp).then_inc(s_exp, 1)

                body(0, 0, first=True)
                with act.Fori(1, NI) as i:
                    body(0, i)
                with act.Fori(1, NG) as g:
                    with act.Fori(0, NI) as i:
                        body(g, i)
                act.wait_ge(s_weighted, NG * NK)
                for g in range(NG):
                    act.wait_ge(s_sums, g + 1)
                    nc.scalar.activation(exps[1 + g].rearrange("p (n h d) -> p n h d", h=G0, d=D0), sums[g], ACT.Copy).then_inc(s_straight, 1)

            @block.vector
            def _(dve):
                step = stepper(dve)
                for tile in value_tile:
                    step(nc.vector.memset(tile[:, :, :], 0.0), s_set, wait=False)
                step(nc.vector.memset(zero[:, :], 0.0), s_set)
                step(nc.vector.memset(packed[:, :, :, 3 * D0 + 3:ROW].bitcast(F32), 0.0), s_constant)
                step(nc.vector.memset(packed[:, :, :, 3 * D0 + 2:3 * D0 + 3].bitcast(F32), 1.0), s_constant)
                dve.wait_ge(s_load, 16)
                bits = nc.vector.value_load(flag[0:1, 1:2].bitcast(I32))

                with dve.Fori(0, NG) as g:
                    heads = scaled[:, :, bass.ds(g * ROW, ROW)].rearrange("p t (h d) -> p t h d", h=G0)
                    guards = guard[:, :, bass.ds(g * G0, G0)]
                    high = packed[:, :, :, 0:D0]
                    nc.vector.tensor_copy(high, heads).then_inc(s_high, 1)
                    nc.vector.tensor_scalar(packed[:, :, :, 3 * D0], guards, -1.0, None, ALU.mult).then_inc(s_high, 1)
                    nc.vector.tensor_copy(packed[:, :, :, 2 * D0:3 * D0], heads).then_inc(s_packed, 1)
                    dve.wait_ge(s_high, g * 2 + 2)
                    nc.vector.tensor_tensor(packed[:, :, :, D0:2 * D0], heads, high.bitcast(F32), ALU.subtract).then_inc(s_packed, 1)
                    nc.vector.scalar_tensor_tensor(packed[:, :, :, 3 * D0 + 1], guards, -1.0, packed[:, :, :, 3 * D0].bitcast(F32),
                                                   ALU.mult, ALU.subtract).then_inc(s_packed, 1)
                    dve.wait_ge(s_turned, g + 1)
                    nc.vector.tensor_scalar(query_rows[:, g, :], two_banks, 1.0, None, ALU.mult).then_inc(s_queries, 1)
                    with dve.If(bits > SAFE_BITS):
                        dve.wait_ge(s_queries, g + 1)

                        def stage_queries(t):
                            nc.vector.tensor_tensor(key_tile[t % 2][:, :, :],
                                                    query_rows[:, g, t * P:(t + 1) * P].bitcast(F32).unsqueeze(1).to_broadcast([P, G0, P]),
                                                    head_rows[:, :].unsqueeze(2).to_broadcast([P, G0, P]), ALU.mult).then_inc(x_alone, 1)

                        nc.vector.memset(row_max[:, :, :], MASKED).then_inc(x_step, 1)
                        with dve.Fori(0, NI) as i:
                            stage_queries(0)
                            for n in range(NT * G0):
                                if n % G0 == 0 and n // G0 + 1 < NT:
                                    stage_queries(n // G0 + 1)
                                dve.wait_ge(x_scores, (g * NI + i) * (NT * G0) + (n + 1))
                                nc.vector.tensor_reduce(chunk_max[:, n // G0, n % G0:n % G0 + 1], ps[:, n % 6, 0:CHUNK], AX.X, ALU.max).then_inc(x_max, 1)
                            dve.wait_ge(x_max, (g * NI + i + 1) * (NT * G0))
                            dve.wait_ge(x_step, g * (NI + 3) + i + 1)
                            nc.vector.tensor_tensor(row_max[:, :, :], row_max[:, :, :], chunk_max[:, :, :], ALU.max).then_inc(x_step, 1)
                            dve.wait_ge(x_step, g * (NI + 3) + i + 2)
                        nc.vector.tensor_tensor(new_guard[:, :, :], row_max[:, :, :], guards, ALU.add).then_inc(x_step, 1)
                        dve.wait_ge(x_step, g * (NI + 3) + NI + 2)
                        nc.vector.tensor_scalar(packed[:, :, :, 3 * D0], new_guard[:, :, :], -1.0, None, ALU.mult).then_inc(x_pack, 1)
                        dve.wait_ge(x_pack, g + 1)
                        nc.vector.scalar_tensor_tensor(packed[:, :, :, 3 * D0 + 1], new_guard[:, :, :], -1.0, packed[:, :, :, 3 * D0].bitcast(F32),
                                                       ALU.mult, ALU.subtract).then_inc(x_packed, 1)
                        dve.wait_ge(x_turned, g + 1)
                        nc.vector.tensor_scalar(query_rows[:, g, :], two_banks, 1.0, None, ALU.mult).then_inc(x_step, 1)

                dve.wait_ge(s_queries, NG)

                def stage_keys(g, i, n):
                    nc.vector.tensor_tensor(key_tile[n][:, :, :], key_rows[:, g, bass.ds(i * CHUNK + n * P, P)].bitcast(F32).unsqueeze(1).to_broadcast([P, G0, P]),
                                            head_rows[:, :].unsqueeze(2).to_broadcast([P, G0, P]), ALU.mult).then_inc(s_key, 1)

                def stage_values(g, i, n):
                    nc.vector.tensor_scalar(value_tile[n][:, :, 0:D0 + 1], values[:, i * U0 + n, bass.ds(g * G0, G0), :], 1.0, None, ALU.mult).then_inc(s_value, 1)

                def body(g, i, last_of_group=False):
                    following = (g + 1, 0) if last_of_group else (g, i + 1)
                    for n in range(U0):
                        dve.wait_ge(s_score, g * SG + i * BODY + G0 * (n + 1))
                        stage_keys(*following, n)
                        dve.wait_ge(s_weighted, g * NK + i * U0 + (n + 1))
                        stage_values(*following, n)

                def keep_sums(g):
                    dve.wait_ge(s_closed, g + 1)
                    for h in range(G0):
                        kept_sums = nc.vector.tensor_scalar(values[:, 0:T // ROW, bass.ds(g * G0 + h, 1), 0:D0].rearrange("p n a d -> p n (a d)"),
                                                            ps[:, 6:8, :].rearrange("p b (n h d) -> p (b n) h d", h=G0, d=D0)[:, :, h, :],
                                                            1.0, None, ALU.mult)
                    kept_sums.then_inc(s_sums, 1)

                for n in range(U0):
                    stage_keys(0, 0, n)
                    stage_values(0, 0, n)
                with dve.Fori(0, NG - 1) as g:
                    with dve.Fori(0, NI - 1) as i:
                        body(g, i)
                    body(g, NI - 1, last_of_group=True)
                    keep_sums(g)
                with dve.Fori(0, NI - 1) as i:
                    body(NG - 1, i)
                keep_sums(NG - 1)
                for g in range(NG):
                    dve.wait_ge(s_back, g + 1)
                    back = ps[:, 2 * g:2 * g + 2, :].rearrange("p b (t h r) -> p (b t) h r", h=G0, r=ROW)
                    if g:
                        dve.wait_ge(s_norm, g)
                    nc.vector.reciprocal(inverse[:, :, :], back[:, :, :, D0]).then_inc(s_inv, 1)
                    dve.wait_ge(s_inv, g + 1)
                    nc.vector.tensor_tensor(attended[:, :, g * ROW:(g + 1) * ROW].rearrange("p t (h d) -> p t h d", h=G0), back[:, :, :, 0:D0],
                                            inverse[:, :, :].unsqueeze(3).to_broadcast([P, NT, G0, D0]), ALU.mult).then_inc(s_norm, 1)


def route_top2(nc, dve, step, s_vec, s_exp_in, s_exp_out, m, logits, order, weights):
    E = order.shape[1]
    peak, prob, total = m["peak"], m["prob"], m["total"]
    larger, equal, rank = m["larger"], m["equal"], m["rank"]
    step(nc.vector.tensor_reduce(peak[:, :], logits, AX.X, ALU.max), s_vec)
    step(nc.vector.tensor_tensor(prob[:, :, :], logits, peak[:, :].unsqueeze(2).to_broadcast([P, NT, E]), ALU.subtract), s_exp_in)
    dve.wait_ge(s_exp_out, 1)
    step(nc.vector.tensor_reduce(total[:, :], prob[:, :, :], AX.X, ALU.add), s_vec)
    step(nc.vector.reciprocal(total[:, :], total[:, :]), s_vec)
    step(nc.vector.tensor_tensor(prob[:, :, :], prob[:, :, :], total[:, :].unsqueeze(2).to_broadcast([P, NT, E]), ALU.mult), s_vec)
    select(nc, step, s_vec, prob, order, larger, equal, rank, 2)
    step(nc.vector.tensor_tensor(weights[:, :, :], prob[:, :, :], rank[:, :, :], ALU.mult), s_vec)
    step(nc.vector.tensor_reduce(total[:, :], weights[:, :, :], AX.X, ALU.add), s_vec)
    step(nc.vector.reciprocal(total[:, :], total[:, :]), s_vec)
    step(nc.vector.tensor_tensor(weights[:, :, :], weights[:, :, :], total[:, :].unsqueeze(2).to_broadcast([P, NT, E]), ALU.mult), s_vec)


def select(nc, step, s_vec, values, order, larger, equal, rank, top):
    E = order.shape[1]
    for t in range(NT):
        other = values[:, t, :].unsqueeze(1).to_broadcast([P, E, E])
        mine = values[:, t, :].unsqueeze(2).to_broadcast([P, E, E])
        step(nc.vector.tensor_tensor(larger[:, t, :, :], other, mine, ALU.is_gt), s_vec, wait=False)
        step(nc.vector.tensor_tensor(equal[:, t, :, :], other, mine, ALU.is_equal), s_vec, wait=t == NT - 1)
    step(nc.vector.tensor_tensor(equal[:, :, :, :].rearrange("p t e f -> p t (e f)"), equal[:, :, :, :].rearrange("p t e f -> p t (e f)"),
                                 order[:, :, :].rearrange("p e f -> p (e f)").unsqueeze(1).to_broadcast([P, NT, E * E]), ALU.mult), s_vec)
    step(nc.vector.tensor_tensor(larger[:, :, :, :], larger[:, :, :, :], equal[:, :, :, :], ALU.add), s_vec)
    step(nc.vector.tensor_reduce(rank[:, :, :], larger[:, :, :, :], AX.X, ALU.add), s_vec)
    step(nc.vector.tensor_scalar(rank[:, :, :], rank[:, :, :], float(top), None, ALU.is_lt), s_vec)


def mixture(nc, kept, ps, a, layer):
    E = 32 if layer else 8
    HID = 64 if layer else 176
    ROUTED = E * HID // P
    SHARED = 1 if layer else 3
    NH = ROUTED + SHARED
    rows_of = [P] * NH
    if not layer:
        rows_of[-1] = 2 * HID - 2 * P
    x, ident = kept["x"], kept["ident"]
    bank = ps[:, :, :].rearrange("p b c -> p (b c)")
    mid = bank[:, 2 * T:3 * T]
    with ExitStack() as stack:
        m = Memory(nc, stack, f"mix{layer}")
        gate_parts, up_parts = ([m.sb(f"w_{n}_{part}", [P, NH * P], F32R) for part in ("high", "low")] for n in ("gate", "up"))
        xn_parts = [m.sb(f"xn_{part}", [P, T], F32R) for part in ("high", "low")]
        w_down = m.sb("w_down", [P, NH, P])
        picks = m.sb("picks", [P, ROUTED, P], F32R)
        route_rows = m.sb("route_rows", [P, T], F32R)
        with ExitStack() as own:
            b = Memory(nc, own, f"mixb{layer}")
            w_gate, w_up, xn = b.sb("w_gate", [P, NH, P]), b.sb("w_up", [P, NH, P]), b.sb("xn", [P, T])
            picks_in = b.sb("picks_in", [P, ROUTED, P])
            router, order = b.sb("router", [P, E]), b.sb("order", [P, 8 if not layer else 4, 8 if not layer else 4])
            raw = b.sb("raw", [P, 3, ROUTED + SHARED, P]) if layer else None
            router_raw, router_bias = (b.sb("router_raw", [E, P]), b.sb("router_bias", [P, E])) if layer else (None, None)
            stats, moments, normed = b.sb("stats", [P, NT, 6]), b.sb("moments", [P, NT, 2]), b.sb("normed", [P, NT, P])
            packed = b.sb("packed", [P, NT, P], F32R)
            weights = b.sb("weights", [P, NT, E])
            R = order.shape[1]
            scratch = {n: b.sb(n, s) for n, s in {"peak": [P, NT], "total": [P, NT], "prob": [P, NT, E], "larger": [P, NT, R, R],
                                                  "equal": [P, NT, R, R], "rank": [P, NT, R], "choice": [P, NT, E], "best": [P, NT, 4, 8],
                                                  "top": [P, NT, 8], "left": [P, NT, E], "groups": [P, NT, 4]}.items()}
            s_raw = [b.sem(f"{n}_loaded") for n in ("gate", "up", "down")] if layer else None
            s_load, s_picks, s_late, s_vec, s_eps, s_root, s_norm, s_turned, s_xn_a, s_xn_v, s_logit, s_exp_in, s_exp_out = (b.sem(n) for n in (
                "loaded", "picks_loaded", "weights_loaded", "vector_step", "variance", "root", "normed", "turned", "xn_scalar", "xn_vector", "logits", "exp_input", "exps"))
            s_packed, s_routes, s_kept, s_w_turned, s_w_kept, s_router, s_high, s_low = (b.sem(n) for n in (
                "packed", "routes_turned", "routes_kept", "weights_turned", "weights_kept", "router_kept", "high_parts", "low_parts"))

            silu = [b.sb(f"silu{n}", [P, T]) for n in range(2)]
            hidden = [b.sb(f"hidden{n}", [P, T]) for n in range(2)]
            zero = b.sb("zero", [P, 1])
            s_zero, s_gate, s_up, s_route, s_silu, s_prod, s_hidden, s_down, s_end, s_out = (b.sem(n) for n in (
                "zero", "gate", "up", "route", "silu", "product", "hidden", "down", "end", "out_written"))

            n_loads, n_late = (3, 0) if layer else (2, 7)
            with nc.Block() as block:
                @block.sync
                def _(sp):
                    if layer:
                        loads = [(router_raw[:, :], a["L1_ffn_gate_w"]), (router_bias[:, :], spread(a["L1_ffn_gate_bias"])),
                                 (order[:, :, :], a["order4"])]
                        late = [(s_raw[0], raw[:, 0, 0:ROUTED, :], a["L1_ffn_expert_gate"].rearrange("e i h -> (e i) h").rearrange("(n p) h -> p n h", p=P)),
                                (s_raw[0], raw[:, 0, ROUTED, :], a["L1_ffn_shared_gate"]),
                                (s_raw[1], raw[:, 1, 0:ROUTED, :], a["L1_ffn_expert_up"].rearrange("e i h -> (e i) h").rearrange("(n p) h -> p n h", p=P)),
                                (s_raw[1], raw[:, 1, ROUTED, :], a["L1_ffn_shared_up"]),
                                (s_raw[2], raw[:, 2, 0:ROUTED, :].rearrange("p n (e i) -> p (n e) i", e=2), a["L1_ffn_expert_down"].rearrange("e h i -> h e i")),
                                (s_raw[2], raw[:, 2, ROUTED, :], a["L1_ffn_shared_down"])]
                    else:
                        loads = [(router[:, :], a["L0_ffn_gate_w"]), (order[:, :, :], a["order8"])]
                        late = []
                        for w, name in ((w_gate, "gate"), (w_up, "up")):
                            flat = w[:, :, :].rearrange("p n c -> p (n c)")
                            late.append((s_late, flat[:, 0:E * HID].rearrange("p (e f) -> p e f", e=E), a[f"L0_ffn_exp_{name}"].rearrange("e d f -> d e f")))
                            late.append((s_late, flat[:, E * HID:(E + 2) * HID].rearrange("p (e f) -> p e f", e=2), a[f"L0_ffn_sh_{name}"].rearrange("e d f -> d e f")))
                        late.append((s_late, w_down[:, 0:ROUTED, :], a["L0_ffn_exp_down"].rearrange("e f d -> (e f) d").rearrange("(n p) d -> p n d", p=P)))
                        shared = a["L0_ffn_sh_down"].rearrange("e f d -> (e f) d")
                        late.append((s_late, w_down[:, ROUTED:ROUTED + 2, :], shared[0:2 * P, :].rearrange("(n p) d -> p n d", p=P)))
                        late.append((s_late, w_down[0:rows_of[-1], NH - 1, :], shared[2 * P:2 * HID, :]))
                    for dst, src in loads:
                        sp.dma_start(dst, src).then_inc(s_load, 16)
                    sp.dma_start(picks_in[:, :, :], a[f"picks{layer}"]).then_inc(s_picks, 16)
                    for semaphore, dst, src in late:
                        sp.dma_start(dst, src).then_inc(semaphore, 16)
                    sp.wait_ge(s_load, len(loads) * 16)
                    sp.wait_ge(s_picks, 16)
                    if layer:
                        for semaphore in s_raw:
                            sp.wait_ge(semaphore, 2 * 16)
                    else:
                        sp.wait_ge(s_late, n_late * 16)
                    if layer:
                        sp.wait_ge(s_end, 1)
                        sp.dma_start(kept["out"][0].rearrange("(t p) c -> p t c", p=P), x[:, :, :]).then_inc(s_out, 16)
                        sp.wait_ge(s_out, 16)

                width = sum(rows_of)
                split = [([part[:, :] for part in xn_parts], xn[:, :])] + [
                    ([part[:, 0:width] for part in parts], w[:, :, :].rearrange("p n c -> p (n c)")[:, 0:width])
                    for parts, w in ((gate_parts, w_gate), (up_parts, w_up))]

                def high_part(n):
                    nc.scalar.activation(split[n][0][0], split[n][1], ACT.Copy).then_inc(s_high, 1)

                @block.gpsimd
                def _(pool):
                    for n, ((high, low), source) in enumerate(split):
                        pool.wait_ge(s_high, n + 1)
                        nc.gpsimd.tensor_tensor(low, source, high.bitcast(F32), ALU.subtract).then_inc(s_low, 1)

                @block.tensor
                def _(pe):
                    pe.wait_ge(s_load, n_loads * 16)
                    if layer:
                        nc.tensor.transpose(ps[:, 3, 0:E], router_raw[:, :], ident[0:E, 0:E]).then_inc(s_w_turned, 1)
                    pe.wait_ge(s_norm, NT)
                    transpose_tiles(nc, pe, bank, normed, ident, s_turned)
                    pe.wait_ge(s_xn_a, 1)
                    pe.wait_ge(s_xn_v, 1)
                    if layer:
                        pe.wait_ge(s_router, 1)
                    for t in range(NT):
                        last = nc.tensor.matmul(ps[:, 2, t * E:(t + 1) * E], xn[:, t * P:(t + 1) * P], router[:, :], start=True, stop=True)
                    last.then_inc(s_logit, 1)
                    if layer:
                        for n in range(3 * NH):
                            if n % NH == 0:
                                pe.wait_ge(s_raw[n // NH], 2 * 16)
                            if n >= 4:
                                pe.wait_ge(s_w_kept, n - 3)
                            nc.tensor.transpose(ps[:, 4 + n % 4, 0:P], raw[:, n // NH, n % NH, :], ident[:, :]).then_inc(s_w_turned, 1)

                    def turn_routes():
                        pe.wait_ge(s_packed, 1)
                        for t in range(NT):
                            last = nc.tensor.transpose(mid[:, t * P:(t + 1) * P], packed[:, t, :].bitcast(F32), ident[:, :])
                        last.then_inc(s_routes, 1)
                        pe.wait_ge(s_kept, 1)

                    def product(w, n, k, bank_of):
                        for c in range(2):
                            for i, (wp, xp) in enumerate(((0, 0), (0, 1), (1, 0))):
                                last = nc.tensor.matmul(ps[0:k, bank_of + c, :], w[wp][:, n * P:n * P + k], xn_parts[xp][:, c * HALF:(c + 1) * HALF],
                                                        start=i == 0, stop=i == 2)
                        return last

                    def down(n):
                        k = rows_of[n]
                        if n == 0 and not layer:
                            pe.wait_ge(s_late, n_late * 16)
                        pe.wait_ge(s_hidden, n + 1)
                        for t in range(NT):
                            last = nc.tensor.matmul(bank[:, 6 * HALF + t * P:6 * HALF + (t + 1) * P], hidden[n % 2][0:k, t * P:(t + 1) * P],
                                                    w_down[0:k, n, :], start=False, stop=n == NH - 1 and t % 4 == 3, skip_group_check=True)
                        last.then_inc(s_down, 1)

                    pe.wait_ge(s_zero, 1)
                    if layer:
                        pe.wait_ge(s_w_kept, 3 * NH)
                    for c in range(2):
                        nc.tensor.matmul(ps[:, 6 + c, :], ident[:, :], zero[:, :].to_broadcast([P, HALF]), start=True, stop=False, skip_group_check=True)
                    pe.wait_ge(s_exp_out, 1)
                    pe.wait_ge(s_low, 2)
                    for n in range(NH):
                        k = rows_of[n]
                        if n:
                            pe.wait_ge(s_silu, n)
                        product(gate_parts, n, k, 0).then_inc(s_gate, 1)
                        if n:
                            pe.wait_ge(s_prod, n)
                        else:
                            pe.wait_ge(s_low, 3)
                        product(up_parts, n, k, 2).then_inc(s_up, 1)
                        if n < ROUTED:
                            if n:
                                pe.wait_ge(s_hidden, n)
                            else:
                                turn_routes()
                            for c in range(2):
                                last = nc.tensor.matmul(ps[:, 4 + c, :], picks[:, n, :], route_rows[:, c * HALF:(c + 1) * HALF], start=True, stop=True)
                            last.then_inc(s_route, 1)
                        if n:
                            down(n - 1)
                    down(NH - 1)

                @block.scalar
                def _(act):
                    root(nc, act, moments, s_eps, s_root)
                    act.wait_ge(s_turned, 1)
                    nc.scalar.activation(xn[:, 0:HALF], bank[:, 0:HALF], ACT.Copy).then_inc(s_xn_a, 1)
                    if layer:
                        act.wait_ge(s_w_turned, 1)
                        nc.scalar.activation(router[:, :], ps[:, 3, 0:E], ACT.Copy).then_inc(s_router, 1)
                    act.wait_ge(s_xn_a, 1)
                    act.wait_ge(s_xn_v, 1)
                    high_part(0)
                    act.wait_ge(s_exp_in, 1)
                    prob = scratch["prob"]
                    if layer:
                        nc.scalar.activation(prob[:, :, :], ps[:, 2, 0:NT * E].rearrange("p (t e) -> p t e", e=E), ACT.Sigmoid).then_inc(s_exp_out, 1)
                        for n in range(3 * NH):
                            act.wait_ge(s_w_turned, n + 2)
                            nc.scalar.activation((w_gate, w_up, w_down)[n // NH][:, n % NH, :], ps[:, 4 + n % 4, 0:P], ACT.Copy).then_inc(s_w_kept, 1)
                            if n in (NH, 2 * NH):
                                act.wait_ge(s_w_kept, n)
                                high_part(n // NH)
                    else:
                        nc.scalar.activation(prob[:, :, :], prob[:, :, :], ACT.Exp).then_inc(s_exp_out, 1)
                        act.wait_ge(s_late, n_late * 16)
                        high_part(1)
                        high_part(2)
                    for n in range(NH):
                        k = rows_of[n]
                        act.wait_ge(s_gate, n + 1)
                        if n >= 2:
                            act.wait_ge(s_prod, n - 1)
                        nc.scalar.activation(silu[n % 2][0:k, :], bank[0:k, 0:T], ACT.Silu).then_inc(s_silu, 1)

                @block.vector
                def _(dve):
                    step = stepper(dve)
                    step(nc.vector.memset(zero[:, :], 0.0), s_zero, wait=False)
                    step(nc.vector.memset(packed[:, :, :].bitcast(F32), 0.0), s_vec)
                    layer_norm(nc, dve, step, s_vec, stats, moments, x, normed, s_eps, s_root, s_norm)
                    dve.wait_ge(s_turned, 2)
                    step(nc.vector.tensor_copy(xn[:, HALF:T], bank[:, HALF:T]), s_xn_v)
                    dve.wait_ge(s_picks, 16)
                    step(nc.vector.tensor_copy(picks[:, :, :], picks_in[:, :, :]), s_vec)
                    dve.wait_ge(s_load, n_loads * 16)
                    dve.wait_ge(s_logit, 1)
                    if layer:
                        step(nc.vector.memset(scratch["peak"][:, :], 0.0), s_exp_in)
                        dve.wait_ge(s_exp_out, 1)
                        route_groups(nc, dve, step, s_vec, scratch, router_bias, order, weights)
                    else:
                        logits = ps[:, 2, 0:NT * E].rearrange("p (t e) -> p t e", e=E)
                        route_top2(nc, dve, step, s_vec, s_exp_in, s_exp_out, scratch, logits, order, weights)
                    step(nc.vector.tensor_copy(packed[:, :, 0:E], weights[:, :, :]), s_vec)
                    step(nc.vector.tensor_tensor(packed[:, :, 32:32 + E], weights[:, :, :], packed[:, :, 0:E].bitcast(F32), ALU.subtract), s_packed)
                    dve.wait_ge(s_routes, 1)
                    step(nc.vector.tensor_copy(route_rows[:, :], mid), s_kept)
                    for n in range(NH):
                        k = rows_of[n]
                        dve.wait_ge(s_silu, n + 1)
                        dve.wait_ge(s_up, n + 1)
                        if n < ROUTED:
                            nc.vector.tensor_tensor(silu[n % 2][0:k, :], silu[n % 2][0:k, :], bank[0:k, T:2 * T], ALU.mult).then_inc(s_prod, 1)
                            dve.wait_ge(s_prod, n + 1)
                            dve.wait_ge(s_route, n + 1)
                        if n >= 2:
                            dve.wait_ge(s_down, n - 1)
                        if n < ROUTED:
                            nc.vector.tensor_tensor(hidden[n % 2][0:k, :], silu[n % 2][0:k, :], bank[0:k, 2 * T:3 * T], ALU.mult).then_inc(s_hidden, 1)
                        else:
                            nc.vector.tensor_tensor(hidden[n % 2][0:k, :], silu[n % 2][0:k, :], bank[0:k, T:2 * T], ALU.mult).then_inc(s_hidden, 1)
                            if n < NH - 1:
                                nc.vector.memset(weights[:, 0, 0:1], 0.0).then_inc(s_prod, 1)
                    dve.wait_ge(s_down, NH)
                    nc.vector.tensor_tensor(x[:, :, :], x[:, :, :], bank[:, 3 * T:4 * T].rearrange("p (t c) -> p t c", c=P), ALU.add).then_inc(s_end, 1)
                    dve.wait_ge(s_end, 1)


def route_groups(nc, dve, step, s_vec, s, bias, order, weights):
    E, scores, choice = 32, s["prob"], s["choice"]
    step(nc.vector.tensor_tensor(choice[:, :, :], scores[:, :, :], bias[:, :].unsqueeze(1).to_broadcast([P, NT, E]), ALU.add), s_vec)
    for n in range(NT * 4):
        t, g = n // 4, n % 4
        step(nc.vector.max(s["best"][:, t, g, :], choice[:, t, g * 8:(g + 1) * 8]), s_vec, wait=n == NT * 4 - 1)
    step(nc.vector.tensor_tensor(s["groups"][:, :, :], s["best"][:, :, :, 0], s["best"][:, :, :, 1], ALU.add), s_vec)
    select(nc, step, s_vec, s["groups"], order, s["larger"], s["equal"], s["rank"], 2)
    step(nc.vector.tensor_tensor(choice[:, :, :].rearrange("p t (g e) -> p (t g) e", g=4), choice[:, :, :].rearrange("p t (g e) -> p (t g) e", g=4),
                                 s["rank"][:, :, :].rearrange("p t g -> p (t g)").unsqueeze(2).to_broadcast([P, NT * 4, 8]), ALU.mult), s_vec)
    for t in range(NT):
        step(nc.vector.max(s["top"][:, t, :], choice[:, t, :]), s_vec, wait=t == NT - 1)
    for t in range(NT):
        step(nc.vector.match_replace(s["left"][:, t, :], s["top"][:, t, :], choice[:, t, :], MASKED), s_vec, wait=t == NT - 1)
    step(nc.vector.tensor_scalar(s["left"][:, :, :], s["left"][:, :, :], MASKED, None, ALU.is_equal), s_vec)
    step(nc.vector.tensor_tensor(weights[:, :, :], scores[:, :, :], s["left"][:, :, :], ALU.mult), s_vec)
    step(nc.vector.tensor_reduce(s["total"][:, :], weights[:, :, :], AX.X, ALU.add), s_vec)
    step(nc.vector.tensor_scalar(s["total"][:, :], s["total"][:, :], 1e-20, None, ALU.add), s_vec)
    step(nc.vector.reciprocal(s["total"][:, :], s["total"][:, :]), s_vec)
    step(nc.vector.tensor_tensor(weights[:, :, :], weights[:, :, :], s["total"][:, :].unsqueeze(2).to_broadcast([P, NT, E]), ALU.mult), s_vec)
    step(nc.vector.tensor_scalar(weights[:, :, :], weights[:, :, :], 2.5, None, ALU.mult), s_vec)


def mixture0(nc, kept, ps, a):
    mixture(nc, kept, ps, a, 0)


def mixture1(nc, kept, ps, a):
    mixture(nc, kept, ps, a, 1)


def lstm_step(nc, kept, ps, a):
    x, ident = kept["x"], kept["ident"]
    bank = ps[:, :, :].rearrange("p b c -> p (b c)")
    with ExitStack() as stack:
        m = Memory(nc, stack, "lstm")
        w, bias = m.sb("w", [P, 4 * P]), m.sb("bias", [P, 4])
        stats, moments, normed, xn = m.sb("stats", [P, NT, 6]), m.sb("moments", [P, NT, 2]), m.sb("normed", [P, NT, P]), m.sb("xn", [P, T])
        gate_in, gate_out, cand = m.sb("gate_in", [P, T]), m.sb("gate_out", [P, T]), m.sb("cand", [P, T])
        s_load, s_vec, s_eps, s_root, s_norm, s_turned, s_xn_a, s_xn_v, s_gates, s_act, s_cell, s_tanh, s_h, s_back, s_x = (m.sem(n) for n in (
            "loaded", "vector_step", "variance", "root", "normed", "turned", "xn_scalar", "xn_vector", "gates", "activated", "cell", "tanh",
            "state", "state_turned", "x_done"))
        with nc.Block() as block:
            @block.sync
            def _(sp):
                sp.dma_start(w[:, :], a["L1_attn_w"]).then_inc(s_load, 16)
                sp.dma_start(bias[:, :], columns(a["L1_attn_bias"])).then_inc(s_load, 16)
                sp.wait_ge(s_load, 2 * 16)

            @block.tensor
            def _(pe):
                pe.wait_ge(s_load, 2 * 16)
                pe.wait_ge(s_norm, NT)
                transpose_tiles(nc, pe, bank, normed, ident, s_turned)
                pe.wait_ge(s_xn_a, 1)
                pe.wait_ge(s_xn_v, 1)
                for n, g in enumerate((0, 2, 3)):
                    for c in range(2):
                        last = nc.tensor.matmul(ps[:, 2 + 2 * n + c, :], w[:, g * P:(g + 1) * P], xn[:, c * HALF:(c + 1) * HALF], start=True, stop=True)
                    last.then_inc(s_gates, 1)
                pe.wait_ge(s_h, 1)
                for t in range(NT):
                    last = nc.tensor.transpose(bank[:, t * P:(t + 1) * P], cand[:, t * P:(t + 1) * P], ident[:, :])
                last.then_inc(s_back, 1)

            @block.scalar
            def _(act):
                root(nc, act, moments, s_eps, s_root)
                act.wait_ge(s_load, 2 * 16)
                act.wait_ge(s_turned, 1)
                nc.scalar.activation(xn[:, 0:HALF], bank[:, 0:HALF], ACT.Copy).then_inc(s_xn_a, 1)
                for n, (dst, g, f) in enumerate(((gate_in, 0, ACT.Sigmoid), (gate_out, 2, ACT.Sigmoid), (cand, 3, ACT.Tanh))):
                    act.wait_ge(s_gates, n + 1)
                    nc.scalar.activation(dst[:, :], bank[:, (n + 1) * T:(n + 2) * T], f, bias=bias[:, g:g + 1]).then_inc(s_act, 1)
                act.wait_ge(s_cell, 1)
                nc.scalar.activation(cand[:, :], cand[:, :], ACT.Tanh).then_inc(s_tanh, 1)

            @block.vector
            def _(dve):
                step = stepper(dve)
                layer_norm(nc, dve, step, s_vec, stats, moments, x, normed, s_eps, s_root, s_norm)
                dve.wait_ge(s_turned, 2)
                step(nc.vector.tensor_copy(xn[:, HALF:T], bank[:, HALF:T]), s_xn_v)
                dve.wait_ge(s_act, 3)
                step(nc.vector.tensor_tensor(cand[:, :], gate_in[:, :], cand[:, :], ALU.mult), s_cell)
                dve.wait_ge(s_tanh, 1)
                step(nc.vector.tensor_tensor(cand[:, :], gate_out[:, :], cand[:, :], ALU.mult), s_h)
                dve.wait_ge(s_back, 1)
                step(nc.vector.tensor_tensor(x[:, :, :], x[:, :, :], bank[:, 0:T].rearrange("p (t c) -> p t c", c=P), ALU.add), s_x)


def latent_attention(nc, kept, ps, a):
    H1 = 8
    NM, NL = NK, NT
    NZ = NM + NL
    x, ident = kept["x"], kept["ident"]
    with ExitStack() as stack:
        m = Memory(nc, stack, "lat")
        z_rows = [m.sb(f"z_rows_{n}", [P, NZ, P], F32R) for n in ("high", "low")]
        z_cols = [m.sb(f"z_cols_{n}", [P, NZ * P], F32R) for n in ("high", "low")]
        mix = m.sb("mix", [P, 2 * P])
        latents = m.sb("latents", [P, T])

        w_q, w_k, w_v, w_o = (m.sb(n, [P, P]) for n in ("w_q", "w_k", "w_v", "w_o"))
        biases = m.sb("biases", [P, 3, H1])
        b_o = m.sb("b_o", [P, P])
        s_bias, s_w_qk, s_w_vo = (m.sem(n) for n in ("biases_loaded", "w_q_k_loaded", "w_v_o_loaded"))

        def load_qk(sp, h):
            sp.dma_start(w_q[:, :], a["L1_xattn_Wq"][:, bass.ds(h * P, P)]).then_inc(s_w_qk, 16)
            sp.dma_start(w_k[:, :], a["L1_xattn_Wkv"][:, bass.ds(h * P, P)]).then_inc(s_w_qk, 16)

        def load_vo(sp, h):
            sp.dma_start(w_v[:, :], a["L1_xattn_Wkv"][:, bass.ds(h * P + H1 * P, P)]).then_inc(s_w_vo, 16)
            sp.dma_start(w_o[:, :], a["L1_xattn_Wo"][bass.ds(h * P, P), :]).then_inc(s_w_vo, 16)

        with ExitStack() as own:
            b = Memory(nc, own, "zed")
            z = b.sb("z", [P, NM, P])
            stats, moments, shift = b.sb("stats", [P, NM, 6]), b.sb("moments", [P, NM, 2]), b.sb("shift", [P, NM])
            fresh, norms = b.sb("fresh", [P, 1]), b.sb("norms", [P, 4])
            lstats, lmoments = b.sb("lstats", [P, NT, 6]), b.sb("lmoments", [P, NT, 2])
            lmoments2, normed, normed2 = b.sb("lmoments2", [P, NT, 2]), b.sb("normed", [P, NT, P]), b.sb("normed2", [P, NT, P])
            s_load, s_rows = b.sem("loaded"), [b.sem(f"rows_loaded{n}") for n in range(3)]
            s_vec, s_stat, s_var, s_root, s_shift, s_z, s_high, s_low, s_turned, s_chigh, s_clow = (b.sem(n) for n in (
                "vector_step", "statistics", "variance", "root", "shift", "z", "rows_high", "rows_low", "turned", "columns_high", "columns_low"))
            normed1 = b.sb("normed1", [P, NT, P])
            s_lrows = b.sem("latent_rows")
            s_eps1, s_root1, s_norm1, s_eps2, s_root2, s_norm2, s_lturned, s_mix = (b.sem(n) for n in (
                "eps1", "root1", "norm1", "eps2", "root2", "norm2", "latents_turned", "mix"))
            ctx = a["ctx_1024"][0]
            parts = ((0, NM // 2), (NM // 2, NM - 1))
            PAIRS = (NI - 2) // 2

            with nc.Block() as block:
                @block.sync
                def _(sp):
                    for n, (lo, hi) in enumerate(parts):
                        sp.dma_start(z[:, lo:hi, :], ctx[lo * P:hi * P, :].rearrange("(t p) c -> p t c", p=P)).then_inc(s_rows[n], 16)
                    sp.dma_start(z[:, NM - 1, :], ctx[LAST:LC, :]).then_inc(s_rows[2], 16)
                    sp.dma_start(fresh[:, :], a["fresh"]).then_inc(s_load, 16)
                    for n, name in enumerate(("gamma_media", "beta_media", "gamma_lat", "beta_lat")):
                        sp.dma_start(norms[:, n:n + 1], columns(a[f"L1_xattn_{name}"])).then_inc(s_load, 16)
                    load_qk(sp, 0)
                    load_vo(sp, 0)
                    for n, name in enumerate(("bq", "bk", "bv")):
                        src = a["L1_xattn_bq"] if n == 0 else a["L1_xattn_bkv"][(n - 1) * H1 * P:n * H1 * P]
                        sp.dma_start(biases[:, n, :], columns(src)).then_inc(s_bias, 16)
                    sp.dma_start(b_o[:, :], spread(a["L1_xattn_bo"])).then_inc(s_bias, 16)
                    sp.wait_ge(s_load, 5 * 16)

                @block.scalar
                def _(act):
                    def norm(j):
                        for n in range(U0):
                            t = j * U0 + n
                            row = z[:, bass.ds(t, 1), :].rearrange("p a c -> p (a c)")
                            nc.scalar.activation(row, row, ACT.Identity, bias=shift[:, bass.ds(t, 1)], scale=moments[:, bass.ds(t, 1), 1]).then_inc(s_z, 1)

                    def high(j, k):
                        act.wait_ge(s_turned, j + 1)
                        nc.scalar.activation(z_cols[0][:, bass.ds(j * (U0 * P), U0 * P)], ps[:, k, 0:U0 * P], ACT.Copy).then_inc(s_chigh, 1)

                    root(nc, act, lmoments, s_eps1, s_root1)
                    root(nc, act, lmoments2, s_eps2, s_root2)
                    act.wait_ge(s_var, 1)
                    nc.scalar.activation(moments[:, :, 1], moments[:, :, 1], ACT.Sqrt).then_inc(s_root, 1)
                    act.wait_ge(s_shift, 1)
                    norm(0)
                    norm(1)
                    with act.Fori(0, PAIRS) as i:
                        for k in range(2):
                            high(i * 2 + k, k)
                            norm(i * 2 + (k + 2))
                    high(NI - 3, 0)
                    norm(NI - 1)
                    high(NI - 2, 1)
                    high(NI - 1, 0)

                @block.tensor
                def _(pe):
                    def turn(j, k):
                        pe.wait_ge(s_z, j * U0 + U0)
                        for n in range(U0):
                            last = nc.tensor.transpose(ps[:, k, n * P:(n + 1) * P], z[:, j * U0 + n, :], ident[:, :])
                        last.then_inc(s_turned, 1)

                    pe.wait_ge(s_norm2, NT)
                    for t in range(NT):
                        last = nc.tensor.transpose(ps[:, 2 + t // 4, (t % 4) * P:(t % 4 + 1) * P], normed2[:, t, :], ident[:, :])
                        if t % 4 == 3:
                            last.then_inc(s_lturned, 1)
                    for j in range(NI):
                        if j >= 2:
                            pe.wait_ge(s_clow, j - 1)
                        turn(j, j % 2)

                @block.gpsimd
                def _(pool):
                    pool.wait_ge(s_norm2, NT)
                    nc.gpsimd.tensor_scalar(normed1[:, :, :], normed2[:, :, :], 1.0, None, ALU.add).then_inc(s_lrows, 1)
                    pool.wait_ge(s_lrows, 1)
                    nc.gpsimd.tensor_scalar(z_rows[0][:, NM:NZ, :], normed1[:, :, :], 1.0, None, ALU.mult).then_inc(s_lrows, 1)
                    pool.wait_ge(s_lrows, 2)
                    nc.gpsimd.tensor_tensor(z_rows[1][:, NM:NZ, :], normed1[:, :, :], z_rows[0][:, NM:NZ, :].bitcast(F32), ALU.subtract).then_inc(s_lrows, 1)

                @block.vector
                def _(dve):
                    step = stepper(dve)

                    def split_rows(j):
                        dve.wait_ge(s_z, j * U0 + U0)
                        tiles = bass.ds(j * U0, U0)
                        nc.vector.tensor_scalar(z_rows[0][:, tiles, :], z[:, tiles, :], 1.0, None, ALU.mult).then_inc(s_high, 1)
                        dve.wait_ge(s_high, j + 1)
                        nc.vector.tensor_tensor(z_rows[1][:, tiles, :], z[:, tiles, :], z_rows[0][:, tiles, :].bitcast(F32), ALU.subtract).then_inc(s_low, 1)

                    def split_columns(j, k):
                        dve.wait_ge(s_chigh, j + 1)
                        cols = bass.ds(j * (U0 * P), U0 * P)
                        nc.vector.tensor_tensor(z_cols[1][:, cols], ps[:, k, 0:U0 * P], z_cols[0][:, cols].bitcast(F32), ALU.subtract).then_inc(s_clow, 1)

                    layer_norm(nc, dve, step, s_vec, lstats, lmoments, x, normed, s_eps1, s_root1, s_norm1)
                    layer_norm(nc, dve, step, s_vec, lstats, lmoments2, normed, normed2, s_eps2, s_root2, s_norm2)
                    for n in range(3):
                        dve.wait_ge(s_rows[n], 16)
                    for t in range(NM):
                        step(nc.vector.bn_stats(stats[:, t, :], z[:, t, :]), s_stat, wait=t == NM - 1)
                    for t in range(NM):
                        step(nc.vector.bn_aggr(moments[:, t, :], stats[:, t, :]), s_stat, wait=t == NM - 1)
                    step(nc.vector.tensor_scalar(moments[:, :, 1], moments[:, :, 1], LN_EPS, None, ALU.add), s_var)
                    dve.wait_ge(s_root, 1)
                    step(nc.vector.reciprocal(moments[:, :, 1], moments[:, :, 1]), s_vec)
                    step(nc.vector.scalar_tensor_tensor(shift[:, :], moments[:, :, 0], -1.0, moments[:, :, 1], ALU.mult, ALU.mult), s_vec)
                    step(nc.vector.tensor_scalar(shift[:, :], shift[:, :], 1.0, None, ALU.add), s_shift)
                    split_rows(0)
                    with dve.Fori(0, (NI - 1) // 2) as i:
                        for k in range(2):
                            split_rows(i * 2 + (k + 1))
                            split_columns(i * 2 + k, k)
                    split_columns(NI - 1, 0)
                    dve.wait_ge(s_load, 5 * 16)
                    dve.wait_ge(s_low, NI)
                    for part in z_rows:
                        step(nc.vector.tensor_scalar(part[:, NM - 1, :], part[:, NM - 1, :].bitcast(F32), fresh[:, 0:1], None, ALU.mult), s_vec)
                    for n in range(2):
                        gain, offset = norms[:, 2 * n:2 * n + 1], norms[:, 2 * n + 1:2 * n + 2]
                        step(nc.vector.tensor_tensor(shift[:, n:n + 1], offset, gain, ALU.subtract), s_vec)
                        step(nc.vector.tensor_scalar(shift[:, n:n + 1], shift[:, n:n + 1], 1.0 / P, None, ALU.mult), s_vec)
                        step(nc.vector.tensor_scalar(mix[:, n * P:(n + 1) * P], ident[:, :], gain, shift[:, n:n + 1], ALU.mult, ALU.add), s_mix)
                    dve.wait_ge(s_lturned, 2)
                    for c in range(2):
                        lo, hi = c * HALF, (c + 1) * HALF
                        step(nc.vector.tensor_scalar(latents[:, lo:hi], ps[:, 2 + c, :], norms[:, 2:3], norms[:, 3:4], ALU.mult, ALU.add), s_vec)
                        step(nc.vector.tensor_scalar(normed[:, 4 * c:4 * c + 4, :].rearrange("p t c -> p (t c)"), ps[:, 2 + c, :], 1.0, None, ALU.add), s_vec)
                        step(nc.vector.tensor_copy(z_cols[0][:, NM * P + lo:NM * P + hi], normed[:, 4 * c:4 * c + 4, :].rearrange("p t c -> p (t c)")), s_vec)
                        step(nc.vector.tensor_tensor(z_cols[1][:, NM * P + lo:NM * P + hi], normed[:, 4 * c:4 * c + 4, :].rearrange("p t c -> p (t c)"),
                                                     z_cols[0][:, NM * P + lo:NM * P + hi].bitcast(F32), ALU.subtract), s_vec)

        latent_heads(nc, kept, ps, z_rows, z_cols, mix, latents, (w_q, w_k, w_v, w_o, biases, b_o),
                     (s_bias, s_w_qk, s_w_vo), (load_qk, load_vo), H1, NM, NL)


def latent_heads(nc, kept, ps, z_rows, z_cols, mix, latents, weights, loaded, loads, H1, NM, NL):
    x, ident = kept["x"], kept["ident"]
    NZ = NM + NL
    REACH = 11.4
    ROUNDS = 3
    U_LATENTS, TAKE_LATENTS, FOLD_V, OUT_WEIGHTS, OUTPUTS, SCALE, ADD = 0, 1, 3, 5, (7, 8), 9, 10
    FOLD_K, QUERY, R_AT, BOUND, EXACT = 12, 14, (16, 24), 30, 32
    SUM, SQUARES = 2, 4
    TAKE_MEDIA, U_MEDIA = NM, NM + 2
    bank = ps[:, :, :].rearrange("p b c -> p (b c)")
    mid = bank[:, 6 * HALF:8 * HALF]
    with ExitStack() as own:
        b = Memory(nc, own, "hed")
        w_q, w_k, w_v, w_o, biases, b_o = weights
        s_bias, s_w_qk, s_w_vo = loaded
        load_qk, load_vo = loads
        k2, v2, w2 = (b.sb(n, [P, 2, P]) for n in ("k2", "v2", "w2"))
        q = b.sb("q", [P, T])
        r = [[b.sb(f"r_{g}_{part}", [P, T], F32R) for part in ("high", "low")] for g in ("media", "latents")]
        r_next = [[b.sb(f"r_next_{g}_{part}", [P, T], F32R) for part in ("high", "low")] for g in ("media", "latents")]
        squares = b.sb("squares", [P, T], F32R)
        ones_in, ones, mean = b.sb("ones_in", [P, P]), b.sb("ones", [P, P], F32R), b.sb("mean", [P, 1])
        peak = b.sb("peak", [P, 2, 2])
        twice, quotient = b.sb("twice", [P, 2]), b.sb("quotient", [P, 2])
        bound, minus, minus_next = b.sb("bound", [P, 1]), b.sb("minus", [P, 1]), b.sb("minus_next", [P, 1])
        exps = [b.sb(f"exps{n}", [P, T]) for n in range(2)]
        high = [b.sb(f"exps_high{n}", [P, T], F32R) for n in range(2)]
        low = [b.sb(f"exps_low{n}", [P, T], F32R) for n in range(2)]
        u = [b.sb(f"u_{g}", [P, T]) for g in ("media", "latents")]
        u_both = q
        inverse = b.sb("inverse", [P, NT])
        row_max, chunk_max, spread_max = b.sb("row_max", [P, NT]), b.sb("chunk_max", [P, NT]), b.sb("spread_max", [P, P])
        s_set, s_end = (b.sem(n) for n in ("set", "end"))
        s_fold_k, s_k2, s_q, s_q_kept, s_r, s_r_high, s_r_low, s_sq, s_bound_mm, s_peak, s_root, s_bound, s_ready = (b.sem(n) for n in (
            "keys_folded", "k2", "q", "q_kept", "r", "r_high", "r_low", "squares", "bound_sums", "peaks", "root", "bound_step", "ready"))
        s_take_low, s_take_high = ([b.sem(f"taken_{part}_{g}") for g in ("media", "latents")] for part in ("low", "high"))
        s_minus = b.sem("minus")
        s_score, s_exp, s_high, s_low, s_weighted = (b.sem(n) for n in ("scores", "exps", "exps_high", "exps_low", "weighted"))
        s_u_media, s_u_latents, s_u_both, s_fold_v, s_v2, s_w2, s_w2_kept, s_den, s_inv, s_y, s_scaled, s_added = (b.sem(n) for n in (
            "u_media", "u_latents", "u_both", "values_folded", "v2", "w2", "w2_kept", "denominators", "inverse", "outputs", "outputs_scaled", "added"))
        x_score, x_max, x_row, x_spread, x_turned, x_fixed, x_done = (b.sem(n) for n in (
            "exact_scores", "exact_max", "exact_row", "exact_spread", "exact_turned", "exact_fixed", "exact_done"))
        XN = NI * NT + 2 * NT
        ROWS = NI + 3

        with nc.Block() as block:
            @block.sync
            def _(sp):
                with sp.Fori(0, H1 - 1) as h:
                    sp.wait_ge(s_q, h + 1)
                    load_qk(sp, h + 1)
                    sp.wait_ge(s_w2, h + 1)
                    load_vo(sp, h + 1)
                sp.wait_ge(s_w_qk, H1 * 2 * 16)
                sp.wait_ge(s_w_vo, H1 * 2 * 16)
                sp.wait_ge(s_bias, 4 * 16)

            @block.tensor
            def _(pe):
                def scores(h, t):
                    if t >= 2:
                        pe.wait_ge(s_high, h * NZ + (t - 1))
                    elif t == 0 and not first_head(h):
                        pe.wait_ge(s_high, h * NZ)
                    if t in (0, NM):
                        pe.wait_ge(s_take_low[t >= NM], h + 1)
                        pe.wait_ge(s_take_high[t >= NM], h + 1)
                    group = r[t >= NM]
                    for c in range(2):
                        for n, (zp, rp) in enumerate(((0, 0), (0, 1), (1, 0))):
                            last = nc.tensor.matmul(ps[:, 2 * (t % 2) + c, :], z_cols[zp][:, t * P:(t + 1) * P], group[rp][:, c * HALF:(c + 1) * HALF],
                                                    start=n == 0, stop=n == 2)
                    last.then_inc(s_score, 1)

                def weigh(h, t):
                    if t == 0 and not first_head(h):
                        pe.wait_ge(s_u_media, h)
                    if t == NM and not first_head(h):
                        pe.wait_ge(s_added, h)
                    pe.wait_ge(s_low, h * NZ + (t + 1))
                    first, last_tile = (0, NM - 1) if t < NM else (NM, NZ - 1)
                    for c in range(2):
                        for n, (zp, e) in enumerate(((0, high), (0, low), (1, high))):
                            last = nc.tensor.matmul(ps[:, (4 if t < NM else 6) + c, :], z_rows[zp][:, t, :], e[t % 2][:, c * HALF:(c + 1) * HALF],
                                                    start=t == first and n == 0, stop=t == last_tile and n == 2)
                    last.then_inc(s_weighted, 1)

                def finish(h, at):
                    if at == U_LATENTS:
                        weigh(h, NZ - 1)
                    elif at == FOLD_V:
                        pe.wait_ge(s_w_vo, h * 32 + 32)
                        pe.wait_ge(s_u_latents, h + 1)
                        nc.tensor.matmul(ps[:, 6, 0:2 * P], w_v[:, :], mix[:, :], start=True, stop=True).then_inc(s_fold_v, 1)
                    elif at == OUT_WEIGHTS:
                        pe.wait_ge(s_v2, h + 1)
                        for g in range(2):
                            last = nc.tensor.matmul(ps[:, 6, g * P:(g + 1) * P], v2[:, g, :], w_o[:, :], start=True, stop=True)
                        last.then_inc(s_w2, 1)
                        pe.wait_ge(s_u_both, h + 1)
                        for t in range(NT):
                            last = nc.tensor.matmul(ps[:, 7, t:t + 1], u_both[:, t * P:(t + 1) * P], mean[:, :], start=True, stop=True)
                        last.then_inc(s_den, 1)
                    elif at in OUTPUTS:
                        if at == OUTPUTS[0]:
                            pe.wait_ge(s_w2_kept, h + 1)
                            pe.wait_ge(s_inv, h + 1)
                        c = OUTPUTS.index(at)
                        for t in range(4 * c, 4 * c + 4):
                            for g in range(2):
                                last = nc.tensor.matmul(mid[:, t * P:(t + 1) * P], u[g][:, t * P:(t + 1) * P], w2[:, g, :], start=g == 0, stop=g == 1)
                        last.then_inc(s_y, 1)

                def prepare(h, at):
                    if at == FOLD_K:
                        pe.wait_ge(s_w_qk, h * 32 + 32)
                        nc.tensor.matmul(ps[:, 6, 0:2 * P], w_k[:, :], mix[:, :], start=True, stop=True).then_inc(s_fold_k, 1)
                    elif at == QUERY:
                        pe.wait_ge(s_k2, h + 1)
                        for c in range(2):
                            last = nc.tensor.matmul(ps[:, 6 + c, :], w_q[:, :], latents[:, c * HALF:(c + 1) * HALF], start=True, stop=True)
                        last.then_inc(s_q, 1)
                    for g in range(2):
                        if at == R_AT[g]:
                            if g == 0:
                                pe.wait_ge(s_q_kept, h + 1)
                            else:
                                pe.wait_ge(s_peak, h * 4 + 2)
                            for c in range(2):
                                last = nc.tensor.matmul(ps[:, 6 + c, :], k2[:, g, :], q[:, c * HALF:(c + 1) * HALF], start=True, stop=True)
                            last.then_inc(s_r, 1)
                        elif at == R_AT[g] + SUM:
                            pe.wait_ge(s_r_low, h * 2 + (g + 1))
                            for c in range(2):
                                last = nc.tensor.matmul(ps[:, 6 + c, :], ones[:, :], r_next[g][0][:, c * HALF:(c + 1) * HALF], start=True, stop=True)
                            last.then_inc(s_bound_mm, 1)
                        elif at == R_AT[g] + SQUARES:
                            pe.wait_ge(s_sq, h * 2 + (g + 1))
                            pe.wait_ge(s_peak, h * 4 + (2 * g + 1))
                            for c in range(2):
                                last = nc.tensor.matmul(ps[:, 6 + c, :], ones[:, :], squares[:, c * HALF:(c + 1) * HALF], start=True, stop=True)
                            last.then_inc(s_bound_mm, 1)
                    if at == EXACT:
                        pe.wait_ge(s_ready, h + 1)
                        nc.tensor.matmul(ps[:, 6, 0:1], ident[:, :], bound[:, :], start=True, stop=True)
                        bits = nc.tensor.value_load(bound[0:1, 0:1].bitcast(I32))
                        with pe.If(bits > SAFE_BITS):
                            exact(h)

                def exact(h):
                    def block_scores(g, cols, n, base, width):
                        if n >= 2:
                            pe.wait_ge(x_max, h * XN + base + (n - 1))
                        for k, (rp, zp) in enumerate(((0, 0), (0, 1), (1, 0))):
                            last = nc.tensor.matmul(ps[:, 6 + n % 2, 0:width], r_next[g][rp][:, n % NT * P:(n % NT + 1) * P], z_cols[zp][:, cols],
                                                    start=k == 0, stop=k == 2)
                        last.then_inc(x_score, 1)

                    with pe.Fori(0, NI) as i:
                        pe.wait_ge(x_row, h * ROWS + i + 1)
                        for n in range(NT):
                            block_scores(0, bass.ds(i * (U0 * P), U0 * P), n, i * NT, U0 * P)
                    pe.wait_ge(x_row, h * ROWS + NI + 1)
                    for n in range(2 * NT):
                        block_scores(1, slice(NM * P + n // NT * HALF, NM * P + (n // NT + 1) * HALF), n, NI * NT, HALF)
                    for t in range(NT):
                        pe.wait_ge(x_spread, h * NT + (t + 1))
                        nc.tensor.matmul(mid[:, t * P:(t + 1) * P], spread_max[:, :], ident[:, :], start=True, stop=True).then_inc(x_turned, 1)
                    pe.wait_ge(x_done, h + 1)

                def head(h, before=True, after=True):
                    for t in range(NZ):
                        scores(h, t)
                        if t >= 2:
                            weigh(h, t - 2)
                        if before:
                            finish(h - 1, t)
                        if after:
                            prepare(h + 1, t)
                    weigh(h, NZ - 2)

                pe.wait_ge(s_set, 4)
                for at in range(NZ):
                    prepare(0, at)
                head(0, before=False)
                with pe.Fori(1, H1 - 1) as h:
                    head(h)
                head(H1 - 1, after=False)
                for at in range(NZ):
                    finish(H1 - 1, at)

            @block.scalar
            def _(act):
                def tile(h, t):
                    act.wait_ge(s_score, h * NZ + (t + 1))
                    if t >= 2:
                        act.wait_ge(s_low, h * NZ + (t - 1))
                    pair = bank[:, 2 * (t % 2) * HALF:(2 * (t % 2) + 2) * HALF]
                    nc.scalar.activation(exps[t % 2][:, :], pair, ACT.Exp, bias=minus[:, 0:1]).then_inc(s_exp, 1)
                    if t >= 2:
                        act.wait_ge(s_weighted, h * NZ + (t - 1))
                    elif t == 0 and not first_head(h):
                        act.wait_ge(s_weighted, h * NZ)
                    nc.scalar.activation(high[t % 2][:, :], pair, ACT.Exp, bias=minus[:, 0:1]).then_inc(s_high, 1)

                def finish(h, at):
                    if at == OUT_WEIGHTS:
                        act.wait_ge(s_w2, h + 1)
                        nc.scalar.activation(w2[:, :, :], ps[:, 6, 0:2 * P].rearrange("p (g c) -> p g c", g=2), ACT.Copy).then_inc(s_w2_kept, 1)

                def prepare(h, at):
                    for g in range(2):
                        if at == R_AT[g]:
                            act.wait_ge(s_r, h * 2 + (g + 1))
                            if not first_head(h):
                                act.wait_ge(s_take_high[g], h)
                            nc.scalar.activation(r_next[g][0][:, :], mid, ACT.Copy).then_inc(s_r_high, 1)
                        elif at == R_AT[g] + SUM:
                            act.wait_ge(s_r_high, h * 2 + (g + 1))
                            if g:
                                act.wait_ge(s_bound_mm, h * 4 + 2)
                            nc.scalar.activation(squares[:, :], r_next[g][0][:, :].bitcast(F32), ACT.Square).then_inc(s_sq, 1)

                def take(h, g):
                    act.wait_ge(s_take_low[g], h + 1)
                    nc.scalar.activation(r[g][0][:, :], r_next[g][0][:, :].bitcast(F32), ACT.Copy).then_inc(s_take_high[g], 1)

                def head(h, before=True, after=True):
                    if before:
                        act.wait_ge(s_high, h * NZ)
                    act.wait_ge(s_take_low[0], h + 1)
                    nc.scalar.activation(minus[:, :], minus_next[:, :], ACT.Copy).then_inc(s_minus, 1)
                    act.wait_ge(s_minus, h + 1)
                    if before:
                        act.wait_ge(s_low, h * NZ)
                    for t in range(NZ):
                        tile(h, t)
                        if t == TAKE_LATENTS:
                            take(h, 1)
                        if before:
                            finish(h - 1, t)
                        if after:
                            prepare(h + 1, t)
                            if t == TAKE_MEDIA:
                                take(h + 1, 0)
                        if t == U_MEDIA:
                            copy_media(h, before)

                def copy_media(h, before):
                    act.wait_ge(s_weighted, h * NZ + NM)
                    if before:
                        act.wait_ge(s_y, h * 2)
                    nc.scalar.activation(u[0][:, :], bank[:, 4 * HALF:6 * HALF], ACT.Copy).then_inc(s_u_media, 1)

                act.wait_ge(s_set, 4)
                for at in range(NZ):
                    prepare(0, at)
                take(0, 0)
                head(0, before=False)
                with act.Fori(1, H1 - 1) as h:
                    head(h)
                head(H1 - 1, after=False)
                for at in range(NZ):
                    finish(H1 - 1, at)

            @block.gpsimd
            def _(pool):
                with pool.Fori(0, H1) as h:
                    pool.wait_ge(s_u_latents, h + 1)
                    pool.wait_ge(s_u_media, h + 1)
                    nc.gpsimd.tensor_tensor(u_both[:, :], u[0][:, :], u[1][:, :], ALU.add).then_inc(s_u_both, 1)

            @block.vector
            def _(dve):
                step = stepper(dve)

                def exact(h):
                    def maxima(base, done, width):
                        dve.wait_ge(x_row, h * ROWS + done)
                        for n in range(NT):
                            dve.wait_ge(x_score, h * XN + base + (n + 1))
                            nc.vector.tensor_reduce(chunk_max[:, n:n + 1], ps[:, 6 + n % 2, 0:width], AX.X, ALU.max).then_inc(x_max, 1)
                        dve.wait_ge(x_max, h * XN + base + NT)
                        nc.vector.tensor_tensor(row_max[:, :], row_max[:, :], chunk_max[:, :], ALU.max).then_inc(x_row, 1)

                    nc.vector.memset(row_max[:, :], MASKED).then_inc(x_row, 1)
                    with dve.Fori(0, NI) as i:
                        maxima(i * NT, i + 1, U0 * P)
                    for k in range(2):
                        maxima(NI * NT + k * NT, NI + 1 + k, HALF)
                    dve.wait_ge(x_row, h * ROWS + NI + 3)
                    for t in range(NT):
                        if t:
                            dve.wait_ge(x_turned, h * NT + t)
                        nc.vector.tensor_copy(spread_max[:, :], row_max[:, t:t + 1].to_broadcast([P, P])).then_inc(x_spread, 1)
                    dve.wait_ge(x_turned, h * NT + NT)
                    for g in range(2):
                        nc.vector.tensor_tensor(q[:, :], r_next[g][0][:, :].bitcast(F32), r_next[g][1][:, :].bitcast(F32), ALU.add).then_inc(x_fixed, 1)
                        dve.wait_ge(x_fixed, h * 8 + (4 * g + 1))
                        nc.vector.scalar_tensor_tensor(q[:, :], mid, -1.0 / P, q[:, :], ALU.mult, ALU.add).then_inc(x_fixed, 1)
                        dve.wait_ge(x_fixed, h * 8 + (4 * g + 2))
                        nc.vector.tensor_copy(r_next[g][0][:, :], q[:, :]).then_inc(x_fixed, 1)
                        dve.wait_ge(x_fixed, h * 8 + (4 * g + 3))
                        nc.vector.tensor_tensor(r_next[g][1][:, :], q[:, :], r_next[g][0][:, :].bitcast(F32), ALU.subtract).then_inc(x_fixed, 1)
                        dve.wait_ge(x_fixed, h * 8 + (4 * g + 4))
                    nc.vector.memset(minus_next[:, :], 0.0).then_inc(x_done, 1)

                def finish(h, at):
                    if at == U_LATENTS:
                        dve.wait_ge(s_weighted, h * NZ + NZ)
                        nc.vector.tensor_copy(u[1][:, :], mid).then_inc(s_u_latents, 1)
                    elif at == FOLD_V:
                        dve.wait_ge(s_fold_v, h + 1)
                        nc.vector.tensor_scalar(v2[:, :, :], ps[:, 6, 0:2 * P].rearrange("p (g c) -> p g c", g=2),
                                                biases[:, 2, bass.ds(h, 1)], None, ALU.add).then_inc(s_v2, 1)
                    elif at == OUT_WEIGHTS:
                        dve.wait_ge(s_den, h + 1)
                        nc.vector.reciprocal(inverse[:, :], ps[:, 7, 0:NT]).then_inc(s_inv, 1)
                    elif at == SCALE:
                        dve.wait_ge(s_y, h * 2 + 2)
                        nc.vector.tensor_tensor(q[:, :].rearrange("p (t c) -> p t c", c=P), mid.rearrange("p (t c) -> p t c", c=P),
                                                inverse[:, :].unsqueeze(2).to_broadcast([P, NT, P]), ALU.mult).then_inc(s_scaled, 1)
                    elif at == ADD:
                        dve.wait_ge(s_scaled, h + 1)
                        if not first_head(h):
                            dve.wait_ge(s_added, h)
                        nc.vector.tensor_tensor(x[:, :, :], x[:, :, :], q[:, :].rearrange("p (t c) -> p t c", c=P), ALU.add).then_inc(s_added, 1)

                def prepare(h, at):
                    if at == FOLD_K:
                        dve.wait_ge(s_fold_k, h + 1)
                        nc.vector.tensor_scalar(k2[:, :, :], ps[:, 6, 0:2 * P].rearrange("p (g c) -> p g c", g=2),
                                                biases[:, 1, bass.ds(h, 1)], None, ALU.add).then_inc(s_k2, 1)
                    elif at == QUERY:
                        dve.wait_ge(s_q, h + 1)
                        if not (first_head(h) or first_head(h - 1)):
                            dve.wait_ge(s_added, h - 1)
                        nc.vector.tensor_scalar(q[:, :], mid, biases[:, 0, bass.ds(h, 1)], float(P) ** -0.5, ALU.add, ALU.mult).then_inc(s_q_kept, 1)
                    for g in range(2):
                        if at == R_AT[g]:
                            dve.wait_ge(s_r_high, h * 2 + (g + 1))
                            if not first_head(h):
                                dve.wait_ge(s_take_low[g], h)
                            nc.vector.tensor_tensor(r_next[g][1][:, :], mid, r_next[g][0][:, :].bitcast(F32), ALU.subtract).then_inc(s_r_low, 1)
                        elif at == R_AT[g] + SUM:
                            dve.wait_ge(s_bound_mm, h * 4 + (2 * g + 1))
                            nc.vector.tensor_reduce(peak[:, g, 0:1], mid, AX.X, ALU.max, apply_absolute_value=True).then_inc(s_peak, 1)
                        elif at == R_AT[g] + SQUARES:
                            dve.wait_ge(s_bound_mm, h * 4 + (2 * g + 2))
                            nc.vector.tensor_reduce(peak[:, g, 1:2], mid, AX.X, ALU.max).then_inc(s_peak, 1)
                    if at == BOUND:
                        dve.wait_ge(s_peak, h * 4 + 4)
                        nc.vector.tensor_scalar(twice[:, :], peak[:, :, 1], 1.0, None, ALU.add).then_inc(s_root, 1)
                        for n in range(ROUNDS):
                            dve.wait_ge(s_root, h * (3 * ROUNDS + 1) + 3 * n + 1)
                            nc.vector.reciprocal(quotient[:, :], twice[:, :]).then_inc(s_root, 1)
                            dve.wait_ge(s_root, h * (3 * ROUNDS + 1) + 3 * n + 2)
                            nc.vector.scalar_tensor_tensor(quotient[:, :], quotient[:, :], 2.0, peak[:, :, 1], ALU.mult, ALU.mult).then_inc(s_root, 1)
                            dve.wait_ge(s_root, h * (3 * ROUNDS + 1) + 3 * n + 3)
                            nc.vector.scalar_tensor_tensor(twice[:, :], twice[:, :], 0.5, quotient[:, :], ALU.mult, ALU.add).then_inc(s_root, 1)
                        dve.wait_ge(s_root, (h + 1) * (3 * ROUNDS + 1))
                        nc.vector.scalar_tensor_tensor(peak[:, :, 0], twice[:, :], REACH / 2, peak[:, :, 0], ALU.mult, ALU.add).then_inc(s_bound, 1)
                        dve.wait_ge(s_bound, h * 2 + 1)
                        nc.vector.tensor_reduce(bound[:, :], peak[:, :, 0], AX.X, ALU.max).then_inc(s_bound, 1)
                        dve.wait_ge(s_bound, h * 2 + 2)
                        if not first_head(h):
                            dve.wait_ge(s_minus, h)
                        nc.vector.tensor_scalar(minus_next[:, :], bound[:, :], -1.0, None, ALU.mult).then_inc(s_ready, 1)
                    elif at == EXACT:
                        bits = nc.vector.value_load(bound[0:1, 0:1].bitcast(I32))
                        with dve.If(bits > SAFE_BITS):
                            exact(h)

                def take(h, g):
                    if not first_head(h):
                        dve.wait_ge(s_score, h * NZ if g else h * NZ - NL)
                    nc.vector.tensor_copy(r[g][1][:, :], r_next[g][1][:, :].bitcast(F32)).then_inc(s_take_low[g], 1)

                def head(h, before=True, after=True):
                    for t in range(NZ):
                        dve.wait_ge(s_high, h * NZ + (t + 1))
                        nc.vector.tensor_tensor(low[t % 2][:, :], exps[t % 2][:, :], high[t % 2][:, :].bitcast(F32), ALU.subtract).then_inc(s_low, 1)
                        if t == TAKE_LATENTS:
                            take(h, 1)
                        if before:
                            finish(h - 1, t)
                        if after:
                            prepare(h + 1, t)
                            if t == TAKE_MEDIA:
                                take(h + 1, 0)

                step(nc.vector.memset(ones_in[:, :], 1.0), s_set)
                step(nc.vector.tensor_copy(ones[:, :], ones_in[:, :]), s_set)
                step(nc.vector.memset(mean[:, :], 1.0 / P), s_set)
                dve.wait_ge(s_bias, 4 * 16)
                step(nc.vector.tensor_scalar(biases[:, 1:3, :], biases[:, 1:3, :], 1.0 / P, None, ALU.mult), s_set)
                for at in range(NZ):
                    prepare(0, at)
                take(0, 0)
                head(0, before=False)
                with dve.Fori(1, H1 - 1) as h:
                    head(h)
                head(H1 - 1, after=False)
                for at in range(NZ):
                    finish(H1 - 1, at)
                dve.wait_ge(s_added, H1)
                step(nc.vector.tensor_tensor(x[:, :, :], x[:, :, :], b_o[:, :].unsqueeze(1).to_broadcast([P, NT, P]), ALU.add), s_end)


def first_head(h):
    return isinstance(h, int) and h == 0


STAGES = [linear_attention, cross_attention, mixture0, lstm_step, latent_attention, mixture1]


def decoder(nc, a, out):
    with nc.allow_non_contiguous_dma(reason="columns of biases"):
        program(nc, a, out)


def program(nc, a, out):
    with ExitStack() as stack:
        kept = {
            "x": stack.enter_context(nc.sbuf_tensor("x", [P, NT, P], F32)),
            "ident": stack.enter_context(nc.sbuf_tensor("ident", [P, P], F32)),
            "out": out,
        }
        ps = stack.enter_context(nc.psum_tensor("ps", [P, 8, HALF], F32))
        for stage in STAGES:
            stage(nc, kept, ps, a)
            nc.clear_and_free_semaphores(list(Memory.taken))
            Memory.taken.clear()
            nc.all_engine_barrier()


def shape_constants():
    def angles(rows, length):
        inv_freq = np.float32(1.0) / np.float32(10000.0) ** (np.arange(0, D0, 2, dtype=np.float32) / np.float32(D0))
        pos = np.float32(10.0) * (np.arange(length, dtype=np.float32) / np.float32(length))
        ang = pos[rows][..., None] * inv_freq
        return np.stack([np.cos(ang), np.sin(ang)], axis=-2).astype(np.float32)

    def before(n):
        return np.broadcast_to(np.tril(np.ones((n, n), np.float32), -1), (P, n, n)).copy()

    def picks(experts, hidden):
        unit = np.arange(experts * hidden) // hidden
        rows = np.arange(P)[:, None]
        return ((rows == unit) | (rows == unit + 32)).astype(np.float32).reshape(P, -1, P)

    p = np.arange(P)
    keys = np.stack([t * P + p if t < NK - 1 else LAST + p for t in range(NK)], axis=1)
    return {
        "ident": np.eye(P, dtype=np.float32),
        "tri": np.triu(np.ones((P, P), np.float32)),
        "rope_q": angles(np.stack([t * P + p for t in range(NT)], axis=1), T),
        "rope_k": angles(keys, LC),
        "fresh": (p >= REPEATED).astype(np.float32)[:, None].copy(),
        "order8": before(8),
        "order4": before(4),
        "picks0": picks(8, 176),
        "picks1": picks(32, 64),
        "head_rows": (p[:, None] // ROW == np.arange(G0)[None, :]).astype(np.float32),
    }


def kernel(**inputs):
    import concourse.bacc as bacc
    from concourse.bass_utils import run_bass_kernel_spmd

    nc = bacc.Bacc("TRN2", target_bir_lowering=False, num_devices=1)
    arrays, aps = {}, {}
    for name, array in {**inputs, **shape_constants()}.items():
        array = np.ascontiguousarray(array)
        if array.dtype == np.bool_:
            array = array.view(np.uint8)
        arrays[f"in_{name}"] = array
        aps[name] = nc.dram_tensor(f"in_{name}", array.shape, mybir.dt.from_np(array.dtype), kind="ExternalInput").ap()
    out = nc.dram_tensor("out", (1, T, P), F32, kind="ExternalOutput").ap()
    decoder(nc, aps, out)
    result = run_bass_kernel_spmd(nc, [arrays], core_ids=[0])
    return result.results[0]["out"]
```
